# Optimizing a Trainium2 kernel written in Bass

```python
import numpy as np
import jax
import jax.numpy as jnp

def _softmax(x, axis=-1):
    return jax.nn.softmax(x, axis=axis)

def _gelu(x):
    return jax.nn.gelu(x, approximate=True)

def _silu(x):
    return jax.nn.silu(x)

def _sigmoid(x):
    return jax.nn.sigmoid(x)

def _layernorm(x, axis=-1, eps=1e-05):
    m = jnp.mean(x, axis=axis, keepdims=True)
    v = jnp.var(x, axis=axis, keepdims=True)
    return (x - m) / jnp.sqrt(v + eps)

def _scatter_add(tgt, idx, src, axis=0):
    return tgt.at[idx].add(src)

def _segment_sum(src, seg, n):
    return jax.ops.segment_sum(src, seg, n)
kernel_name = 'mk_sandwich_d1_jaxref_r8_60807b'

def setup_inputs(seed: int=0):
    np.random.seed(seed)
    _w = jnp.asarray

    def _L0_attn_setup():
        import jax, jax.numpy as jnp
        from jax import lax
        import numpy as np
        D_MODEL = 128
        D_STATE = 64
        D_CONV = 4
        EXPAND = 2
        HEADDIM = 128
        NGROUPS = 1
        CHUNK = 32
        D_INNER = EXPAND * D_MODEL
        NHEADS = D_INNER // HEADDIM
        CONV_DIM = D_INNER + 2 * NGROUPS * D_STATE
        D_IN_PROJ = D_INNER + CONV_DIM + NHEADS

        def _segsum_exp(t):
            T = t.shape[-1]
            cs = jnp.cumsum(t, axis=-1)
            d = cs[..., :, None] - cs[..., None, :]
            mask = jnp.tril(jnp.ones((T, T), dtype=bool))
            return jnp.where(mask, jnp.exp(jnp.where(mask, d, 0.0)), 0.0)

        def _ssd_scan(x, dt, A, Bm, Cm, chunk):
            Bz, L, H, P = x.shape
            G, N = (Bm.shape[2], Bm.shape[3])
            nc = L // chunk
            rep = H // G
            Bh = jnp.repeat(Bm, rep, axis=2)
            Ch = jnp.repeat(Cm, rep, axis=2)
            xc = x.reshape(Bz, nc, chunk, H, P)
            dtc = dt.reshape(Bz, nc, chunk, H)
            Bc = Bh.reshape(Bz, nc, chunk, H, N)
            Cc = Ch.reshape(Bz, nc, chunk, H, N)
            dA = dtc * A[None, None, None, :]
            dAh = jnp.transpose(dA, (0, 1, 3, 2))
            A_cs = jnp.cumsum(dAh, axis=-1)
            Lmat = _segsum_exp(dAh)
            Y_diag = jnp.einsum('bcqhn,bckhn,bchqk,bckh,bckhp->bcqhp', Cc, Bc, Lmat, dtc, xc)
            decay_states = jnp.exp(A_cs[..., -1:] - A_cs)
            states = jnp.einsum('bckhn,bchk,bckh,bckhp->bchpn', Bc, decay_states, dtc, xc)
            chunk_total = jnp.transpose(A_cs[..., -1], (0, 2, 1))
            padded = jnp.pad(chunk_total, ((0, 0), (0, 0), (1, 0)))
            decay_chunk = _segsum_exp(padded)
            states_cat = jnp.concatenate([jnp.zeros_like(states[:, :1]), states], axis=1)
            new_states = jnp.einsum('bhzc,bchpn->bzhpn', decay_chunk, states_cat)
            prev = new_states[:, :-1]
            Y_off = jnp.einsum('bcqhn,bchpn,bchq->bcqhp', Cc, prev, jnp.exp(A_cs))
            return (Y_diag + Y_off).reshape(Bz, L, H, P)
        key = jax.random.key(seed)
        ks = jax.random.split(key, 8)
        x = jax.random.normal(ks[0], (2, 512, D_MODEL), dtype=jnp.float32)
        W_in = jax.random.normal(ks[1], (D_IN_PROJ, D_MODEL), dtype=jnp.float32) * 0.02
        conv_w = jax.random.normal(ks[2], (CONV_DIM, 1, D_CONV), dtype=jnp.float32) * 0.2
        conv_b = jnp.zeros((CONV_DIM,), dtype=jnp.float32)
        A_init = jax.random.uniform(ks[3], (NHEADS,), minval=1.0, maxval=16.0)
        A_log = jnp.log(A_init).astype(jnp.float32)
        dtv = jnp.exp(jax.random.uniform(ks[4], (NHEADS,)) * (np.log(0.1) - np.log(0.001)) + np.log(0.001))
        dtv = jnp.clip(dtv, 0.001, None)
        dt_bias = (dtv + jnp.log(-jnp.expm1(-dtv))).astype(jnp.float32)
        D_skip = jnp.ones((NHEADS,), dtype=jnp.float32)
        W_out = jax.random.normal(ks[5], (D_MODEL, D_INNER), dtype=jnp.float32) * 0.02
        return {'x': x, 'W_in': W_in, 'conv_w': conv_w, 'conv_b': conv_b, 'A_log': A_log, 'dt_bias': dt_bias, 'D_skip': D_skip, 'W_out': W_out}
    _L0_attn_in = _L0_attn_setup()

    def _L0_ffn_setup():
        import jax, jax.numpy as jnp
        import numpy as np
        DIM = 128
        DEPTH = 6
        HEADS = 16
        DIM_HEAD = 64
        WINDOW = 32
        INNER = HEADS * DIM_HEAD
        DIM_INNER = int(DIM * 4 * 2 / 3)
        QK_SCALE = 8.0

        def shift_tokens(t):
            a, s = jnp.split(t, 2, -1)
            s = jnp.pad(s, ((0, 0), (1, 0), (0, 0)))[:, :-1]
            return jnp.concatenate([a, s], -1)

        def l2norm(t):
            return t / jnp.maximum(jnp.linalg.norm(t, axis=-1, keepdims=True), 1e-12)

        def rotate_half(x):
            x1, x2 = jnp.split(x, 2, -1)
            return jnp.concatenate([-x2, x1], -1)

        def rotary_tables(n):
            half = jnp.arange(0, DIM_HEAD, 2, dtype=jnp.float32)
            inv_freq = 1.0 / 10000.0 ** (half / DIM_HEAD)
            t = jnp.arange(n, dtype=jnp.float32)
            freqs = t[:, None] * inv_freq[None, :]
            freqs = jnp.concatenate([freqs, freqs], -1)
            base_scale = (half + 0.4 * DIM_HEAD) / (1.4 * DIM_HEAD)
            power = (t - n // 2) / (WINDOW // 2)
            scale = base_scale[None, :] ** power[:, None]
            scale = jnp.concatenate([scale, scale], -1)
            return (freqs, scale)

        def local_attention(q, k, v):
            b, h, n, d = q.shape
            w = WINDOW
            nw = n // w
            bq = q.reshape(b, h, nw, w, d)
            bk = k.reshape(b, h, nw, w, d)
            bv = v.reshape(b, h, nw, w, d)

            def look(t):
                p = jnp.pad(t, ((0, 0), (0, 0), (1, 0), (0, 0), (0, 0)))
                return jnp.concatenate([p[:, :, :nw], p[:, :, 1:]], axis=3)
            bk2, bv2 = (look(bk), look(bv))
            seq = jnp.arange(n).reshape(nw, w)
            seq_p = jnp.pad(seq, ((1, 0), (0, 0)), constant_values=-1)
            jt = jnp.concatenate([seq_p[:nw], seq_p[1:]], axis=1)
            it = seq[:, :, None]
            jb = jt[:, None, :]
            mask = (it < jb) | (it > jb + w) | (jb == -1)
            sim = jnp.einsum('bhwie,bhwje->bhwij', bq, bk2) * QK_SCALE
            sim = jnp.where(mask, -jnp.finfo(sim.dtype).max, sim)
            attn = jax.nn.softmax(sim, -1)
            out = jnp.einsum('bhwij,bhwje->bhwie', attn, bv2)
            return out.reshape(b, h, n, d)

        def attn_layer(x, Wqkv, qs, ksc, Wo):
            b, n, _ = x.shape
            qkv = x @ Wqkv
            q, k, v = jnp.split(qkv, 3, -1)
            sh = lambda t: t.reshape(b, n, HEADS, DIM_HEAD).transpose(0, 2, 1, 3)
            q, k, v = (sh(q), sh(k), sh(v))
            q = l2norm(q) * qs
            k = l2norm(k) * ksc
            freqs, scale = rotary_tables(n)
            cos, sin = (jnp.cos(freqs), jnp.sin(freqs))
            q = q * cos * scale + rotate_half(q) * sin * scale
            inv = 1.0 / scale
            k = k * cos * inv + rotate_half(k) * sin * inv
            out = local_attention(q, k, v)
            out = out.transpose(0, 2, 1, 3).reshape(b, n, INNER)
            return out @ Wo

        def ffn_layer(x, g, bln, W1, b1, W2, b2):
            mu = x.mean(-1, keepdims=True)
            var = ((x - mu) ** 2).mean(-1, keepdims=True)
            xn = (x - mu) / jnp.sqrt(var + 1e-05) * g + bln
            hg = xn @ W1 + b1
            a, gate = jnp.split(hg, 2, -1)
            return a * jax.nn.gelu(gate, approximate=False) @ W2 + b2
        key = jax.random.key(seed)
        ks = jax.random.split(key, 8)
        B, N = (2, 256)
        init = lambda k, shape: jax.random.normal(k, shape, jnp.float32) * 0.02
        return {'x': jax.random.normal(ks[0], (B, N, DIM), jnp.float32), 'Wqkv': init(ks[1], (DEPTH, DIM, 3 * INNER)), 'q_scale': jnp.ones((DEPTH, DIM_HEAD), jnp.float32), 'k_scale': jnp.ones((DEPTH, DIM_HEAD), jnp.float32), 'Wo': init(ks[2], (DEPTH, INNER, DIM)), 'ln_g': jnp.ones((DEPTH, DIM), jnp.float32), 'ln_b': jnp.zeros((DEPTH, DIM), jnp.float32), 'W1': init(ks[3], (DEPTH, DIM, 2 * DIM_INNER)), 'b1': jnp.zeros((DEPTH, 2 * DIM_INNER), jnp.float32), 'W2': init(ks[4], (DEPTH, DIM_INNER, DIM)), 'b2': jnp.zeros((DEPTH, DIM), jnp.float32)}
    _L0_ffn_in = _L0_ffn_setup()
    _d = {'L0_attn_x': _L0_attn_in['x'], 'L0_attn_W_in': _L0_attn_in['W_in'], 'L0_attn_conv_w': _L0_attn_in['conv_w'], 'L0_attn_conv_b': _L0_attn_in['conv_b'], 'L0_attn_A_log': _L0_attn_in['A_log'], 'L0_attn_dt_bias': _L0_attn_in['dt_bias'], 'L0_attn_D_skip': _L0_attn_in['D_skip'], 'L0_attn_W_out': _L0_attn_in['W_out'], 'L0_ffn_Wqkv': _L0_ffn_in['Wqkv'], 'L0_ffn_q_scale': _L0_ffn_in['q_scale'], 'L0_ffn_k_scale': _L0_ffn_in['k_scale'], 'L0_ffn_Wo': _L0_ffn_in['Wo'], 'L0_ffn_ln_g': _L0_ffn_in['ln_g'], 'L0_ffn_ln_b': _L0_ffn_in['ln_b'], 'L0_ffn_W1': _L0_ffn_in['W1'], 'L0_ffn_b1': _L0_ffn_in['b1'], 'L0_ffn_W2': _L0_ffn_in['W2'], 'L0_ffn_b2': _L0_ffn_in['b2']}
    _x0 = _d['L0_attn_x']
    _d['L0_attn_x'] = jax.random.normal(jax.random.fold_in(jax.random.key(seed), 1), (8, 256, 128), dtype=_x0.dtype)
    del _x0
    return _d

def reference(L0_attn_x, L0_attn_W_in, L0_attn_conv_w, L0_attn_conv_b, L0_attn_A_log, L0_attn_dt_bias, L0_attn_D_skip, L0_attn_W_out, L0_ffn_Wqkv, L0_ffn_q_scale, L0_ffn_k_scale, L0_ffn_Wo, L0_ffn_ln_g, L0_ffn_ln_b, L0_ffn_W1, L0_ffn_b1, L0_ffn_W2, L0_ffn_b2):

    def _L0_attn_ref(x, W_in, conv_w, conv_b, A_log, dt_bias, D_skip, W_out):
        import jax, jax.numpy as jnp
        from jax import lax
        import numpy as np
        D_MODEL = 128
        D_STATE = 64
        D_CONV = 4
        EXPAND = 2
        HEADDIM = 128
        NGROUPS = 1
        CHUNK = 32
        D_INNER = EXPAND * D_MODEL
        NHEADS = D_INNER // HEADDIM
        CONV_DIM = D_INNER + 2 * NGROUPS * D_STATE
        D_IN_PROJ = D_INNER + CONV_DIM + NHEADS

        def _segsum_exp(t):
            T = t.shape[-1]
            cs = jnp.cumsum(t, axis=-1)
            d = cs[..., :, None] - cs[..., None, :]
            mask = jnp.tril(jnp.ones((T, T), dtype=bool))
            return jnp.where(mask, jnp.exp(jnp.where(mask, d, 0.0)), 0.0)

        def _ssd_scan(x, dt, A, Bm, Cm, chunk):
            Bz, L, H, P = x.shape
            G, N = (Bm.shape[2], Bm.shape[3])
            nc = L // chunk
            rep = H // G
            Bh = jnp.repeat(Bm, rep, axis=2)
            Ch = jnp.repeat(Cm, rep, axis=2)
            xc = x.reshape(Bz, nc, chunk, H, P)
            dtc = dt.reshape(Bz, nc, chunk, H)
            Bc = Bh.reshape(Bz, nc, chunk, H, N)
            Cc = Ch.reshape(Bz, nc, chunk, H, N)
            dA = dtc * A[None, None, None, :]
            dAh = jnp.transpose(dA, (0, 1, 3, 2))
            A_cs = jnp.cumsum(dAh, axis=-1)
            Lmat = _segsum_exp(dAh)
            Y_diag = jnp.einsum('bcqhn,bckhn,bchqk,bckh,bckhp->bcqhp', Cc, Bc, Lmat, dtc, xc)
            decay_states = jnp.exp(A_cs[..., -1:] - A_cs)
            states = jnp.einsum('bckhn,bchk,bckh,bckhp->bchpn', Bc, decay_states, dtc, xc)
            chunk_total = jnp.transpose(A_cs[..., -1], (0, 2, 1))
            padded = jnp.pad(chunk_total, ((0, 0), (0, 0), (1, 0)))
            decay_chunk = _segsum_exp(padded)
            states_cat = jnp.concatenate([jnp.zeros_like(states[:, :1]), states], axis=1)
            new_states = jnp.einsum('bhzc,bchpn->bzhpn', decay_chunk, states_cat)
            prev = new_states[:, :-1]
            Y_off = jnp.einsum('bcqhn,bchpn,bchq->bcqhp', Cc, prev, jnp.exp(A_cs))
            return (Y_diag + Y_off).reshape(Bz, L, H, P)
        Bz, L, _ = x.shape
        proj = x @ W_in.T
        z = proj[..., :D_INNER]
        xBC = proj[..., D_INNER:D_INNER + CONV_DIM]
        dt_raw = proj[..., D_INNER + CONV_DIM:]
        xBC_t = jnp.transpose(xBC, (0, 2, 1))
        conv = lax.conv_general_dilated(xBC_t, conv_w, (1,), [(D_CONV - 1, 0)], dimension_numbers=('NCH', 'OIH', 'NCH'), feature_group_count=CONV_DIM)
        xBC = jnp.transpose(conv + conv_b[None, :, None], (0, 2, 1))
        xBC = jax.nn.silu(xBC)
        x_ssm = xBC[..., :D_INNER].reshape(Bz, L, NHEADS, HEADDIM)
        B_ssm = xBC[..., D_INNER:D_INNER + NGROUPS * D_STATE].reshape(Bz, L, NGROUPS, D_STATE)
        C_ssm = xBC[..., D_INNER + NGROUPS * D_STATE:].reshape(Bz, L, NGROUPS, D_STATE)
        dt = jax.nn.softplus(dt_raw + dt_bias[None, None, :])
        A = -jnp.exp(A_log)
        y = _ssd_scan(x_ssm, dt, A, B_ssm, C_ssm, CHUNK)
        y = y + x_ssm * D_skip[None, None, :, None]
        y = y.reshape(Bz, L, D_INNER)
        y = y * jax.nn.silu(z)
        return y @ W_out.T

    def _L0_ffn_ref(x, Wqkv, q_scale, k_scale, Wo, ln_g, ln_b, W1, b1, W2, b2):
        import jax, jax.numpy as jnp
        import numpy as np
        DIM = 128
        DEPTH = 6
        HEADS = 16
        DIM_HEAD = 64
        WINDOW = 32
        INNER = HEADS * DIM_HEAD
        DIM_INNER = int(DIM * 4 * 2 / 3)
        QK_SCALE = 8.0

        def shift_tokens(t):
            a, s = jnp.split(t, 2, -1)
            s = jnp.pad(s, ((0, 0), (1, 0), (0, 0)))[:, :-1]
            return jnp.concatenate([a, s], -1)

        def l2norm(t):
            return t / jnp.maximum(jnp.linalg.norm(t, axis=-1, keepdims=True), 1e-12)

        def rotate_half(x):
            x1, x2 = jnp.split(x, 2, -1)
            return jnp.concatenate([-x2, x1], -1)

        def rotary_tables(n):
            half = jnp.arange(0, DIM_HEAD, 2, dtype=jnp.float32)
            inv_freq = 1.0 / 10000.0 ** (half / DIM_HEAD)
            t = jnp.arange(n, dtype=jnp.float32)
            freqs = t[:, None] * inv_freq[None, :]
            freqs = jnp.concatenate([freqs, freqs], -1)
            base_scale = (half + 0.4 * DIM_HEAD) / (1.4 * DIM_HEAD)
            power = (t - n // 2) / (WINDOW // 2)
            scale = base_scale[None, :] ** power[:, None]
            scale = jnp.concatenate([scale, scale], -1)
            return (freqs, scale)

        def local_attention(q, k, v):
            b, h, n, d = q.shape
            w = WINDOW
            nw = n // w
            bq = q.reshape(b, h, nw, w, d)
            bk = k.reshape(b, h, nw, w, d)
            bv = v.reshape(b, h, nw, w, d)

            def look(t):
                p = jnp.pad(t, ((0, 0), (0, 0), (1, 0), (0, 0), (0, 0)))
                return jnp.concatenate([p[:, :, :nw], p[:, :, 1:]], axis=3)
            bk2, bv2 = (look(bk), look(bv))
            seq = jnp.arange(n).reshape(nw, w)
            seq_p = jnp.pad(seq, ((1, 0), (0, 0)), constant_values=-1)
            jt = jnp.concatenate([seq_p[:nw], seq_p[1:]], axis=1)
            it = seq[:, :, None]
            jb = jt[:, None, :]
            mask = (it < jb) | (it > jb + w) | (jb == -1)
            sim = jnp.einsum('bhwie,bhwje->bhwij', bq, bk2) * QK_SCALE
            sim = jnp.where(mask, -jnp.finfo(sim.dtype).max, sim)
            attn = jax.nn.softmax(sim, -1)
            out = jnp.einsum('bhwij,bhwje->bhwie', attn, bv2)
            return out.reshape(b, h, n, d)

        def attn_layer(x, Wqkv, qs, ksc, Wo):
            b, n, _ = x.shape
            qkv = x @ Wqkv
            q, k, v = jnp.split(qkv, 3, -1)
            sh = lambda t: t.reshape(b, n, HEADS, DIM_HEAD).transpose(0, 2, 1, 3)
            q, k, v = (sh(q), sh(k), sh(v))
            q = l2norm(q) * qs
            k = l2norm(k) * ksc
            freqs, scale = rotary_tables(n)
            cos, sin = (jnp.cos(freqs), jnp.sin(freqs))
            q = q * cos * scale + rotate_half(q) * sin * scale
            inv = 1.0 / scale
            k = k * cos * inv + rotate_half(k) * sin * inv
            out = local_attention(q, k, v)
            out = out.transpose(0, 2, 1, 3).reshape(b, n, INNER)
            return out @ Wo

        def ffn_layer(x, g, bln, W1, b1, W2, b2):
            mu = x.mean(-1, keepdims=True)
            var = ((x - mu) ** 2).mean(-1, keepdims=True)
            xn = (x - mu) / jnp.sqrt(var + 1e-05) * g + bln
            hg = xn @ W1 + b1
            a, gate = jnp.split(hg, 2, -1)
            return a * jax.nn.gelu(gate, approximate=False) @ W2 + b2
        for i in range(DEPTH):
            x = attn_layer(shift_tokens(x), Wqkv[i], q_scale[i], k_scale[i], Wo[i]) + x
            x = ffn_layer(shift_tokens(x), ln_g[i], ln_b[i], W1[i], b1[i], W2[i], b2[i]) + x
        return x
    x = L0_attn_x
    x = x + _layernorm(_L0_attn_ref(_layernorm(x, axis=-1), L0_attn_W_in, L0_attn_conv_w, L0_attn_conv_b, L0_attn_A_log, L0_attn_dt_bias, L0_attn_D_skip, L0_attn_W_out), axis=-1)
    x = x + _layernorm(_L0_ffn_ref(_layernorm(x, axis=-1), L0_ffn_Wqkv, L0_ffn_q_scale, L0_ffn_k_scale, L0_ffn_Wo, L0_ffn_ln_g, L0_ffn_ln_b, L0_ffn_W1, L0_ffn_b1, L0_ffn_W2, L0_ffn_b2), axis=-1)
    return x

_drawn_inputs = setup_inputs


def setup_inputs(seed=0):
    import zlib

    import numpy as np

    out = dict(_drawn_inputs(seed))
    spreads = {'L0_attn_conv_b': (0.0, 0.1),
     'L0_attn_D_skip': (1.0, 0.2),
     'L0_ffn_q_scale': (1.0, 0.6),
     'L0_ffn_k_scale': (1.0, 0.6),
     'L0_ffn_ln_g': (1.0, 0.6),
     'L0_ffn_ln_b': (0.0, 0.8),
     'L0_ffn_b1': (0.0, 0.8),
     'L0_ffn_b2': (0.0, 0.1)}
    factors = {'L0_attn_A_log': 8.0, 'L0_attn_dt_bias': 64.0, 'L0_ffn_W1': 4.164, 'L0_ffn_W2': 4.092}
    for name, (base, spread) in spreads.items():
        noise = np.random.default_rng([zlib.crc32(name.encode()), seed]).standard_normal(out[name].shape)
        drawn = base * np.exp(spread * noise) if base else spread * noise
        out[name] = jnp.asarray(drawn.astype(out[name].dtype))
    for name, factor in factors.items():
        out[name] = (out[name] * factor).astype(out[name].dtype)
    return out
```

```python
from contextlib import ExitStack

import numpy as np

import concourse.bass as bass
from concourse import mybir

F32 = mybir.dt.float32
F32R = mybir.dt.float32r
BF16 = mybir.dt.bfloat16
ALU = mybir.AluOpType
ACT = mybir.ActivationFunctionType
AX = mybir.AxisListType

P = 128
BATCH, SEQ, DIM = 8, 256, 128
TOK = BATCH * SEQ
TILES = SEQ // P
D_INNER, D_STATE, D_CONV, NHEADS = 256, 64, 4, 2
CONV_DIM = D_INNER + 2 * D_STATE
PROJ = D_INNER + CONV_DIM + NHEADS
GROUPS = 4
GT = TOK // GROUPS
DEPTH, HEADS, DH, WIN = 6, 16, 64, 32
PAIRS = HEADS // 2
INNER = HEADS * DH
DIM_INNER = int(DIM * 4 * 2 / 3)
HC = 3
HLAST = DIM_INNER - 2 * P
UNITS = DEPTH * BATCH
VW = DH + 1
LN_EPS = 1e-5
N_PROJ, N_SC, N_TR, N_PV, N_F = 12, 4, 16, 6, 7
QK_COLS = 2 * INNER
SPLIT = QK_COLS // BATCH
PV_CHUNKS = [(0, 3), (3, 6), (6, 8)]
C_G, C_B, C_B2, C_B1A, C_B1G = 0, 1, 2, 3, 6
N_COLS = 9


def started(value):
    return not isinstance(value, int) or value > 0


def build(nc, x, w_in_t, conv_cols, a_log, dt_bias, d_skip, w_out_t, w_qk, w_v, w_o, w_1, w_2,
          q_scale, k_scale, cols_in, rope, consts, mask_in, out):
    whole = ExitStack()
    with whole:
        def sb(stack, name, shape, dt=F32):
            return stack.enter_context(nc.sbuf_tensor(name, shape, dt))

        def sem(stack, name):
            return stack.enter_context(nc.semaphore(name))

        ident = sb(whole, "ident", [P, P])
        ones_mean = sb(whole, "ones_mean", [P, P])
        eps_col = sb(whole, "eps_col", [P, 1])
        x1 = sb(whole, "x1", [P, TOK])
        xs = sb(whole, "xs", [P, BATCH, SEQ + 1])
        bank = [whole.enter_context(nc.psum_tensor(f"bank{i}", [P, 512], F32)) for i in range(8)]

        with ExitStack() as mixer:
            build_mixer(nc, mixer, sb, sem, bank, ident, ones_mean, eps_col, x1, xs, x, w_in_t, conv_cols,
                        a_log, dt_bias, d_skip, w_out_t, consts)
        with ExitStack() as layers:
            build_layers(nc, layers, sb, sem, bank, ident, ones_mean, eps_col, xs, w_qk, w_v, w_o, w_1,
                         w_2, q_scale, k_scale, cols_in, rope, mask_in)
        with ExitStack() as last:
            build_last(nc, last, sb, sem, bank, ident, ones_mean, eps_col, x1, xs, out)


def build_mixer(nc, ctx, sb, sem, bank, ident, ones_mean, eps_col, x1, xs, x, w_in_t, conv_cols, a_log,
                dt_bias, d_skip, w_out_t, consts):
    NT = TOK // P
    HB = BATCH * TILES * NHEADS
    xin = sb(ctx, "xin", [P, NT, P])
    win = sb(ctx, "win", [P, PROJ])
    wout = sb(ctx, "wout", [P, NHEADS, DIM])
    tri = sb(ctx, "tri", [P, 3 * P])
    convw = sb(ctx, "convw", [P, 3, D_CONV + 1])
    heads = sb(ctx, "heads", [P, 4, NHEADS])
    xc = sb(ctx, "xc", [P, TOK])
    sq = sb(ctx, "sq", [P, TOK])
    rstd = sb(ctx, "rstd", [P, TOK])
    xn = sb(ctx, "xn", [P, TOK])
    zs = sb(ctx, "zs", [P, 2, TOK])
    raw = sb(ctx, "raw", [P, 3, BATCH, SEQ + 3])
    cv = sb(ctx, "cv", [P, 3, BATCH, SEQ])
    c_low = sb(ctx, "c_low", [D_STATE, BATCH, SEQ])
    sp = sb(ctx, "sp", [P, 12, HB])
    dec = sb(ctx, "dec", [P, 2, NHEADS, 3 * P])
    gm = sb(ctx, "gm", [P, 2, 3 * P])
    st = sb(ctx, "st", [P, 2, NHEADS, 3 * P])
    xnat = sb(ctx, "xnat", [P, 2, 4, P])
    yy = sb(ctx, "yy", [P, 2, NHEADS, SEQ])
    BIAS, R, NEG, E, U, L, V, M, DT, DA, CS, TMP = range(12)

    x_in = [sem(ctx, f"m_x_in{g}") for g in range(GROUPS)]
    w_dma = sem(ctx, "m_w_dma")
    setup = sem(ctx, "m_setup")
    xt_mm = sem(ctx, "m_xt_mm")
    xt_evac = sem(ctx, "m_xt_evac")
    mean_mm = sem(ctx, "m_mean_mm")
    centred = sem(ctx, "m_centred")
    squared = sem(ctx, "m_squared")
    var_mm = sem(ctx, "m_var_mm")
    log_done = sem(ctx, "m_log_done")
    rstd_done = sem(ctx, "m_rstd_done")
    norm_done = sem(ctx, "m_norm_done")
    proj_mm = sem(ctx, "m_proj_mm")
    proj_evac = sem(ctx, "m_proj_evac")
    dt_mm = sem(ctx, "m_dt_mm")
    tap = sem(ctx, "m_tap")
    conv_done = sem(ctx, "m_conv_done")
    silu_done = sem(ctx, "m_silu_done")
    c_moved = sem(ctx, "m_c_moved")
    sp_step = sem(ctx, "m_sp_step")
    sp_act = sem(ctx, "m_sp_act")
    cs_mm = sem(ctx, "m_cs_mm")
    row_mm = sem(ctx, "m_row_mm")
    diff_done = sem(ctx, "m_diff_done")
    dec_done = sem(ctx, "m_dec_done")
    g_mm = sem(ctx, "m_g_mm")
    g_done = sem(ctx, "m_g_done")
    s_done = sem(ctx, "m_s_done")
    xnat_mm = sem(ctx, "m_xnat_mm")
    xnat_evac = sem(ctx, "m_xnat_evac")
    y_mm = sem(ctx, "m_y_mm")
    y_skip = sem(ctx, "m_y_skip")
    y_done = sem(ctx, "m_y_done")
    o_mm = sem(ctx, "m_o_mm")
    o_evac = sem(ctx, "m_o_evac")
    x1_done = sem(ctx, "m_x1_done")
    xs_done = sem(ctx, "m_xs_done")

    DT_STEPS, CS_STEPS = 13, 14

    def tok(g):
        return slice(g * GT, (g + 1) * GT)

    def yo(t):
        return t[:, :, :].rearrange("p n d -> p (n d)")

    block = ctx.enter_context(nc.Block())

    @block.sync
    def _(sync):
        xv = x.rearrange("b (t p) d -> p (b t) d", p=P)
        sync.dma_start(ident[:, :], consts[:, 0:P]).then_inc(w_dma, 16)
        for g in range(GROUPS):
            sync.dma_start(xin[:, 4 * g:4 * g + 4, :], xv[:, 4 * g:4 * g + 4, :]).then_inc(x_in[g], 16)
        sync.dma_start(win[:, :], w_in_t).then_inc(w_dma, 16)
        sync.dma_start(convw[:, :, :], conv_cols).then_inc(w_dma, 16)
        sync.dma_start(tri[:, :], consts[:, P:4 * P]).then_inc(w_dma, 16)
        sync.dma_start(wout[:, :, :], w_out_t.rearrange("(h p) d -> p h d", p=P)).then_inc(w_dma, 16)
        for n, row in enumerate((a_log, dt_bias, d_skip)):
            sync.dma_start(heads[:, n, :], row.partition_broadcast(P)).then_inc(w_dma, 16)
        for g in range(GROUPS):
            sync.wait_ge(silu_done, 2 * GROUPS + g + 1)
            sync.dma_start(c_low[:, 2 * g:2 * g + 2, :], cv[D_STATE:P, 2, 2 * g:2 * g + 2, :]).then_inc(c_moved, 16)

    W_ALL = 8 * 16

    @block.gpsimd
    def _(pool):
        nc.gpsimd.memset(ones_mean[:, :], 1.0 / DIM).then_inc(setup, 1)
        nc.gpsimd.memset(eps_col[:, :], LN_EPS).then_inc(setup, 1)
        nc.gpsimd.memset(raw[:, :, :, 0:3], 0.0).then_inc(setup, 1)
        nc.gpsimd.memset(xs[:, :, 0:1], 0.0).then_inc(setup, 1)

    @block.tensor
    def _(pe):
        pe.wait_ge(setup, 4)
        pe.wait_ge(w_dma, W_ALL)

        def mean_of(n, src, g, ready, count):
            pe.wait_ge(ready, count)
            if n >= 2:
                pe.wait_ge(log_done, n - 1)
            nc.tensor.matmul(bank[n % 2][:, :], ones_mean[:, :], src[:, tok(g)], start=True, stop=True).then_inc(mean_mm, 1)

        def var_of(n, g):
            pe.wait_ge(squared, n + 1)
            nc.tensor.matmul(bank[n % 2][:, :], ones_mean[:, :], sq[:, tok(g)], start=True, stop=True).then_inc(var_mm, 1)

        for g in range(GROUPS):
            pe.wait_ge(x_in[g], 16)
            if g >= 2:
                pe.wait_ge(xt_evac, g - 1)
            for t in range(4):
                mm = nc.tensor.transpose(bank[2 + g % 2][:, t * P:(t + 1) * P], xin[:, 4 * g + t, :], ident[:, :])
            mm.then_inc(xt_mm, 1)
        for g in range(GROUPS):
            mean_of(g, x1, g, xt_evac, g + 1)
            if g:
                var_of(g - 1, g - 1)
        var_of(GROUPS - 1, GROUPS - 1)
        n = 0
        for c in range(5):
            for g in range(GROUPS):
                pe.wait_ge(norm_done, g + 1)
                if n >= 4:
                    pe.wait_ge(proj_evac, n - 3)
                else:
                    pe.wait_ge(xt_evac, GROUPS)
                nc.tensor.matmul(bank[2 + n % 4][:, :], win[:, c * P:(c + 1) * P], xn[:, tok(g)],
                                 start=True, stop=True).then_inc(proj_mm, 1)
                n += 1
        for t in range(NT):
            mm = nc.tensor.matmul(bank[6][:, NHEADS * t:NHEADS * (t + 1)], xn[:, t * P:(t + 1) * P],
                                  win[:, PROJ - NHEADS:PROJ], start=True, stop=True)
        mm.then_inc(dt_mm, 1)
        pe.wait_ge(sp_step, DT_STEPS)
        nc.tensor.matmul(bank[7][:, 0:HB], tri[:, 0:P], sp[:, DA, :], start=True, stop=True).then_inc(cs_mm, 1)

        def rows(b):
            for h in range(NHEADS):
                c0, c1 = (2 * b) * NHEADS + h, (2 * b + 1) * NHEADS + h
                dst = bank[h]
                if b:
                    pe.wait_ge(diff_done, 2 * (b - 1) + h + 1)
                else:
                    pe.wait_ge(log_done, GROUPS)
                first = sp[:, DA, c0:c0 + 1].to_broadcast([P, P])
                second = sp[:, DA, c1:c1 + 1].to_broadcast([P, P])
                nc.tensor.matmul(dst[:, 0:2 * P], first, tri[:, 0:2 * P], start=True, stop=True, skip_group_check=True)
                nc.tensor.matmul(dst[:, P:2 * P], second, tri[:, 0:P], start=False, stop=True, skip_group_check=True)
                nc.tensor.matmul(dst[:, 2 * P:3 * P], second, tri[:, 0:P], start=False, stop=True,
                                 skip_group_check=True).then_inc(row_mm, 1)

        def scores(b):
            if b:
                pe.wait_ge(g_done, b)
            else:
                pe.wait_ge(c_moved, 16 * GROUPS)
                pe.wait_ge(proj_evac, 5 * GROUPS)
            nc.tensor.matmul(bank[2][:, 0:2 * P], cv[0:D_STATE, 2, b, 0:P], c_low[:, b, :], start=True, stop=True)
            nc.tensor.matmul(bank[2][:, 2 * P:3 * P], cv[0:D_STATE, 2, b, P:2 * P], c_low[:, b, P:2 * P],
                             start=True, stop=True).then_inc(g_mm, 1)

        def to_nat(b):
            if b:
                pe.wait_ge(xnat_evac, b)
            for h in range(NHEADS):
                for t in range(TILES):
                    mm = nc.tensor.transpose(bank[3][:, (2 * h + t) * P:(2 * h + t + 1) * P],
                                             cv[:, h, b, t * P:(t + 1) * P], ident[:, :])
            mm.then_inc(xnat_mm, 1)

        def ys(b):
            pe.wait_ge(xnat_evac, b + 1)
            if b >= 2:
                pe.wait_ge(y_skip, 2 * (b - 2) + 2)
            for h in range(NHEADS):
                pe.wait_ge(s_done, 2 * b + h + 1)
                dst = bank[4 + b % 2][:, h * SEQ:(h + 1) * SEQ]
                nc.tensor.matmul(dst, xnat[:, b % 2, 2 * h, :], st[:, b % 2, h, 0:SEQ], start=True, stop=True,
                                 skip_group_check=True)
                mm = nc.tensor.matmul(dst[:, P:SEQ], xnat[:, b % 2, 2 * h + 1, :], st[:, b % 2, h, SEQ:SEQ + P],
                                      start=False, stop=True, skip_group_check=True)
            mm.then_inc(y_mm, 1)

        def outs(b):
            pe.wait_ge(y_done, b + 1)
            g = b // 2
            if g >= 2 and b % 2 == 0:
                pe.wait_ge(o_evac, g - 1)
            elif b == 0:
                pe.wait_ge(cs_mm, 1)
                pe.wait_ge(sp_step, CS_STEPS)
            for h in range(NHEADS):
                mm = nc.tensor.matmul(bank[6 + g % 2][:, (b % 2) * SEQ:(b % 2 + 1) * SEQ], wout[:, h, :],
                                      yy[:, b % 2, h, :], start=(h == 0), stop=(h == NHEADS - 1), skip_group_check=True)
            mm.then_inc(o_mm, 1)

        for b in range(BATCH + 2):
            if b < BATCH:
                rows(b)
                scores(b)
                to_nat(b)
            if 1 <= b <= BATCH:
                ys(b - 1)
            if b >= 2:
                outs(b - 2)
        for k, (src, ready, base) in enumerate(((yo(xin), o_evac, 0), (x1, x1_done, 0))):
            for g in range(GROUPS):
                n = GROUPS * (k + 1) + g
                if g < 2 and k == 0:
                    pe.wait_ge(diff_done, 2 * BATCH)
                mean_of(n, src, g, ready, g + 1)
                if g:
                    var_of(n - 1, g - 1)
            var_of(n, g)

    @block.scalar
    def _(act):
        for g in range(GROUPS):
            act.wait_ge(xt_mm, g + 1)
            nc.scalar.copy(x1[:, tok(g)], bank[2 + g % 2][:, :]).then_inc(xt_evac, 1)

        def norm_steps(k):
            def square(g):
                act.wait_ge(centred, GROUPS * k + g + 1)
                if k:
                    act.wait_ge(var_mm, GROUPS * (k - 1) + g + 1)
                nc.scalar.activation(sq[:, tok(g)], xc[:, tok(g)], ACT.Square).then_inc(squared, 1)

            def root(g):
                n = GROUPS * k + g
                act.wait_ge(var_mm, n + 1)
                if k:
                    act.wait_ge(norm_done, n - GROUPS + 1)
                nc.scalar.activation(rstd[:, tok(g)], bank[n % 2][:, :], ACT.Ln, bias=eps_col[:, 0:1]).then_inc(log_done, 1)
                act.wait_ge(log_done, n + 1)
                nc.scalar.activation(rstd[:, tok(g)], rstd[:, tok(g)], ACT.Exp, scale=-0.5).then_inc(rstd_done, 1)

            for g in range(GROUPS):
                square(g)
                if g:
                    root(g - 1)
            root(GROUPS - 1)

        norm_steps(0)
        n = 0
        for c in range(5):
            for g in range(GROUPS):
                act.wait_ge(proj_mm, n + 1)
                src = bank[2 + n % 4]
                if c < 2:
                    nc.scalar.activation(zs[:, c, tok(g)], src[:, :], ACT.Silu).then_inc(proj_evac, 1)
                else:
                    nc.scalar.copy(raw[:, c - 2, 2 * g:2 * g + 2, 3:], src[:, :].rearrange("p (b s) -> p b s", b=2))\
                        .then_inc(proj_evac, 1)
                n += 1
        for c in range(3):
            for g in range(GROUPS):
                act.wait_ge(conv_done, GROUPS * c + g + 1)
                dst = cv[:, c, 2 * g:2 * g + 2, :]
                nc.scalar.activation(dst, dst, ACT.Silu).then_inc(silu_done, 1)
        act.wait_ge(w_dma, W_ALL)
        act.wait_ge(sp_step, 3)
        nc.scalar.activation(sp[:, E, :], sp[:, NEG, :], ACT.Exp).then_inc(sp_act, 1)
        nc.scalar.activation(heads[:, 3, :], heads[:, 0, :], ACT.Exp).then_inc(sp_act, 1)
        act.wait_ge(sp_step, 4)
        nc.scalar.activation(sp[:, L, :], sp[:, U, :], ACT.Ln).then_inc(sp_act, 1)

        for b in range(BATCH):
            act.wait_ge(xnat_mm, b + 1)
            if b >= 2:
                act.wait_ge(y_mm, b - 1)
            nc.scalar.copy(xnat[:, b % 2, :, :], bank[3][:, :].rearrange("p (k d) -> p k d", k=4)).then_inc(xnat_evac, 1)
            for h in range(NHEADS):
                act.wait_ge(diff_done, 2 * b + h + 1)
                nc.scalar.activation(dec[:, b % 2, h, :], dec[:, b % 2, h, :], ACT.Exp).then_inc(dec_done, 1)
            if b >= 3 and b % 2 == 1:
                g = (b - 3) // 2
                act.wait_ge(o_mm, 2 * g + 2)
                nc.scalar.copy(yo(xin)[:, tok(g)], bank[6 + g % 2][:, :]).then_inc(o_evac, 1)
        act.wait_ge(o_mm, BATCH)
        nc.scalar.copy(yo(xin)[:, tok(3)], bank[7][:, :]).then_inc(o_evac, 1)
        norm_steps(1)
        norm_steps(2)

    @block.vector
    def _(dve):
        def centre(k, src):
            def one(g):
                n = GROUPS * k + g
                dve.wait_ge(mean_mm, n + 1)
                if k:
                    dve.wait_ge(norm_done, n - GROUPS + 1)
                    dve.wait_ge(squared, n - GROUPS + 1)
                nc.vector.tensor_tensor(xc[:, tok(g)], src[:, tok(g)], bank[n % 2][:, :], ALU.subtract).then_inc(centred, 1)
            return one

        def scale(k, write):
            def one(g):
                dve.wait_ge(rstd_done, GROUPS * k + g + 1)
                write(g)
            return one

        def norm(k, src, write):
            c, s = centre(k, src), scale(k, write)
            c(0)
            c(1)
            for g in range(GROUPS):
                s(g)
                if g + 2 < GROUPS:
                    c(g + 2)

        def write_xn(g):
            nc.vector.tensor_tensor(xn[:, tok(g)], xc[:, tok(g)], rstd[:, tok(g)], ALU.mult).then_inc(norm_done, 1)

        norm(0, x1, write_xn)
        dve.wait_ge(w_dma, W_ALL)
        dve.wait_ge(setup, 4)
        taps = 0
        for c in range(3):
            for g in range(GROUPS):
                dve.wait_ge(proj_evac, GROUPS * (c + 2) + g + 1)
                b0 = 2 * g
                dst = cv[:, c, b0:b0 + 2, :]
                nc.vector.tensor_scalar(dst, raw[:, c, b0:b0 + 2, 0:SEQ], convw[:, c, 0:1], convw[:, c, D_CONV:D_CONV + 1],
                                        ALU.mult, ALU.add).then_inc(tap, 1)
                for k in range(1, D_CONV):
                    taps += 1
                    dve.wait_ge(tap, taps)
                    ins = nc.vector.scalar_tensor_tensor(out=dst, in0=raw[:, c, b0:b0 + 2, k:k + SEQ],
                                                         scalar=convw[:, c, k:k + 1], in1=dst, op0=ALU.mult, op1=ALU.add)
                    ins.then_inc(tap if k < D_CONV - 1 else conv_done, 1)
        steps = [0]

        def step(ins):
            steps[0] += 1
            ins.then_inc(sp_step, 1)
            dve.wait_ge(sp_step, steps[0])

        def bc(row):
            return heads[:, row, :].unsqueeze(1).broadcast_to([P, HB // NHEADS, NHEADS])

        def v3(row):
            return sp[:, row, :].rearrange("p (n h) -> p n h", h=NHEADS)

        dve.wait_ge(dt_mm, 1)
        step(nc.vector.tensor_tensor(v3(R), bank[6][:, 0:HB].rearrange("p (n h) -> p n h", h=NHEADS), bc(1), ALU.add))
        step(nc.vector.tensor_scalar(sp[:, TMP, :], sp[:, R, :], -1.0, None, ALU.mult))
        step(nc.vector.tensor_tensor(sp[:, NEG, :], sp[:, R, :], sp[:, TMP, :], ALU.min))
        dve.wait_ge(sp_act, 1)
        step(nc.vector.tensor_scalar(sp[:, U, :], sp[:, E, :], 1.0, None, ALU.add))
        step(nc.vector.tensor_scalar(sp[:, V, :], sp[:, U, :], -1.0, None, ALU.add))
        step(nc.vector.tensor_scalar(sp[:, M, :], sp[:, V, :], 0.0, None, ALU.is_equal))
        step(nc.vector.tensor_tensor(sp[:, V, :], sp[:, V, :], sp[:, M, :], ALU.add))
        step(nc.vector.reciprocal(sp[:, TMP, :], sp[:, V, :]))
        dve.wait_ge(sp_act, 3)
        step(nc.vector.tensor_tensor(sp[:, L, :], sp[:, L, :], sp[:, M, :], ALU.add))
        step(nc.vector.tensor_tensor(sp[:, L, :], sp[:, L, :], sp[:, TMP, :], ALU.mult))
        step(nc.vector.tensor_tensor(sp[:, L, :], sp[:, L, :], sp[:, E, :], ALU.mult))
        step(nc.vector.scalar_tensor_tensor(out=sp[:, DT, :], in0=sp[:, R, :], scalar=0.0, in1=sp[:, L, :],
                                            op0=ALU.max, op1=ALU.add))
        step(nc.vector.scalar_tensor_tensor(out=v3(DA), in0=v3(DT), scalar=-1.0, in1=bc(3), op0=ALU.mult, op1=ALU.mult))
        assert steps[0] == DT_STEPS
        dve.wait_ge(cs_mm, 1)
        step(nc.vector.tensor_copy(sp[:, CS, :], bank[7][:, 0:HB]))
        assert steps[0] == CS_STEPS

        def decay(b):
            for h in range(NHEADS):
                dve.wait_ge(row_mm, 2 * b + h + 1)
                if b >= 2:
                    dve.wait_ge(s_done, 2 * (b - 2) + h + 1)
                c0, c1 = (2 * b) * NHEADS + h, (2 * b + 1) * NHEADS + h
                nc.vector.tensor_scalar(dec[:, b % 2, h, 0:SEQ], bank[h][:, 0:SEQ], sp[:, CS, c0:c0 + 1], 0.0,
                                        ALU.subtract, ALU.min)
                nc.vector.tensor_scalar(dec[:, b % 2, h, SEQ:], bank[h][:, SEQ:3 * P], sp[:, CS, c1:c1 + 1], 0.0,
                                        ALU.subtract, ALU.min).then_inc(diff_done, 1)

        def masked(b):
            dve.wait_ge(g_mm, b + 1)
            if b >= 2:
                dve.wait_ge(s_done, 2 * (b - 2) + 2)
            nc.vector.tensor_tensor(gm[:, b % 2, :], bank[2][:, 0:3 * P], tri[:, :], ALU.mult).then_inc(g_done, 1)

        def weights(b):
            dve.wait_ge(g_done, b + 1)
            for h in range(NHEADS):
                dve.wait_ge(dec_done, 2 * b + h + 1)
                if b >= 2:
                    dve.wait_ge(y_mm, b - 1)
                c0, c1 = (2 * b) * NHEADS + h, (2 * b + 1) * NHEADS + h
                for lo, hi, c in ((0, SEQ, c0), (SEQ, 3 * P, c1)):
                    ins = nc.vector.scalar_tensor_tensor(out=st[:, b % 2, h, lo:hi], in0=dec[:, b % 2, h, lo:hi],
                                                         scalar=sp[:, DT, c:c + 1], in1=gm[:, b % 2, lo:hi],
                                                         op0=ALU.mult, op1=ALU.mult)
                ins.then_inc(s_done, 1)

        def gate(b):
            dve.wait_ge(y_mm, b + 1)
            if b >= 2:
                dve.wait_ge(o_mm, b - 1)
            for h in range(NHEADS):
                nc.vector.scalar_tensor_tensor(out=yy[:, b % 2, h, :], in0=cv[:, h, b, :], scalar=heads[:, 2, h:h + 1],
                                               in1=bank[4 + b % 2][:, h * SEQ:(h + 1) * SEQ], op0=ALU.mult,
                                               op1=ALU.add).then_inc(y_skip, 1)
            dve.wait_ge(y_skip, 2 * b + 2)
            nc.vector.tensor_tensor(yy[:, b % 2, :, :], yy[:, b % 2, :, :], zs[:, :, b * SEQ:(b + 1) * SEQ],
                                    ALU.mult).then_inc(y_done, 1)

        dve.wait_ge(silu_done, 3 * GROUPS)
        for b in range(BATCH + 1):
            if b < BATCH:
                decay(b)
                masked(b)
            if b:
                gate(b - 1)
            if b < BATCH:
                weights(b)

        added = [0]

        def write_x1(g):
            nc.vector.tensor_tensor(xn[:, tok(g)], xc[:, tok(g)], rstd[:, tok(g)], ALU.mult).then_inc(norm_done, 1)
            dve.wait_ge(norm_done, GROUPS + g + 1)
            nc.vector.tensor_tensor(x1[:, tok(g)], x1[:, tok(g)], xn[:, tok(g)], ALU.add).then_inc(x1_done, 1)

        def write_xs(g):
            for half in range(2):
                rows = slice(DH * half, DH * half + DH)
                nc.vector.tensor_tensor(xs[rows, 2 * g:2 * g + 2, half:half + SEQ],
                                        xc[rows, tok(g)].rearrange("p (b s) -> p b s", b=2),
                                        rstd[rows, tok(g)].rearrange("p (b s) -> p b s", b=2), ALU.mult)\
                    .then_inc(xs_done, 1)

        norm(1, yo(xin), write_x1)
        norm(2, x1, write_xs)


def build_layers(nc, ctx, sb, sem, bank, ident, ones_mean, eps_col, xs, w_qk, w_v, w_o, w_1, w_2,
                 q_scale, k_scale, cols_in, rope, mask_in):
    wh = sb(ctx, "wh", [P, 2, QK_COLS], F32R)
    wl = sb(ctx, "wl", [P, 2, QK_COLS], F32R)
    wv = sb(ctx, "wv", [P, INNER])
    wraw = sb(ctx, "wraw", [P, SPLIT])
    wo = sb(ctx, "wo", [P, PAIRS, DIM])
    w1 = sb(ctx, "w1", [P, 2 * DIM_INNER])
    w2 = sb(ctx, "w2", [P, HC, DIM])
    cols = sb(ctx, "cols", [P, DEPTH, N_COLS])
    tab = sb(ctx, "tab", [P, DEPTH, TILES, 4, DH])
    identb = sb(ctx, "identb", [P, P], BF16)
    maskb = sb(ctx, "maskb", [P, TILES, 2 * WIN], BF16)
    xh = sb(ctx, "xh", [P, SEQ], F32R)
    xl = sb(ctx, "xl", [P, SEQ], F32R)
    xf = sb(ctx, "xf", [P, SEQ])
    qk = [sb(ctx, f"qk{t}", [P, QK_COLS]) for t in range(TILES)]
    rot = sb(ctx, "rot", [P, QK_COLS])
    sqr = sb(ctx, "sqr", [P, 2, 512])
    ss = [sb(ctx, f"ss{t}", [P, 2 * HEADS]) for t in range(TILES)]
    rn = [sb(ctx, f"rn{t}", [P, 2 * HEADS]) for t in range(TILES)]
    qT = [sb(ctx, f"qT{t}", [P, PAIRS, P]) for t in range(TILES)]
    kbd = sb(ctx, "kbd", [P, PAIRS, 2, WIN + SEQ])
    v_odd = sb(ctx, "v_odd", [P, SEQ // (2 * WIN), 2, PAIRS, VW])
    v_even = sb(ctx, "v_even", [P, SEQ // (2 * WIN), 2, PAIRS, VW])
    pr = [sb(ctx, f"pr{t}", [P, PAIRS, 2, 2 * WIN]) for t in range(TILES)]
    mx = sb(ctx, "mx", [P, 2, PAIRS])
    pT = sb(ctx, "pT", [P, PAIRS, P])
    rs = sb(ctx, "rs", [P, 2, 6])
    o = sb(ctx, "o", [P, PAIRS, 2, DH])
    oT = sb(ctx, "oT", [P, PAIRS, SEQ])
    fx = sb(ctx, "fx", [P, SEQ])
    fq = sb(ctx, "fq", [P, SEQ])
    fr = sb(ctx, "fr", [P, SEQ])
    gp = sb(ctx, "gp", [P, HC, SEQ])
    ap = sb(ctx, "ap", [P, HC, SEQ])

    proj_bank, sc_bank, tr_bank, pv_bank, f_bank = bank[0:2], bank[2:4], bank[4:6], bank[6], bank[7]

    first_dma = sem(ctx, "first_dma")
    scale_dma = sem(ctx, "scale_dma")
    zeroed = sem(ctx, "zeroed")
    consts_done = sem(ctx, "consts_done")
    raw_dma = sem(ctx, "raw_dma")
    wv_dma = sem(ctx, "wv_dma")
    split_hi = sem(ctx, "split_hi")
    split_done = sem(ctx, "split_done")
    wo_dma = sem(ctx, "wo_dma")
    w1_dma = sem(ctx, "w1_dma")
    w2_dma = sem(ctx, "w2_dma")
    x_hi = sem(ctx, "x_hi")
    x_staged = sem(ctx, "x_staged")
    proj_mm = sem(ctx, "proj_mm")
    squared = sem(ctx, "squared")
    roped = sem(ctx, "roped")
    sums_done = sem(ctx, "sums_done")
    floored = sem(ctx, "floored")
    rn_log = sem(ctx, "rn_log")
    rn_done = sem(ctx, "rn_done")
    rope_added = sem(ctx, "rope_added")
    qk_done = sem(ctx, "qk_done")
    tr_mm = sem(ctx, "tr_mm")
    tr_evac = sem(ctx, "tr_evac")
    sc_mm = sem(ctx, "sc_mm")
    max_done = sem(ctx, "max_done")
    sc_evac = sem(ctx, "sc_evac")
    exp_done = sem(ctx, "exp_done")
    v_evac = sem(ctx, "v_evac")
    ve_dma = sem(ctx, "ve_dma")
    pv_mm = sem(ctx, "pv_mm")
    recip_done = sem(ctx, "recip_done")
    pv_evac = sem(ctx, "pv_evac")
    f_mm = sem(ctx, "f_mm")
    res1 = sem(ctx, "res1")
    f_centred = sem(ctx, "f_centred")
    f_squared = sem(ctx, "f_squared")
    f_log = sem(ctx, "f_log")
    f_rstd = sem(ctx, "f_rstd")
    f_scaled = sem(ctx, "f_scaled")
    f_norm = sem(ctx, "f_norm")
    h_evac = sem(ctx, "h_evac")
    gelu_done = sem(ctx, "gelu_done")
    h_done = sem(ctx, "h_done")
    state_ready = sem(ctx, "state_ready")

    TQ, PT, OT = (0, 6), (4, 12), (10, 14)

    def over_units(eng, body):
        for it in (-1, 0, 1):
            body(it)
        with eng.Fori(2, UNITS - 1) as it:
            body(it)
        for it in (UNITS - 1, UNITS):
            body(it)

    def has(it, lag):
        return not isinstance(it, int) or 0 <= it + lag < UNITS

    block = ctx.enter_context(nc.Block())

    @block.sync
    def _(sync):
        for n, (dst, src) in enumerate(((wo[:, :, :], w_o[0].rearrange("p (n d) -> p n d", n=PAIRS)),
                                        (w1[:, :], w_1[0]),
                                        (w2[:, :, :], w_2[0].rearrange("p (n d) -> p n d", n=HC)))):
            sync.dma_start(dst, src).then_inc((wo_dma, w1_dma, w2_dma)[n], 16)
        sync.dma_start(wv[:, :], w_v[0]).then_inc(wv_dma, 16)
        sync.dma_start(qk[0][:, :], w_qk[0]).then_inc(first_dma, 16)
        sync.dma_start(cols[:, :, :], cols_in).then_inc(first_dma, 16)
        sync.dma_start(qk[1][:, 0:TILES * 4 * DH], rope).then_inc(scale_dma, 16)
        for n, row in enumerate((q_scale, k_scale)):
            at = TILES * 4 * DH + n * 2 * DEPTH * DH
            dst = qk[1][:, at:at + 2 * DEPTH * DH].rearrange("p (w l d) -> p w l d", w=2, l=DEPTH)
            whole_row = row.partition_broadcast(P)
            sync.dma_start(dst[:, 0, :, :], whole_row).then_inc(scale_dma, 16)
            sync.dma_start(dst[:, 1, :, 0:WIN], whole_row[:, :, WIN:DH]).then_inc(scale_dma, 16)
            sync.dma_start(dst[:, 1, :, WIN:DH], whole_row[:, :, 0:WIN]).then_inc(scale_dma, 16)
        sync.dma_start(rot[:, 0:TILES * 2 * WIN], mask_in).then_inc(scale_dma, 16)

        def ahead(value):
            if not isinstance(value, int):
                sync.to_reg(value)
            return value

        def unit_loads(v):
            part, dram_layer = v % BATCH, (v // BATCH + 1) % DEPTH
            src = w_qk[bass.ds(dram_layer, 1), :, bass.ds(part * SPLIT, SPLIT)].rearrange("l p n -> (l p) n")
            projected, split_before = ahead(N_PROJ * v), ahead(v + 1)
            ahead((dram_layer * (DIM * QK_COLS) + part * SPLIT) * 4)
            if started(v):
                sync.wait_ge(proj_mm, projected)
            sync.wait_ge(split_done, split_before)
            sync.dma_start(wraw[:, :], src).then_inc(raw_dma, 16)

        def value_weights(layer):
            sync.dma_start(wv[:, :], w_v[bass.ds(layer, 1)].rearrange("l p n -> (l p) n")).then_inc(wv_dma, 16)

        def even_values(v):
            written = ahead(4 * v + 4)
            sync.wait_ge(v_evac, written)
            for half in range(2):
                for odd in range(2):
                    r = slice(64 * half + 32 * odd, 64 * half + 32 * odd + 32)
                    n = SEQ // (2 * WIN) - odd
                    sync.dma_start(v_even[r, odd:odd + n, half, :, :], v_odd[r, 0:n, half, :, :]).then_inc(ve_dma, 16)

        def reload(layer):
            last = N_F * (BATCH * layer - 1)
            at = bass.ds(layer, 1)
            src_o = w_o[at].rearrange("l p (n d) -> (l p) n d", n=PAIRS)
            src_1 = w_1[at].rearrange("l p n -> (l p) n")
            src_2 = w_2[at].rearrange("l p (n d) -> (l p) n d", n=HC)
            counts = [ahead(last + k) for k in (1, 6, 7)]
            for size in (INNER * DIM, DIM * 2 * DIM_INNER, HC * P * DIM):
                ahead(layer * size * 4)
            sync.wait_ge(f_mm, counts[0])
            sync.dma_start(wo[:, :, :], src_o).then_inc(wo_dma, 16)
            sync.wait_ge(f_mm, counts[1])
            sync.dma_start(w1[:, :], src_1).then_inc(w1_dma, 16)
            sync.wait_ge(f_mm, counts[2])
            sync.dma_start(w2[:, :, :], src_2).then_inc(w2_dma, 16)

        sync.wait_ge(zeroed, 4)
        for v in range(2):
            unit_loads(v)
            even_values(v)
        with sync.Fori(0, DEPTH - 1) as layer:
            with sync.Fori(2, BATCH) as part:
                unit_loads(layer * BATCH + part)
                even_values(layer * BATCH + part)
            unit_loads(layer * BATCH + BATCH)
            value_weights(layer + 1)
            even_values(layer * BATCH + BATCH)
            unit_loads(layer * BATCH + BATCH + 1)
            even_values(layer * BATCH + BATCH + 1)
            reload(layer + 1)
        with sync.Fori(UNITS - BATCH + 2, UNITS) as v:
            unit_loads(v)
            even_values(v)



    @block.gpsimd
    def _(pool):
        nc.gpsimd.memset(kbd[:, :, :, :], 0.0).then_inc(zeroed, 1)
        for v in (v_odd, v_even):
            nc.gpsimd.memset(v[:, :, :, :, :], 0.0).then_inc(zeroed, 1)
        nc.gpsimd.memset(gp[:, :, :], 0.0).then_inc(zeroed, 1)
        nc.gpsimd.memset(ap[:, :, :], 0.0).then_inc(zeroed, 1)
        pool.wait_ge(zeroed, 5)
        for half in range(2):
            r = slice(64 * half, 64 * half + 64)
            for v in (v_odd, v_even):
                nc.gpsimd.memset(v[r, :, half, :, DH:VW], 1.0).then_inc(zeroed, 1)

        def rope_norm(u, t):
            n = 2 * u + t
            for half in range(2):
                r = slice(half * INNER, (half + 1) * INNER)
                pool.wait_ge(roped, 4 * n + 2 * half + 2)
                nc.gpsimd.tensor_tensor(qk[t][:, r], qk[t][:, r], rot[:, r], ALU.add).then_inc(rope_added, 1)
            pool.wait_ge(rn_done, n + 1)
            for half in range(2):
                r = slice(half * INNER, (half + 1) * INNER)
                pool.wait_ge(rope_added, 2 * n + half + 1)
                v = qk[t][:, r].rearrange("p (h d) -> p h d", d=DH)
                w = rn[t][:, half * HEADS:(half + 1) * HEADS].unsqueeze(2).broadcast_to([P, HEADS, DH])
                nc.gpsimd.tensor_tensor(v, v, w, ALU.mult).then_inc(qk_done, 1)

        def hidden(u):
            pool.wait_ge(gelu_done, u + 1)
            nc.gpsimd.tensor_tensor(gp[:, :, :], gp[:, :, :], ap[:, :, :], ALU.mult).then_inc(h_done, 1)

        def body(it):
            if has(it, 1):
                rope_norm(it + 1, 0)
            if has(it, -1):
                hidden(it - 1)
            if has(it, 1):
                rope_norm(it + 1, 1)

        over_units(pool, body)

    @block.tensor
    def _(pe):
        pe.wait_ge(consts_done, 4)
        pe.wait_ge(zeroed, 9)

        def project_qk(v, t):
            layer = v // BATCH
            par = layer % 2
            pe.wait_ge(x_staged, v + 1)
            pe.wait_ge(split_done, BATCH * layer + 1)
            for c in range(4):
                n = 4 * t + c
                if n >= 2:
                    pe.wait_ge(roped, 8 * v + n - 1)
                elif started(v):
                    pe.wait_ge(v_evac, 4 * v - 1 + n)
                dst = proj_bank[n % 2][:, :]
                tile = slice(t * P, (t + 1) * P)
                w_hi = wh[:, bass.ds(par, 1), c * 512:(c + 1) * 512].rearrange("p l n -> p (l n)")
                w_lo = wl[:, bass.ds(par, 1), c * 512:(c + 1) * 512].rearrange("p l n -> p (l n)")
                nc.tensor.matmul(dst, xh[:, tile], w_hi, start=True, stop=False)
                nc.tensor.matmul(dst, xh[:, tile], w_lo, start=False, stop=False)
                nc.tensor.matmul(dst, xl[:, tile], w_hi, start=False, stop=True).then_inc(proj_mm, 1)

        def project_v(v, slot):
            layer = v // BATCH
            n = 8 + slot
            if slot == 0:
                pe.wait_ge(wv_dma, 16 * (layer + 1))
            if slot < 2:
                pe.wait_ge(roped, 8 * v + n - 1)
            else:
                pe.wait_ge(v_evac, 4 * v + slot - 1)
            for half in range(2):
                for odd in range(2):
                    r = 64 * half + 32 * odd
                    w = WIN * (2 * slot + odd)
                    mm = nc.tensor.matmul(proj_bank[n % 2][r:r + 32, :], xf[:, w:w + WIN],
                                          wv[:, half * 512:(half + 1) * 512], start=True, stop=True)
            mm.then_inc(proj_mm, 1)

        def tr_bank_free(u, idx):
            n = idx - 1
            if not isinstance(u, int) or N_TR * u + n > 0:
                pe.wait_ge(tr_evac, N_TR * u + n)
            return tr_bank[idx % 2]

        def transpose_qk(u, t):
            for c in range(4):
                pe.wait_ge(qk_done, 4 * u + 2 * t + c // 2 + 1)
                dst = tr_bank_free(u, TQ[t] + c)
                for m in range(4):
                    mm = nc.tensor.transpose(dst[:, m * P:(m + 1) * P], qk[t][:, (4 * c + m) * P:(4 * c + m + 1) * P],
                                             ident[:, :])
                mm.then_inc(tr_mm, 1)

        def score(u, t):
            for n in range(2):
                last = 4 * u + 2 * t + n - 1
                if started(last):
                    pe.wait_ge(sc_evac, last)
                pe.wait_ge(tr_evac, N_TR * u + TQ[t] + 3 + n)
                dst = sc_bank[n]
                nc.tensor.matmul(dst[:, :], identb[:, :], maskb[:, t, :].unsqueeze(1).broadcast_to([P, 8, 2 * WIN]),
                                 start=True, stop=False, skip_group_check=True)
                for m in range(4):
                    for j in range(4):
                        w = 4 * t + j
                        keys = kbd[:, 4 * n + m, :, WIN * w:WIN * w + 2 * WIN]
                        if w % 2 == 0:
                            keys = keys.rearrange("p b (k c) -> p b k c", k=2)[:, :, ::-1, :]
                        mm = nc.tensor.matmul(dst[32 * j:32 * j + 32, m * P:(m + 1) * P],
                                              qT[t][:, 4 * n + m, WIN * j:WIN * j + WIN], keys,
                                              start=False, stop=True, skip_group_check=True)
                mm.then_inc(sc_mm, 1)

        def transpose_p(u, t):
            for m in range(2):
                pe.wait_ge(exp_done, 4 * u + 2 * t + m + 1)
                dst = tr_bank_free(u, PT[t] + m)
                for k in range(4):
                    mm = nc.tensor.transpose(dst[:, k * P:(k + 1) * P], pr[t][:, 4 * m + k, :, :].rearrange("p b c -> p (b c)"),
                                             ident[:, :])
                mm.then_inc(tr_mm, 1)

        def attend(u, t, c):
            last = N_PV * u + 3 * t + c
            if started(last):
                pe.wait_ge(pv_evac, last)
            lo, hi = PV_CHUNKS[c]
            if c == 0:
                pe.wait_ge(tr_evac, N_TR * u + PT[t] + 2)
                if t == 0:
                    pe.wait_ge(ve_dma, 64 * (u + 1))
                    pe.wait_ge(v_evac, 4 * u + 4)
            for k in range(lo, hi):
                for j in range(4):
                    v = v_odd if j % 2 else v_even
                    mm = nc.tensor.matmul(pv_bank[32 * j:32 * j + 32, (k - lo) * 2 * VW:(k - lo + 1) * 2 * VW],
                                          pT[:, k, WIN * j:WIN * j + WIN], v[:, 2 * t + j // 2, :, k, :],
                                          start=True, stop=True, skip_group_check=True)
            mm.then_inc(pv_mm, 1)

        def transpose_o(u, t):
            for m in range(2):
                pe.wait_ge(pv_evac, N_PV * u + 3 * t + 2 + m)
                dst = tr_bank_free(u, OT[t] + m)
                for k in range(4):
                    mm = nc.tensor.transpose(dst[:, k * P:(k + 1) * P], o[:, 4 * m + k, :, :].rearrange("p b d -> p (b d)"),
                                             ident[:, :])
                mm.then_inc(tr_mm, 1)

        def out_proj(u):
            pe.wait_ge(wo_dma, 16 * (u // BATCH + 1))
            pe.wait_ge(tr_evac, N_TR * (u + 1))
            if started(u):
                pe.wait_ge(state_ready, BATCH + u)
            for k in range(PAIRS):
                mm = nc.tensor.matmul(f_bank[:, 0:SEQ], wo[:, k, :], oT[:, k, :], start=(k == 0), stop=(k == PAIRS - 1))
            mm.then_inc(f_mm, 1)

        def norm_mean(u):
            pe.wait_ge(res1, u + 1)
            nc.tensor.matmul(f_bank[:, 0:SEQ], ones_mean[:, :],
                             xs[:, bass.ds(u % BATCH, 1), 0:SEQ].rearrange("p b s -> p (b s)"),
                             start=True, stop=True).then_inc(f_mm, 1)

        def norm_var(u):
            pe.wait_ge(f_squared, u + 1)
            nc.tensor.matmul(f_bank[:, 0:SEQ], ones_mean[:, :], fq[:, :], start=True, stop=True).then_inc(f_mm, 1)

        def ffn_in(u, c):
            rows = P if c < HC - 1 else HLAST
            if c == 0:
                pe.wait_ge(w1_dma, 16 * (u // BATCH + 1))
                pe.wait_ge(f_norm, u + 1)
            else:
                pe.wait_ge(h_evac, HC * u + c)
            nc.tensor.matmul(f_bank[0:rows, 0:SEQ], w1[:, c * P:c * P + rows], fx[:, :], start=True, stop=True,
                             skip_group_check=True)
            nc.tensor.matmul(f_bank[0:rows, SEQ:2 * SEQ], w1[:, DIM_INNER + c * P:DIM_INNER + c * P + rows], fx[:, :],
                             start=True, stop=True, skip_group_check=True).then_inc(f_mm, 1)

        def ffn_out(u):
            pe.wait_ge(w2_dma, 16 * (u // BATCH + 1))
            pe.wait_ge(h_done, u + 1)
            for c in range(HC):
                mm = nc.tensor.matmul(f_bank[:, 0:SEQ], w2[:, c, :], gp[:, c, :], start=(c == 0), stop=(c == HC - 1))
            mm.then_inc(f_mm, 1)

        def body(it):
            proj, attn, ffn = has(it, 1), has(it, 0), has(it, -1)
            if attn:
                transpose_qk(it, 0)
            if ffn:
                out_proj(it - 1)
            if attn:
                score(it, 0)
            if ffn:
                norm_mean(it - 1)
            if proj:
                project_qk(it + 1, 0)
            if ffn:
                norm_var(it - 1)
            if attn:
                transpose_p(it, 0)
                transpose_qk(it, 1)
            for c in range(3):
                if attn:
                    attend(it, 0, c)
                if ffn:
                    ffn_in(it - 1, c)
            if attn:
                score(it, 1)
                transpose_o(it, 0)
            if proj:
                project_qk(it + 1, 1)
                project_v(it + 1, 0)
            if attn:
                transpose_p(it, 1)
            if proj:
                project_v(it + 1, 1)
            for c in range(3):
                if attn:
                    attend(it, 1, c)
                if c == 0 and ffn:
                    ffn_out(it - 1)
            if proj:
                project_v(it + 1, 2)
                project_v(it + 1, 3)
            if attn:
                transpose_o(it, 1)

        over_units(pe, body)

    @block.scalar
    def _(act):
        act.wait_ge(first_dma, 32)
        act.wait_ge(zeroed, 9)

        def evac_qk(u, t):
            for c in range(4):
                act.wait_ge(tr_mm, N_TR * u + TQ[t] + c + 1)
                src = tr_bank[c % 2][:, :].rearrange("p (m s) -> p m s", m=4)
                if c < 2:
                    if c == 0 and started(u):
                        act.wait_ge(sc_mm, 4 * (u - 1) + 2 * t + 2)
                    nc.scalar.copy(qT[t][:, 4 * c:4 * c + 4, :], src).then_inc(tr_evac, 1)
                else:
                    k0 = 4 * (c - 2)
                    at = slice(WIN + t * P, WIN + (t + 1) * P)
                    if c == 2 and started(u):
                        act.wait_ge(sc_mm, 4 * u)
                    nc.scalar.copy(kbd[0:DH, k0:k0 + 4, 0, at], src[0:DH])
                    nc.scalar.copy(kbd[DH:P, k0:k0 + 4, 1, at], src[DH:P]).then_inc(tr_evac, 1)

        def exps(u, t):
            for n in range(2):
                act.wait_ge(sc_evac, 4 * u + 2 * t + n + 1)
                v = pr[t][:, 4 * n:4 * n + 4, :, :]
                nc.scalar.activation(v, v, ACT.Exp).then_inc(exp_done, 1)

        def evac_pt(u, t):
            for m in range(2):
                act.wait_ge(tr_mm, N_TR * u + PT[t] + m + 1)
                if m == 0 and started(2 * u + t if isinstance(u, int) else u):
                    act.wait_ge(pv_mm, N_PV * u + 3 * t)
                nc.scalar.copy(pT[:, 4 * m:4 * m + 4, :], tr_bank[(PT[t] + m) % 2][:, :].rearrange("p (k s) -> p k s", k=4))\
                    .then_inc(tr_evac, 1)

        def evac_ot(u, t):
            for m in range(2):
                act.wait_ge(tr_mm, N_TR * u + OT[t] + m + 1)
                if m == 0 and t == 0 and started(u):
                    act.wait_ge(f_mm, N_F * (u - 1) + 1)
                nc.scalar.copy(oT[:, 4 * m:4 * m + 4, t * P:(t + 1) * P],
                               tr_bank[(OT[t] + m) % 2][:, :].rearrange("p (k s) -> p k s", k=4)).then_inc(tr_evac, 1)

        def squares(v, t):
            for c in range(4):
                n = 8 * v + 4 * t + c
                act.wait_ge(proj_mm, N_PROJ * v + 4 * t + c + 1)
                if not isinstance(n, int) or n >= 2:
                    act.wait_ge(sums_done, n - 1)
                nc.scalar.activation(sqr[:, c % 2, :], proj_bank[c % 2][:, :], ACT.Square).then_inc(squared, 1)

        def inverse_norms(v, t):
            n = 2 * v + t
            act.wait_ge(floored, n + 1)
            if started(v):
                act.wait_ge(qk_done, 2 * (n - 2) + 2)
            nc.scalar.activation(rn[t][:, :], ss[t][:, :], ACT.Ln).then_inc(rn_log, 1)
            act.wait_ge(rn_log, n + 1)
            nc.scalar.activation(rn[t][:, :], rn[t][:, :], ACT.Exp, scale=-0.5).then_inc(rn_done, 1)

        def evac_v(v, slot):
            act.wait_ge(proj_mm, N_PROJ * v + 8 + slot + 1)
            if slot == 0 and started(v):
                act.wait_ge(ve_dma, 64 * v)
                act.wait_ge(pv_mm, N_PV * (v - 1) + 3)
            if slot == 2 and started(v):
                act.wait_ge(pv_mm, N_PV * v)
            src = proj_bank[slot % 2]
            nc.scalar.copy(v_odd[0:DH, slot, 0, :, 0:DH], src[0:DH, :].rearrange("p (h d) -> p h d", d=DH))
            nc.scalar.copy(v_odd[DH:P, slot, 1, :, 0:DH], src[DH:P, :].rearrange("p (h d) -> p h d", d=DH))\
                .then_inc(v_evac, 1)

        def norm_square(u):
            act.wait_ge(f_centred, u + 1)
            if started(u):
                act.wait_ge(f_mm, N_F * (u - 1) + 3)
            nc.scalar.activation(fq[:, :], fx[:, :], ACT.Square).then_inc(f_squared, 1)

        def norm_root(u):
            act.wait_ge(f_mm, N_F * u + 3)
            if started(u):
                act.wait_ge(f_scaled, u)
            nc.scalar.activation(fr[:, :], f_bank[:, 0:SEQ], ACT.Ln, bias=eps_col[:, 0:1]).then_inc(f_log, 1)
            act.wait_ge(f_log, u + 1)
            nc.scalar.activation(fr[:, :], fr[:, :], ACT.Exp, scale=-0.5).then_inc(f_rstd, 1)

        def evac_hidden(u, c):
            rows = P if c < HC - 1 else HLAST
            layer = u // BATCH
            act.wait_ge(f_mm, N_F * u + 4 + c)
            if c == 0 and started(u):
                act.wait_ge(f_mm, N_F * u)
            for dst, half, col in ((ap, 0, C_B1A), (gp, 1, C_B1G)):
                ins = nc.scalar.activation(dst[0:rows, c, :], f_bank[0:rows, half * SEQ:(half + 1) * SEQ], ACT.Identity,
                                           bias=cols[0:rows, bass.ds(layer, 1), col + c:col + c + 1].rearrange("p l c -> p (l c)"))
            ins.then_inc(h_evac, 1)

        def gelu(u):
            act.wait_ge(h_evac, HC * (u + 1))
            nc.scalar.activation(gp[:, :, :], gp[:, :, :], ACT.Gelu).then_inc(gelu_done, 1)

        def body(it):
            proj, attn, ffn = has(it, 1), has(it, 0), has(it, -1)
            if attn:
                evac_qk(it, 0)
                exps(it, 0)
            if ffn:
                norm_square(it - 1)
            if proj:
                squares(it + 1, 0)
            if ffn:
                norm_root(it - 1)
            if attn:
                evac_pt(it, 0)
                evac_qk(it, 1)
            if proj:
                inverse_norms(it + 1, 0)
            if ffn:
                for c in range(HC):
                    evac_hidden(it - 1, c)
            if attn:
                exps(it, 1)
                evac_ot(it, 0)
            if ffn:
                gelu(it - 1)
            if proj:
                squares(it + 1, 1)
                evac_v(it + 1, 0)
            if attn:
                evac_pt(it, 1)
            if proj:
                evac_v(it + 1, 1)
                inverse_norms(it + 1, 1)
                evac_v(it + 1, 2)
                evac_v(it + 1, 3)
            if attn:
                evac_ot(it, 1)

        over_units(act, body)

    @block.vector
    def _(dve):
        dve.wait_ge(scale_dma, 16 * 8)
        base = qk[1][:, 0:TILES * 4 * DH].rearrange("p (t k d) -> p t k d", t=TILES, k=4)
        for t in range(TILES):
            for kind in range(4):
                at = TILES * 4 * DH + kind * DEPTH * DH
                row = qk[1][:, at:at + DEPTH * DH].rearrange("p (l d) -> p l d", l=DEPTH)
                ins = nc.vector.tensor_tensor(tab[:, :, t, kind, :], row,
                                              base[:, t, kind, :].unsqueeze(1).broadcast_to([P, DEPTH, DH]), ALU.mult)
        ins.then_inc(consts_done, 1)
        nc.vector.tensor_copy(maskb[:, :, :], rot[:, 0:TILES * 2 * WIN].rearrange("p (t c) -> p t c", t=TILES)).then_inc(consts_done, 1)
        nc.vector.tensor_copy(identb[:, :], ident[:, :]).then_inc(consts_done, 1)
        nc.vector.memset(ss[0][:, :], 0.0).then_inc(state_ready, BATCH)
        dve.wait_ge(first_dma, 32)
        nc.vector.tensor_copy(wh[:, 0, :], qk[0][:, :]).then_inc(consts_done, 1)
        dve.wait_ge(consts_done, 4)
        nc.vector.tensor_tensor(wl[:, 0, :], qk[0][:, :], wh[:, 0, :].bitcast(F32), ALU.subtract).then_inc(split_done, 1)
        dve.wait_ge(split_done, 1)

        def stage(v):
            src = xs[:, bass.ds(v % BATCH, 1), 0:SEQ].rearrange("p b s -> p (b s)")
            if started(v):
                dve.wait_ge(proj_mm, N_PROJ * v)
            dve.wait_ge(state_ready, v + 1)
            nc.vector.tensor_copy(xf[:, :], src)
            nc.vector.tensor_copy(xh[:, :], src).then_inc(x_hi, 1)
            dve.wait_ge(x_hi, v + 1)
            nc.vector.tensor_tensor(xl[:, :], src, xh[:, :].bitcast(F32), ALU.subtract).then_inc(x_staged, 1)

        def split(v):
            par = (v // BATCH + 1) % 2
            r = bass.ds((v % BATCH) * SPLIT, SPLIT)
            hi = wh[:, bass.ds(par, 1), r].rearrange("p l n -> p (l n)")
            lo = wl[:, bass.ds(par, 1), r].rearrange("p l n -> p (l n)")
            dve.wait_ge(raw_dma, 16 * (v + 1))
            nc.vector.tensor_copy(hi, wraw[:, :]).then_inc(split_hi, 1)
            dve.wait_ge(split_hi, v + 1)
            nc.vector.tensor_tensor(lo, wraw[:, :], hi.bitcast(F32), ALU.subtract).then_inc(split_done, 1)

        def rotate(v, t):
            layer = v // BATCH
            for c in range(4):
                n = 4 * t + c
                kind = 2 * (c // 2)
                dve.wait_ge(squared, 8 * v + n + 1)
                if c == 0:
                    if started(2 * v + t if isinstance(v, int) else v):
                        dve.wait_ge(rope_added, 2 * (2 * v + t))
                    if started(v):
                        dve.wait_ge(tr_mm, N_TR * (v - 1) + TQ[t] + 4)
                        dve.wait_ge(rn_log, 2 * v + t - 1)
                src = proj_bank[n % 2][:, :].rearrange("p (h a d) -> p h a d", a=2, d=WIN)
                cos = tab[:, bass.ds(layer, 1), t, kind, :].broadcast_to([P, 8, DH])
                sin = tab[:, bass.ds(layer, 1), t, kind + 1, :].broadcast_to([P, 8, DH])
                r = slice(c * 512, (c + 1) * 512)
                nc.vector.tensor_tensor(qk[t][:, r].rearrange("p (h d) -> p h d", d=DH),
                                        proj_bank[n % 2][:, :].rearrange("p (h d) -> p h d", d=DH), cos, ALU.mult)
                nc.vector.tensor_tensor(rot[:, r].rearrange("p (h a d) -> p h a d", a=2, d=WIN), src[:, :, ::-1, :],
                                        sin.rearrange("p h (a d) -> p h a d", a=2), ALU.mult).then_inc(roped, 1)
                nc.vector.tensor_reduce(ss[t][:, c * 8:(c + 1) * 8], sqr[:, c % 2, :].rearrange("p (h d) -> p h d", d=DH),
                                        AX.X, ALU.add).then_inc(sums_done, 1)
            dve.wait_ge(sums_done, 8 * v + 4 * t + 4)
            nc.vector.tensor_scalar(ss[t][:, :], ss[t][:, :], 1e-24, None, ALU.max).then_inc(floored, 1)

        def softmax_max(u, t):
            for n in range(2):
                k = 4 * u + 2 * t + n
                dve.wait_ge(sc_mm, k + 1)
                src = sc_bank[n][:, :].rearrange("p (h c) -> p h c", c=2 * WIN)
                nc.vector.tensor_reduce(mx[:, n, :], src, AX.X, ALU.max).then_inc(max_done, 1)
                dve.wait_ge(max_done, k + 1)
                if n == 0 and started(u):
                    dve.wait_ge(tr_mm, N_TR * (u - 1) + PT[t] + 2)
                nc.vector.tensor_tensor(pr[t][:, 4 * n:4 * n + 4, :, :].rearrange("p k b c -> p (k b) c"), src,
                                        mx[:, n, :].unsqueeze(2).broadcast_to([P, 8, 2 * WIN]), ALU.subtract)\
                    .then_inc(sc_evac, 1)

        def normalise(u, t):
            for c, (lo, hi) in enumerate(PV_CHUNKS):
                n = N_PV * u + 3 * t + c
                m = 2 * (hi - lo)
                dve.wait_ge(pv_mm, n + 1)
                src = pv_bank[:, 0:m * VW].rearrange("p (h e) -> p h e", e=VW)
                nc.vector.reciprocal(rs[:, c % 2, 0:m], src[:, :, DH]).then_inc(recip_done, 1)
                dve.wait_ge(recip_done, n + 1)
                if c == 0:
                    if t == 1:
                        dve.wait_ge(tr_mm, N_TR * u + OT[0] + 2)
                    elif started(u):
                        dve.wait_ge(tr_mm, N_TR * u)
                nc.vector.tensor_tensor(o[:, lo:hi, :, :].rearrange("p k b d -> p (k b) d"), src[:, :, 0:DH],
                                        rs[:, c % 2, 0:m].unsqueeze(2).broadcast_to([P, m, DH]), ALU.mult).then_inc(pv_evac, 1)

        def halves(u):
            b = bass.ds(u % BATCH, 1)
            for half in range(2):
                r = slice(64 * half, 64 * half + 64)
                yield r, xs[r, b, half:half + SEQ].rearrange("p b s -> p (b s)")

        def residual1(u):
            dve.wait_ge(f_mm, N_F * u + 1)
            for r, v in halves(u):
                ins = nc.vector.tensor_tensor(v, f_bank[r, 0:SEQ], v, ALU.add)
            ins.then_inc(res1, 1)

        def norm_centre(u):
            dve.wait_ge(f_mm, N_F * u + 2)
            nc.vector.tensor_tensor(fx[:, :], xs[:, bass.ds(u % BATCH, 1), 0:SEQ].rearrange("p b s -> p (b s)"),
                                    f_bank[:, 0:SEQ], ALU.subtract).then_inc(f_centred, 1)

        def norm_scale(u):
            layer = bass.ds(u // BATCH, 1)
            g, b = (cols[:, layer, c:c + 1].rearrange("p l c -> p (l c)") for c in (C_G, C_B))
            dve.wait_ge(f_rstd, u + 1)
            nc.vector.scalar_tensor_tensor(out=fx[:, :], in0=fx[:, :], scalar=g, in1=fr[:, :], op0=ALU.mult,
                                           op1=ALU.mult).then_inc(f_scaled, 1)
            dve.wait_ge(f_scaled, u + 1)
            nc.vector.tensor_scalar(fx[:, :], fx[:, :], b, None, ALU.add).then_inc(f_norm, 1)

        def residual2(u):
            layer = bass.ds(u // BATCH, 1)
            dve.wait_ge(f_mm, N_F * u + 7)
            for r, v in halves(u):
                ins = nc.vector.scalar_tensor_tensor(out=v, in0=f_bank[r, 0:SEQ],
                                                     scalar=cols[r, layer, C_B2:C_B2 + 1].rearrange("p l c -> p (l c)"),
                                                     in1=v, op0=ALU.add, op1=ALU.add)
            ins.then_inc(state_ready, 1)

        def body(it):
            proj, attn, ffn = has(it, 1), has(it, 0), has(it, -1)
            if proj:
                stage(it + 1)
            if ffn:
                residual1(it - 1)
            if attn:
                softmax_max(it, 0)
            if ffn:
                norm_centre(it - 1)
            if proj:
                rotate(it + 1, 0)
            if ffn:
                norm_scale(it - 1)
            if attn:
                normalise(it, 0)
                softmax_max(it, 1)
            if proj:
                rotate(it + 1, 1)
            if attn:
                normalise(it, 1)
            if ffn:
                residual2(it - 1)
            if proj:
                split(it + 1)

        over_units(dve, body)


def build_last(nc, ctx, sb, sem, bank, ident, ones_mean, eps_col, x1, xs, out):
    y = sb(ctx, "y", [P, TOK])
    xc = sb(ctx, "xc2", [P, TOK])
    sq = sb(ctx, "sq2", [P, TOK])
    rstd = sb(ctx, "rstd2", [P, TOK])
    res = sb(ctx, "res", [P, TOK])
    copied = sem(ctx, "l_copied")
    mean_mm = sem(ctx, "l_mean_mm")
    centred = sem(ctx, "l_centred")
    squared = sem(ctx, "l_squared")
    var_mm = sem(ctx, "l_var_mm")
    log_done = sem(ctx, "l_log_done")
    rstd_done = sem(ctx, "l_rstd_done")
    scaled = sem(ctx, "l_scaled")
    added = sem(ctx, "l_added")
    out_mm = sem(ctx, "l_out_mm")
    out_evac = sem(ctx, "l_out_evac")
    stored = sem(ctx, "l_stored")

    def tok(g):
        return slice(g * GT, (g + 1) * GT)

    block = ctx.enter_context(nc.Block())

    @block.sync
    def _(sync):
        ov = out.rearrange("b (t p) d -> p (b t) d", p=P)
        for g in range(GROUPS):
            sync.wait_ge(out_evac, g + 1)
            sync.dma_start(ov[:, 4 * g:4 * g + 4, :], res[:, tok(g)].rearrange("p (t d) -> p t d", d=DIM)).then_inc(stored, 16)
        sync.wait_ge(stored, 16 * GROUPS)

    @block.tensor
    def _(pe):
        for g in range(GROUPS):
            pe.wait_ge(copied, g + 1)
            nc.tensor.matmul(bank[g][:, :], ones_mean[:, :], y[:, tok(g)], start=True, stop=True).then_inc(mean_mm, 1)
        for g in range(GROUPS):
            pe.wait_ge(squared, g + 1)
            nc.tensor.matmul(bank[4 + g][:, :], ones_mean[:, :], sq[:, tok(g)], start=True, stop=True).then_inc(var_mm, 1)
        for g in range(GROUPS):
            pe.wait_ge(added, g + 1)
            for t in range(4):
                mm = nc.tensor.transpose(bank[g][:, t * P:(t + 1) * P], xc[:, g * GT + t * P:g * GT + (t + 1) * P], ident[:, :])
            mm.then_inc(out_mm, 1)

    @block.scalar
    def _(act):
        for g in range(GROUPS):
            act.wait_ge(centred, g + 1)
            nc.scalar.activation(sq[:, tok(g)], xc[:, tok(g)], ACT.Square).then_inc(squared, 1)
        for g in range(GROUPS):
            act.wait_ge(var_mm, g + 1)
            nc.scalar.activation(rstd[:, tok(g)], bank[4 + g][:, :], ACT.Ln, bias=eps_col[:, 0:1]).then_inc(log_done, 1)
            act.wait_ge(log_done, g + 1)
            nc.scalar.activation(rstd[:, tok(g)], rstd[:, tok(g)], ACT.Exp, scale=-0.5).then_inc(rstd_done, 1)
        for g in range(GROUPS):
            act.wait_ge(out_mm, g + 1)
            nc.scalar.copy(res[:, tok(g)], bank[g][:, :]).then_inc(out_evac, 1)

    @block.vector
    def _(dve):
        for g in range(GROUPS):
            for half in range(2):
                r = slice(64 * half, 64 * half + 64)
                ins = nc.vector.tensor_copy(y[r, tok(g)].rearrange("p (b s) -> p b s", b=2), xs[r, 2 * g:2 * g + 2, half:half + SEQ])
            ins.then_inc(copied, 1)
        for g in range(GROUPS):
            dve.wait_ge(mean_mm, g + 1)
            dve.wait_ge(copied, g + 1)
            nc.vector.tensor_tensor(xc[:, tok(g)], y[:, tok(g)], bank[g][:, :], ALU.subtract).then_inc(centred, 1)
        for g in range(GROUPS):
            dve.wait_ge(rstd_done, g + 1)
            nc.vector.tensor_tensor(xc[:, tok(g)], xc[:, tok(g)], rstd[:, tok(g)], ALU.mult).then_inc(scaled, 1)
            dve.wait_ge(scaled, g + 1)
            nc.vector.tensor_tensor(xc[:, tok(g)], xc[:, tok(g)], x1[:, tok(g)], ALU.add).then_inc(added, 1)


def rotary_constants():
    half = np.arange(0, DH, 2, dtype=np.float64)
    freqs = np.arange(SEQ)[:, None] / 10000.0 ** (half / DH)[None, :]
    base = (half + 0.4 * DH) / (1.4 * DH)
    scale = base[None, :] ** ((np.arange(SEQ) - SEQ // 2) / (WIN // 2))[:, None]
    cos, sin = np.cos(freqs), np.sin(freqs)
    cos2, sin2, sc2 = (np.concatenate(p, 1) for p in ((cos, cos), (-sin, sin), (scale, scale)))
    t = np.stack([cos2 * sc2 * 8.0, sin2 * sc2 * 8.0, cos2 / sc2, sin2 / sc2], 1)
    return np.ascontiguousarray(t.reshape(TILES, P, 4, DH).transpose(1, 0, 2, 3).reshape(P, -1)).astype(np.float32)


def mask_constants():
    m = np.zeros((P, TILES, 2 * WIN), np.float32)
    r, c = np.arange(WIN)[:, None], np.arange(WIN)[None, :]
    for t in range(TILES):
        for j in range(4):
            rows = slice(WIN * j, WIN * (j + 1))
            before, own = np.where(r > c, -1e30, 0.0), np.where(c > r, -1e30, 0.0)
            if t == 0 and j == 0:
                before = np.full((WIN, WIN), -1e30)
            m[rows, t] = np.concatenate((before, own) if j % 2 else (own, before), 1)
    return np.ascontiguousarray(m.reshape(P, -1))


def matrix_constants():
    u = np.triu(np.ones((P, P), np.float32))
    return np.concatenate([np.eye(P, dtype=np.float32), u, np.ones((P, P), np.float32), u], 1)


def kernel(**inputs):
    import concourse.bacc as bacc
    from concourse.bass_utils import run_bass_kernel_spmd

    a = {k.replace("L0_attn_", "a_").replace("L0_ffn_", "f_"): np.asarray(v) for k, v in inputs.items()}
    wqkv = a["f_Wqkv"]
    wv = wqkv[:, :, 2 * INNER:].reshape(DEPTH, DIM, PAIRS, 2, DH).transpose(0, 1, 3, 2, 4).reshape(DEPTH, DIM, INNER)
    wo = a["f_Wo"].reshape(DEPTH, PAIRS, P, DIM).transpose(0, 2, 1, 3).reshape(DEPTH, P, PAIRS * DIM)
    w2 = np.zeros((DEPTH, HC * P, DIM), np.float32)
    w2[:, :DIM_INNER] = a["f_W2"]
    w2 = w2.reshape(DEPTH, HC, P, DIM).transpose(0, 2, 1, 3).reshape(DEPTH, P, HC * DIM)
    b1 = np.zeros((DEPTH, 2, HC * P), np.float32)
    b1[:, :, :DIM_INNER] = a["f_b1"].reshape(DEPTH, 2, DIM_INNER)
    cols = np.zeros((P, DEPTH, N_COLS), np.float32)
    cols[:, :, C_G] = a["f_ln_g"].T
    cols[:, :, C_B] = a["f_ln_b"].T
    cols[:, :, C_B2] = a["f_b2"].T
    cols[:, :, C_B1A:C_B1A + 2 * HC] = b1.reshape(DEPTH, 2 * HC, P).transpose(2, 0, 1)
    conv = np.concatenate([a["a_conv_w"].reshape(CONV_DIM, D_CONV), a["a_conv_b"].reshape(CONV_DIM, 1)], 1)
    conv = conv.reshape(3, P, D_CONV + 1).transpose(1, 0, 2)
    arrays = {
        "x": a["a_x"], "w_in_t": a["a_W_in"].T, "conv_cols": conv, "a_log": a["a_A_log"],
        "dt_bias": a["a_dt_bias"], "d_skip": a["a_D_skip"], "w_out_t": a["a_W_out"].T,
        "w_qk": wqkv[:, :, :2 * INNER], "w_v": wv, "w_o": wo, "w_1": a["f_W1"], "w_2": w2,
        "q_scale": a["f_q_scale"], "k_scale": a["f_k_scale"], "cols_in": cols,
        "rope": rotary_constants(), "consts": matrix_constants(), "mask_in": mask_constants(),
    }
    arrays = {k: np.ascontiguousarray(v) for k, v in arrays.items()}
    nc = bacc.Bacc("TRN2", target_bir_lowering=False, num_devices=1)
    aps = {k: nc.dram_tensor(f"in_{k}", v.shape, mybir.dt.from_np(v.dtype), kind="ExternalInput").ap()
           for k, v in arrays.items()}
    out = nc.dram_tensor("out_y", (BATCH, SEQ, DIM), F32, kind="ExternalOutput").ap()
    build(nc, out=out, **aps)
    got = run_bass_kernel_spmd(nc, [{f"in_{k}": v for k, v in arrays.items()}], core_ids=[0])
    return got.results[0]["out_y"]
```

```python
from contextlib import ExitStack

import numpy as np

import concourse.bass as bass
from concourse import mybir

F32 = mybir.dt.float32
F32R = mybir.dt.float32r
BF16 = mybir.dt.bfloat16
ALU = mybir.AluOpType
ACT = mybir.ActivationFunctionType
AX = mybir.AxisListType

P = 128
BATCH, SEQ, DIM = 8, 256, 128
TOK = BATCH * SEQ
TILES = SEQ // P
D_INNER, D_STATE, D_CONV, NHEADS = 256, 64, 4, 2
CONV_DIM = D_INNER + 2 * D_STATE
PROJ = D_INNER + CONV_DIM + NHEADS
GROUPS = 4
GT = TOK // GROUPS
DEPTH, HEADS, DH, WIN = 6, 16, 64, 32
PAIRS = HEADS // 2
INNER = HEADS * DH
DIM_INNER = int(DIM * 4 * 2 / 3)
HC = 3
HLAST = DIM_INNER - 2 * P
UNITS = DEPTH * BATCH
VW = DH + 1
LN_EPS = 1e-5
LN_EXP_SET = 6
N_PROJ, N_SC, N_TR, N_PV, N_F = 12, 4, 16, 6, 7
QK_COLS = 2 * INNER
SPLIT = QK_COLS // BATCH
PV_CHUNKS = [(0, 3), (3, 6), (6, 8)]
C_G, C_B, C_B2, C_B1A, C_B1G = 0, 1, 2, 3, 6
N_COLS = 9


def started(value):
    return not isinstance(value, int) or value > 0


def build(nc, x, w_in_t, conv_cols, a_log, dt_bias, d_skip, w_out_t, w_qk, w_v, w_o, w_1, w_2,
          q_scale, k_scale, cols_in, rope, consts, mask_in, out):
    whole = ExitStack()
    with whole:
        def sb(stack, name, shape, dt=F32):
            return stack.enter_context(nc.sbuf_tensor(name, shape, dt))

        def sem(stack, name):
            return stack.enter_context(nc.semaphore(name))

        ident = sb(whole, "ident", [P, P])
        ones_mean = sb(whole, "ones_mean", [P, P])
        eps_col = sb(whole, "eps_col", [P, 1])
        x1 = sb(whole, "x1", [P, TOK])
        xs = sb(whole, "xs", [P, BATCH, SEQ + 1])
        bank = [whole.enter_context(nc.psum_tensor(f"bank{i}", [P, 512], F32)) for i in range(8)]

        with ExitStack() as mixer:
            build_mixer(nc, mixer, sb, sem, bank, ident, ones_mean, eps_col, x1, xs, x, w_in_t, conv_cols,
                        a_log, dt_bias, d_skip, w_out_t, consts)
        with ExitStack() as layers:
            build_layers(nc, layers, sb, sem, bank, ident, ones_mean, eps_col, xs, w_qk, w_v, w_o, w_1,
                         w_2, q_scale, k_scale, cols_in, rope, mask_in)
        with ExitStack() as last:
            build_last(nc, last, sb, sem, bank, ident, ones_mean, eps_col, x1, xs, out)


def load_ln_exp(nc, act):
    act.add_instruction(mybir.InstLoadActFuncSet(name=nc.get_next_instruction_name(), act_func_set_id=LN_EXP_SET,
                                                 ins=[], outs=[]))


def build_mixer(nc, ctx, sb, sem, bank, ident, ones_mean, eps_col, x1, xs, x, w_in_t, conv_cols, a_log,
                dt_bias, d_skip, w_out_t, consts):
    NT = TOK // P
    HB = BATCH * TILES * NHEADS
    xin = sb(ctx, "xin", [P, NT, P])
    win = sb(ctx, "win", [P, PROJ])
    wout = sb(ctx, "wout", [P, NHEADS, DIM])
    tri = sb(ctx, "tri", [P, 3 * P])
    convw = sb(ctx, "convw", [P, 3, D_CONV + 1])
    heads = sb(ctx, "heads", [P, 4, NHEADS])
    xc = sb(ctx, "xc", [P, TOK])
    sq = sb(ctx, "sq", [P, TOK])
    rstd = sb(ctx, "rstd", [P, TOK])
    xn = sb(ctx, "xn", [P, TOK])
    zs = sb(ctx, "zs", [P, 2, TOK])
    raw = sb(ctx, "raw", [P, 3, BATCH, SEQ + 3])
    cv = sb(ctx, "cv", [P, 3, BATCH, SEQ])
    c_low = sb(ctx, "c_low", [D_STATE, BATCH, SEQ])
    sp = sb(ctx, "sp", [P, 12, HB])
    dec = sb(ctx, "dec", [P, 2, NHEADS, 3 * P])
    gm = sb(ctx, "gm", [P, 2, 3 * P])
    st = sb(ctx, "st", [P, 2, NHEADS, 3 * P])
    xnat = sb(ctx, "xnat", [P, 2, 4, P])
    yy = sb(ctx, "yy", [P, 2, NHEADS, SEQ])
    BIAS, R, NEG, E, U, L, V, M, DT, DA, CS, TMP = range(12)

    x_in = [sem(ctx, f"m_x_in{g}") for g in range(GROUPS)]
    w_dma = sem(ctx, "m_w_dma")
    setup = sem(ctx, "m_setup")
    xt_mm = sem(ctx, "m_xt_mm")
    xt_evac = sem(ctx, "m_xt_evac")
    mean_mm = sem(ctx, "m_mean_mm")
    centred = sem(ctx, "m_centred")
    squared = sem(ctx, "m_squared")
    var_mm = sem(ctx, "m_var_mm")
    log_done = sem(ctx, "m_log_done")
    rstd_done = sem(ctx, "m_rstd_done")
    norm_done = sem(ctx, "m_norm_done")
    proj_mm = sem(ctx, "m_proj_mm")
    proj_evac = sem(ctx, "m_proj_evac")
    dt_mm = sem(ctx, "m_dt_mm")
    tap = sem(ctx, "m_tap")
    conv_done = sem(ctx, "m_conv_done")
    silu_done = sem(ctx, "m_silu_done")
    c_moved = sem(ctx, "m_c_moved")
    sp_step = sem(ctx, "m_sp_step")
    sp_act = sem(ctx, "m_sp_act")
    cs_mm = sem(ctx, "m_cs_mm")
    row_mm = sem(ctx, "m_row_mm")
    diff_done = sem(ctx, "m_diff_done")
    dec_done = sem(ctx, "m_dec_done")
    g_mm = sem(ctx, "m_g_mm")
    g_done = sem(ctx, "m_g_done")
    s_done = sem(ctx, "m_s_done")
    xnat_mm = sem(ctx, "m_xnat_mm")
    xnat_evac = sem(ctx, "m_xnat_evac")
    y_mm = sem(ctx, "m_y_mm")
    y_skip = sem(ctx, "m_y_skip")
    y_done = sem(ctx, "m_y_done")
    o_mm = sem(ctx, "m_o_mm")
    o_evac = sem(ctx, "m_o_evac")
    x1_done = sem(ctx, "m_x1_done")
    xs_done = sem(ctx, "m_xs_done")

    DT_STEPS, CS_STEPS = 13, 14

    def tok(g):
        return slice(g * GT, (g + 1) * GT)

    def yo(t):
        return t[:, :, :].rearrange("p n d -> p (n d)")

    block = ctx.enter_context(nc.Block())

    @block.sync
    def _(sync):
        xv = x.rearrange("b (t p) d -> p (b t) d", p=P)
        sync.dma_start(ident[:, :], consts[:, 0:P]).then_inc(w_dma, 16)
        for g in range(GROUPS):
            sync.dma_start(xin[:, 4 * g:4 * g + 4, :], xv[:, 4 * g:4 * g + 4, :]).then_inc(x_in[g], 16)
        sync.dma_start(win[:, :], w_in_t).then_inc(w_dma, 16)
        sync.dma_start(convw[:, :, :], conv_cols).then_inc(w_dma, 16)
        sync.dma_start(tri[:, :], consts[:, P:4 * P]).then_inc(w_dma, 16)
        sync.dma_start(wout[:, :, :], w_out_t.rearrange("(h p) d -> p h d", p=P)).then_inc(w_dma, 16)
        for n, row in enumerate((a_log, dt_bias, d_skip)):
            sync.dma_start(heads[:, n, :], row.partition_broadcast(P)).then_inc(w_dma, 16)
        for g in range(GROUPS):
            sync.wait_ge(silu_done, 2 * GROUPS + g + 1)
            sync.dma_start(c_low[:, 2 * g:2 * g + 2, :], cv[D_STATE:P, 2, 2 * g:2 * g + 2, :]).then_inc(c_moved, 16)

    W_ALL = 8 * 16

    @block.gpsimd
    def _(pool):
        nc.gpsimd.memset(ones_mean[:, :], 1.0 / DIM).then_inc(setup, 1)
        nc.gpsimd.memset(eps_col[:, :], LN_EPS).then_inc(setup, 1)
        nc.gpsimd.memset(raw[:, :, :, 0:3], 0.0).then_inc(setup, 1)
        nc.gpsimd.memset(xs[:, :, 0:1], 0.0).then_inc(setup, 1)

    @block.tensor
    def _(pe):
        pe.wait_ge(setup, 4)
        pe.wait_ge(w_dma, W_ALL)

        def mean_of(n, src, g, ready, count):
            pe.wait_ge(ready, count)
            if n >= 2:
                pe.wait_ge(log_done, n - 1)
            nc.tensor.matmul(bank[n % 2][:, :], ones_mean[:, :], src[:, tok(g)], start=True, stop=True).then_inc(mean_mm, 1)

        def var_of(n, g):
            pe.wait_ge(squared, n + 1)
            nc.tensor.matmul(bank[n % 2][:, :], ones_mean[:, :], sq[:, tok(g)], start=True, stop=True).then_inc(var_mm, 1)

        for g in range(GROUPS):
            pe.wait_ge(x_in[g], 16)
            if g >= 2:
                pe.wait_ge(xt_evac, g - 1)
            for t in range(4):
                mm = nc.tensor.transpose(bank[2 + g % 2][:, t * P:(t + 1) * P], xin[:, 4 * g + t, :], ident[:, :])
            mm.then_inc(xt_mm, 1)
        for g in range(GROUPS):
            mean_of(g, x1, g, xt_evac, g + 1)
            if g:
                var_of(g - 1, g - 1)
        var_of(GROUPS - 1, GROUPS - 1)
        n = 0
        for c in range(5):
            for g in range(GROUPS):
                pe.wait_ge(norm_done, g + 1)
                if n >= 4:
                    pe.wait_ge(proj_evac, n - 3)
                else:
                    pe.wait_ge(xt_evac, GROUPS)
                nc.tensor.matmul(bank[2 + n % 4][:, :], win[:, c * P:(c + 1) * P], xn[:, tok(g)],
                                 start=True, stop=True).then_inc(proj_mm, 1)
                n += 1
        for t in range(NT):
            mm = nc.tensor.matmul(bank[6][:, NHEADS * t:NHEADS * (t + 1)], xn[:, t * P:(t + 1) * P],
                                  win[:, PROJ - NHEADS:PROJ], start=True, stop=True)
        mm.then_inc(dt_mm, 1)
        pe.wait_ge(sp_step, DT_STEPS)
        nc.tensor.matmul(bank[7][:, 0:HB], tri[:, 0:P], sp[:, DA, :], start=True, stop=True).then_inc(cs_mm, 1)

        def rows(b):
            for h in range(NHEADS):
                c0, c1 = (2 * b) * NHEADS + h, (2 * b + 1) * NHEADS + h
                dst = bank[h]
                if b:
                    pe.wait_ge(diff_done, 2 * (b - 1) + h + 1)
                else:
                    pe.wait_ge(log_done, GROUPS)
                first = sp[:, DA, c0:c0 + 1].to_broadcast([P, P])
                second = sp[:, DA, c1:c1 + 1].to_broadcast([P, P])
                nc.tensor.matmul(dst[:, 0:2 * P], first, tri[:, 0:2 * P], start=True, stop=True, skip_group_check=True)
                nc.tensor.matmul(dst[:, P:2 * P], second, tri[:, 0:P], start=False, stop=True, skip_group_check=True)
                nc.tensor.matmul(dst[:, 2 * P:3 * P], second, tri[:, 0:P], start=False, stop=True,
                                 skip_group_check=True).then_inc(row_mm, 1)

        def scores(b):
            if b:
                pe.wait_ge(g_done, b)
            else:
                pe.wait_ge(c_moved, 16 * GROUPS)
                pe.wait_ge(proj_evac, 5 * GROUPS)
            nc.tensor.matmul(bank[2][:, 0:2 * P], cv[0:D_STATE, 2, b, 0:P], c_low[:, b, :], start=True, stop=True)
            nc.tensor.matmul(bank[2][:, 2 * P:3 * P], cv[0:D_STATE, 2, b, P:2 * P], c_low[:, b, P:2 * P],
                             start=True, stop=True).then_inc(g_mm, 1)

        def to_nat(b):
            if b:
                pe.wait_ge(xnat_evac, b)
            for h in range(NHEADS):
                for t in range(TILES):
                    mm = nc.tensor.transpose(bank[3][:, (2 * h + t) * P:(2 * h + t + 1) * P],
                                             cv[:, h, b, t * P:(t + 1) * P], ident[:, :])
            mm.then_inc(xnat_mm, 1)

        def ys(b):
            pe.wait_ge(xnat_evac, b + 1)
            if b >= 2:
                pe.wait_ge(y_skip, 2 * (b - 2) + 2)
            for h in range(NHEADS):
                pe.wait_ge(s_done, 2 * b + h + 1)
                dst = bank[4 + b % 2][:, h * SEQ:(h + 1) * SEQ]
                nc.tensor.matmul(dst, xnat[:, b % 2, 2 * h, :], st[:, b % 2, h, 0:SEQ], start=True, stop=True,
                                 skip_group_check=True)
                mm = nc.tensor.matmul(dst[:, P:SEQ], xnat[:, b % 2, 2 * h + 1, :], st[:, b % 2, h, SEQ:SEQ + P],
                                      start=False, stop=True, skip_group_check=True)
            mm.then_inc(y_mm, 1)

        def outs(b):
            pe.wait_ge(y_done, b + 1)
            g = b // 2
            if g >= 2 and b % 2 == 0:
                pe.wait_ge(o_evac, g - 1)
            elif b == 0:
                pe.wait_ge(cs_mm, 1)
                pe.wait_ge(sp_step, CS_STEPS)
            for h in range(NHEADS):
                mm = nc.tensor.matmul(bank[6 + g % 2][:, (b % 2) * SEQ:(b % 2 + 1) * SEQ], wout[:, h, :],
                                      yy[:, b % 2, h, :], start=(h == 0), stop=(h == NHEADS - 1), skip_group_check=True)
            mm.then_inc(o_mm, 1)

        for b in range(BATCH + 2):
            if b < BATCH:
                rows(b)
                scores(b)
                to_nat(b)
            if 1 <= b <= BATCH:
                ys(b - 1)
            if b >= 2:
                outs(b - 2)
        for k, (src, ready, base) in enumerate(((yo(xin), o_evac, 0), (x1, x1_done, 0))):
            for g in range(GROUPS):
                n = GROUPS * (k + 1) + g
                if g < 2 and k == 0:
                    pe.wait_ge(diff_done, 2 * BATCH)
                mean_of(n, src, g, ready, g + 1)
                if g:
                    var_of(n - 1, g - 1)
            var_of(n, g)

    @block.scalar
    def _(act):
        for g in range(GROUPS):
            act.wait_ge(xt_mm, g + 1)
            nc.scalar.copy(x1[:, tok(g)], bank[2 + g % 2][:, :]).then_inc(xt_evac, 1)

        def norm_steps(k):
            def square(g):
                act.wait_ge(centred, GROUPS * k + g + 1)
                if k:
                    act.wait_ge(var_mm, GROUPS * (k - 1) + g + 1)
                nc.scalar.activation(sq[:, tok(g)], xc[:, tok(g)], ACT.Square).then_inc(squared, 1)

            def root(g):
                n = GROUPS * k + g
                act.wait_ge(var_mm, n + 1)
                if k:
                    act.wait_ge(norm_done, n - GROUPS + 1)
                nc.scalar.activation(rstd[:, tok(g)], bank[n % 2][:, :], ACT.Ln, bias=eps_col[:, 0:1]).then_inc(log_done, 1)
                act.wait_ge(log_done, n + 1)
                nc.scalar.activation(rstd[:, tok(g)], rstd[:, tok(g)], ACT.Exp, scale=-0.5).then_inc(rstd_done, 1)

            for g in range(GROUPS):
                square(g)
                if g:
                    root(g - 1)
            root(GROUPS - 1)

        norm_steps(0)
        n = 0
        for c in range(5):
            for g in range(GROUPS):
                act.wait_ge(proj_mm, n + 1)
                src = bank[2 + n % 4]
                if c < 2:
                    nc.scalar.activation(zs[:, c, tok(g)], src[:, :], ACT.Silu).then_inc(proj_evac, 1)
                else:
                    nc.scalar.copy(raw[:, c - 2, 2 * g:2 * g + 2, 3:], src[:, :].rearrange("p (b s) -> p b s", b=2))\
                        .then_inc(proj_evac, 1)
                n += 1
        for c in range(3):
            for g in range(GROUPS):
                act.wait_ge(conv_done, GROUPS * c + g + 1)
                dst = cv[:, c, 2 * g:2 * g + 2, :]
                nc.scalar.activation(dst, dst, ACT.Silu).then_inc(silu_done, 1)
        act.wait_ge(w_dma, W_ALL)
        act.wait_ge(sp_step, 3)
        nc.scalar.activation(sp[:, E, :], sp[:, NEG, :], ACT.Exp).then_inc(sp_act, 1)
        nc.scalar.activation(heads[:, 3, :], heads[:, 0, :], ACT.Exp).then_inc(sp_act, 1)
        act.wait_ge(sp_step, 4)
        nc.scalar.activation(sp[:, L, :], sp[:, U, :], ACT.Ln).then_inc(sp_act, 1)

        for b in range(BATCH):
            act.wait_ge(xnat_mm, b + 1)
            if b >= 2:
                act.wait_ge(y_mm, b - 1)
            nc.scalar.copy(xnat[:, b % 2, :, :], bank[3][:, :].rearrange("p (k d) -> p k d", k=4)).then_inc(xnat_evac, 1)
            for h in range(NHEADS):
                act.wait_ge(diff_done, 2 * b + h + 1)
                nc.scalar.activation(dec[:, b % 2, h, :], dec[:, b % 2, h, :], ACT.Exp).then_inc(dec_done, 1)
            if b >= 3 and b % 2 == 1:
                g = (b - 3) // 2
                act.wait_ge(o_mm, 2 * g + 2)
                nc.scalar.copy(yo(xin)[:, tok(g)], bank[6 + g % 2][:, :]).then_inc(o_evac, 1)
        act.wait_ge(o_mm, BATCH)
        nc.scalar.copy(yo(xin)[:, tok(3)], bank[7][:, :]).then_inc(o_evac, 1)
        norm_steps(1)
        norm_steps(2)

    @block.vector
    def _(dve):
        def centre(k, src):
            def one(g):
                n = GROUPS * k + g
                dve.wait_ge(mean_mm, n + 1)
                if k:
                    dve.wait_ge(norm_done, n - GROUPS + 1)
                    dve.wait_ge(squared, n - GROUPS + 1)
                nc.vector.tensor_tensor(xc[:, tok(g)], src[:, tok(g)], bank[n % 2][:, :], ALU.subtract).then_inc(centred, 1)
            return one

        def scale(k, write):
            def one(g):
                dve.wait_ge(rstd_done, GROUPS * k + g + 1)
                write(g)
            return one

        def norm(k, src, write):
            c, s = centre(k, src), scale(k, write)
            c(0)
            c(1)
            for g in range(GROUPS):
                s(g)
                if g + 2 < GROUPS:
                    c(g + 2)

        def write_xn(g):
            nc.vector.tensor_tensor(xn[:, tok(g)], xc[:, tok(g)], rstd[:, tok(g)], ALU.mult).then_inc(norm_done, 1)

        norm(0, x1, write_xn)
        dve.wait_ge(w_dma, W_ALL)
        dve.wait_ge(setup, 4)
        taps = 0
        for c in range(3):
            for g in range(GROUPS):
                dve.wait_ge(proj_evac, GROUPS * (c + 2) + g + 1)
                b0 = 2 * g
                dst = cv[:, c, b0:b0 + 2, :]
                nc.vector.tensor_scalar(dst, raw[:, c, b0:b0 + 2, 0:SEQ], convw[:, c, 0:1], convw[:, c, D_CONV:D_CONV + 1],
                                        ALU.mult, ALU.add).then_inc(tap, 1)
                for k in range(1, D_CONV):
                    taps += 1
                    dve.wait_ge(tap, taps)
                    ins = nc.vector.scalar_tensor_tensor(out=dst, in0=raw[:, c, b0:b0 + 2, k:k + SEQ],
                                                         scalar=convw[:, c, k:k + 1], in1=dst, op0=ALU.mult, op1=ALU.add)
                    ins.then_inc(tap if k < D_CONV - 1 else conv_done, 1)
        steps = [0]

        def step(ins):
            steps[0] += 1
            ins.then_inc(sp_step, 1)
            dve.wait_ge(sp_step, steps[0])

        def bc(row):
            return heads[:, row, :].unsqueeze(1).broadcast_to([P, HB // NHEADS, NHEADS])

        def v3(row):
            return sp[:, row, :].rearrange("p (n h) -> p n h", h=NHEADS)

        dve.wait_ge(dt_mm, 1)
        step(nc.vector.tensor_tensor(v3(R), bank[6][:, 0:HB].rearrange("p (n h) -> p n h", h=NHEADS), bc(1), ALU.add))
        step(nc.vector.tensor_scalar(sp[:, TMP, :], sp[:, R, :], -1.0, None, ALU.mult))
        step(nc.vector.tensor_tensor(sp[:, NEG, :], sp[:, R, :], sp[:, TMP, :], ALU.min))
        dve.wait_ge(sp_act, 1)
        step(nc.vector.tensor_scalar(sp[:, U, :], sp[:, E, :], 1.0, None, ALU.add))
        step(nc.vector.tensor_scalar(sp[:, V, :], sp[:, U, :], -1.0, None, ALU.add))
        step(nc.vector.tensor_scalar(sp[:, M, :], sp[:, V, :], 0.0, None, ALU.is_equal))
        step(nc.vector.tensor_tensor(sp[:, V, :], sp[:, V, :], sp[:, M, :], ALU.add))
        step(nc.vector.reciprocal(sp[:, TMP, :], sp[:, V, :]))
        dve.wait_ge(sp_act, 3)
        step(nc.vector.tensor_tensor(sp[:, L, :], sp[:, L, :], sp[:, M, :], ALU.add))
        step(nc.vector.tensor_tensor(sp[:, L, :], sp[:, L, :], sp[:, TMP, :], ALU.mult))
        step(nc.vector.tensor_tensor(sp[:, L, :], sp[:, L, :], sp[:, E, :], ALU.mult))
        step(nc.vector.scalar_tensor_tensor(out=sp[:, DT, :], in0=sp[:, R, :], scalar=0.0, in1=sp[:, L, :],
                                            op0=ALU.max, op1=ALU.add))
        step(nc.vector.scalar_tensor_tensor(out=v3(DA), in0=v3(DT), scalar=-1.0, in1=bc(3), op0=ALU.mult, op1=ALU.mult))
        assert steps[0] == DT_STEPS
        dve.wait_ge(cs_mm, 1)
        step(nc.vector.tensor_copy(sp[:, CS, :], bank[7][:, 0:HB]))
        assert steps[0] == CS_STEPS

        def decay(b):
            for h in range(NHEADS):
                dve.wait_ge(row_mm, 2 * b + h + 1)
                if b >= 2:
                    dve.wait_ge(s_done, 2 * (b - 2) + h + 1)
                c0, c1 = (2 * b) * NHEADS + h, (2 * b + 1) * NHEADS + h
                nc.vector.tensor_scalar(dec[:, b % 2, h, 0:SEQ], bank[h][:, 0:SEQ], sp[:, CS, c0:c0 + 1], 0.0,
                                        ALU.subtract, ALU.min)
                nc.vector.tensor_scalar(dec[:, b % 2, h, SEQ:], bank[h][:, SEQ:3 * P], sp[:, CS, c1:c1 + 1], 0.0,
                                        ALU.subtract, ALU.min).then_inc(diff_done, 1)

        def masked(b):
            dve.wait_ge(g_mm, b + 1)
            if b >= 2:
                dve.wait_ge(s_done, 2 * (b - 2) + 2)
            nc.vector.tensor_tensor(gm[:, b % 2, :], bank[2][:, 0:3 * P], tri[:, :], ALU.mult).then_inc(g_done, 1)

        def weights(b):
            dve.wait_ge(g_done, b + 1)
            for h in range(NHEADS):
                dve.wait_ge(dec_done, 2 * b + h + 1)
                if b >= 2:
                    dve.wait_ge(y_mm, b - 1)
                c0, c1 = (2 * b) * NHEADS + h, (2 * b + 1) * NHEADS + h
                for lo, hi, c in ((0, SEQ, c0), (SEQ, 3 * P, c1)):
                    ins = nc.vector.scalar_tensor_tensor(out=st[:, b % 2, h, lo:hi], in0=dec[:, b % 2, h, lo:hi],
                                                         scalar=sp[:, DT, c:c + 1], in1=gm[:, b % 2, lo:hi],
                                                         op0=ALU.mult, op1=ALU.mult)
                ins.then_inc(s_done, 1)

        def gate(b):
            dve.wait_ge(y_mm, b + 1)
            if b >= 2:
                dve.wait_ge(o_mm, b - 1)
            for h in range(NHEADS):
                nc.vector.scalar_tensor_tensor(out=yy[:, b % 2, h, :], in0=cv[:, h, b, :], scalar=heads[:, 2, h:h + 1],
                                               in1=bank[4 + b % 2][:, h * SEQ:(h + 1) * SEQ], op0=ALU.mult,
                                               op1=ALU.add).then_inc(y_skip, 1)
            dve.wait_ge(y_skip, 2 * b + 2)
            nc.vector.tensor_tensor(yy[:, b % 2, :, :], yy[:, b % 2, :, :], zs[:, :, b * SEQ:(b + 1) * SEQ],
                                    ALU.mult).then_inc(y_done, 1)

        dve.wait_ge(silu_done, 3 * GROUPS)
        for b in range(BATCH + 1):
            if b < BATCH:
                decay(b)
                masked(b)
            if b:
                gate(b - 1)
            if b < BATCH:
                weights(b)

        added = [0]

        def write_x1(g):
            nc.vector.tensor_tensor(xn[:, tok(g)], xc[:, tok(g)], rstd[:, tok(g)], ALU.mult).then_inc(norm_done, 1)
            dve.wait_ge(norm_done, GROUPS + g + 1)
            nc.vector.tensor_tensor(x1[:, tok(g)], x1[:, tok(g)], xn[:, tok(g)], ALU.add).then_inc(x1_done, 1)

        def write_xs(g):
            for half in range(2):
                rows = slice(DH * half, DH * half + DH)
                nc.vector.tensor_tensor(xs[rows, 2 * g:2 * g + 2, half:half + SEQ],
                                        xc[rows, tok(g)].rearrange("p (b s) -> p b s", b=2),
                                        rstd[rows, tok(g)].rearrange("p (b s) -> p b s", b=2), ALU.mult)\
                    .then_inc(xs_done, 1)

        norm(1, yo(xin), write_x1)
        norm(2, x1, write_xs)


def build_layers(nc, ctx, sb, sem, bank, ident, ones_mean, eps_col, xs, w_qk, w_v, w_o, w_1, w_2,
                 q_scale, k_scale, cols_in, rope, mask_in):
    wh = sb(ctx, "wh", [P, 2, QK_COLS], F32R)
    wl = sb(ctx, "wl", [P, 2, QK_COLS], F32R)
    wv = sb(ctx, "wv", [P, INNER])
    wraw = sb(ctx, "wraw", [P, SPLIT])
    wo = sb(ctx, "wo", [P, PAIRS, DIM])
    w1 = sb(ctx, "w1", [P, 2 * DIM_INNER])
    w2 = sb(ctx, "w2", [P, HC, DIM])
    cols = sb(ctx, "cols", [P, DEPTH, N_COLS])
    tab = sb(ctx, "tab", [P, DEPTH, TILES, 4, DH])
    centre = sb(ctx, "centre", [P, P])
    identb = sb(ctx, "identb", [P, P], BF16)
    maskb = sb(ctx, "maskb", [P, TILES, 2 * WIN], BF16)
    xh = sb(ctx, "xh", [P, SEQ], F32R)
    xl = sb(ctx, "xl", [P, SEQ], F32R)
    xf = sb(ctx, "xf", [P, SEQ])
    qk = [sb(ctx, f"qk{t}", [P, QK_COLS]) for t in range(TILES)]
    rot = sb(ctx, "rot", [P, QK_COLS])
    sqr = sb(ctx, "sqr", [P, 2, 512])
    ss = [sb(ctx, f"ss{t}", [P, 2 * HEADS]) for t in range(TILES)]
    rn = [sb(ctx, f"rn{t}", [P, 2 * HEADS]) for t in range(TILES)]
    qT = [sb(ctx, f"qT{t}", [P, PAIRS, P]) for t in range(TILES)]
    kbd = sb(ctx, "kbd", [P, PAIRS, 2, WIN + SEQ])
    v_odd = sb(ctx, "v_odd", [P, SEQ // (2 * WIN), 2, PAIRS, VW])
    v_even = sb(ctx, "v_even", [P, SEQ // (2 * WIN), 2, PAIRS, VW])
    pr = [sb(ctx, f"pr{t}", [P, PAIRS, 2, 2 * WIN]) for t in range(TILES)]
    mx = sb(ctx, "mx", [P, 2, PAIRS])
    pT = sb(ctx, "pT", [P, PAIRS, P])
    rs = sb(ctx, "rs", [P, 2, 6])
    o = sb(ctx, "o", [P, PAIRS, 2, DH])
    oT = sb(ctx, "oT", [P, PAIRS, SEQ])
    fx = sb(ctx, "fx", [P, SEQ])
    fq = sb(ctx, "fq", [P, SEQ])
    fr = sb(ctx, "fr", [P, SEQ])
    gp = sb(ctx, "gp", [P, HC, SEQ])
    ap = sb(ctx, "ap", [P, HC, SEQ])

    proj_bank, sc_bank, tr_bank, pv_bank, f_bank = bank[0:2], bank[2:4], bank[4:6], bank[6], bank[7]

    first_dma = sem(ctx, "first_dma")
    scale_dma = sem(ctx, "scale_dma")
    zeroed = sem(ctx, "zeroed")
    consts_done = sem(ctx, "consts_done")
    raw_dma = sem(ctx, "raw_dma")
    wv_dma = sem(ctx, "wv_dma")
    split_hi = sem(ctx, "split_hi")
    split_done = sem(ctx, "split_done")
    wo_dma = sem(ctx, "wo_dma")
    w1_dma = sem(ctx, "w1_dma")
    w2_dma = sem(ctx, "w2_dma")
    x_hi = sem(ctx, "x_hi")
    x_staged = sem(ctx, "x_staged")
    proj_mm = sem(ctx, "proj_mm")
    squared = sem(ctx, "squared")
    roped = sem(ctx, "roped")
    sums_done = sem(ctx, "sums_done")
    floored = sem(ctx, "floored")
    rn_log = sem(ctx, "rn_log")
    rn_done = sem(ctx, "rn_done")
    rope_added = sem(ctx, "rope_added")
    qk_done = sem(ctx, "qk_done")
    tr_mm = sem(ctx, "tr_mm")
    tr_evac = sem(ctx, "tr_evac")
    sc_mm = sem(ctx, "sc_mm")
    max_done = sem(ctx, "max_done")
    sc_evac = sem(ctx, "sc_evac")
    exp_done = sem(ctx, "exp_done")
    v_evac = sem(ctx, "v_evac")
    ve_dma = sem(ctx, "ve_dma")
    pv_mm = sem(ctx, "pv_mm")
    recip_done = sem(ctx, "recip_done")
    pv_evac = sem(ctx, "pv_evac")
    f_mm = sem(ctx, "f_mm")
    res1 = sem(ctx, "res1")
    f_squared = sem(ctx, "f_squared")
    f_log = sem(ctx, "f_log")
    f_rstd = sem(ctx, "f_rstd")
    f_scaled = sem(ctx, "f_scaled")
    f_norm = sem(ctx, "f_norm")
    h_evac = sem(ctx, "h_evac")
    gelu_done = sem(ctx, "gelu_done")
    h_done = sem(ctx, "h_done")
    state_ready = sem(ctx, "state_ready")

    TR = {step: n for n, step in enumerate((
        ("qk", 0, 0), ("qk", 0, 1), ("qk", 0, 2), ("qk", 0, 3),
        ("qk", 1, 0), ("qk", 1, 1), ("qk", 1, 2), ("qk", 1, 3),
        ("p", 0, 0), ("p", 0, 1), ("p", 1, 0), ("p", 1, 1),
        ("o", 0, 0), ("o", 0, 1), ("o", 1, 0), ("o", 1, 1),
    ))}

    def over_units(eng, body):
        for it in (-1, 0, 1):
            body(it)
        with eng.Fori(0, (UNITS - 4) // 2) as k:
            body(2 * k + 2)
            body(2 * k + 3)
        for it in (UNITS - 2, UNITS - 1, UNITS):
            body(it)

    def has(it, lag):
        return not isinstance(it, int) or 0 <= it + lag < UNITS

    block = ctx.enter_context(nc.Block())

    @block.sync
    def _(sync):
        for n, (dst, src) in enumerate(((wo[:, :, :], w_o[0].rearrange("p (n d) -> p n d", n=PAIRS)),
                                        (w1[:, :], w_1[0]),
                                        (w2[:, :, :], w_2[0].rearrange("p (n d) -> p n d", n=HC)))):
            sync.dma_start(dst, src).then_inc((wo_dma, w1_dma, w2_dma)[n], 16)
        sync.dma_start(wv[:, :], w_v[0]).then_inc(wv_dma, 16)
        sync.dma_start(qk[0][:, :], w_qk[0]).then_inc(first_dma, 16)
        sync.dma_start(cols[:, :, :], cols_in).then_inc(first_dma, 16)
        sync.dma_start(qk[1][:, 0:TILES * 4 * DH], rope).then_inc(scale_dma, 16)
        for n, row in enumerate((q_scale, k_scale)):
            at = TILES * 4 * DH + n * 2 * DEPTH * DH
            dst = qk[1][:, at:at + 2 * DEPTH * DH].rearrange("p (w l d) -> p w l d", w=2, l=DEPTH)
            whole_row = row.partition_broadcast(P)
            sync.dma_start(dst[:, 0, :, :], whole_row).then_inc(scale_dma, 16)
            sync.dma_start(dst[:, 1, :, 0:WIN], whole_row[:, :, WIN:DH]).then_inc(scale_dma, 16)
            sync.dma_start(dst[:, 1, :, WIN:DH], whole_row[:, :, 0:WIN]).then_inc(scale_dma, 16)
        sync.dma_start(rot[:, 0:TILES * 2 * WIN], mask_in).then_inc(scale_dma, 16)

        def ahead(value):
            if not isinstance(value, int):
                sync.to_reg(value)
            return value

        def unit_loads(v):
            part, dram_layer = v % BATCH, (v // BATCH + 1) % DEPTH
            src = w_qk[bass.ds(dram_layer, 1), :, bass.ds(part * SPLIT, SPLIT)].rearrange("l p n -> (l p) n")
            projected, split_before = ahead(N_PROJ * v), ahead(v + 1)
            ahead((dram_layer * (DIM * QK_COLS) + part * SPLIT) * 4)
            if started(v):
                sync.wait_ge(proj_mm, projected)
            sync.wait_ge(split_done, split_before)
            sync.dma_start(wraw[:, :], src).then_inc(raw_dma, 16)

        def value_weights(layer):
            sync.dma_start(wv[:, :], w_v[bass.ds(layer, 1)].rearrange("l p n -> (l p) n")).then_inc(wv_dma, 16)

        def even_values(v):
            written = ahead(4 * v + 4)
            sync.wait_ge(v_evac, written)
            for half in range(2):
                for odd in range(2):
                    r = slice(64 * half + 32 * odd, 64 * half + 32 * odd + 32)
                    n = SEQ // (2 * WIN) - odd
                    sync.dma_start(v_even[r, odd:odd + n, half, :, :], v_odd[r, 0:n, half, :, :]).then_inc(ve_dma, 16)

        def reload(layer):
            last = N_F * (BATCH * layer - 1)
            at = bass.ds(layer, 1)
            src_o = w_o[at].rearrange("l p (n d) -> (l p) n d", n=PAIRS)
            src_1 = w_1[at].rearrange("l p n -> (l p) n")
            src_2 = w_2[at].rearrange("l p (n d) -> (l p) n d", n=HC)
            counts = [ahead(last + k) for k in (1, 6, 7)]
            for size in (INNER * DIM, DIM * 2 * DIM_INNER, HC * P * DIM):
                ahead(layer * size * 4)
            sync.wait_ge(f_mm, counts[0])
            sync.dma_start(wo[:, :, :], src_o).then_inc(wo_dma, 16)
            sync.wait_ge(f_mm, counts[1])
            sync.dma_start(w1[:, :], src_1).then_inc(w1_dma, 16)
            sync.wait_ge(f_mm, counts[2])
            sync.dma_start(w2[:, :, :], src_2).then_inc(w2_dma, 16)

        sync.wait_ge(zeroed, 4)
        for v in range(2):
            unit_loads(v)
            even_values(v)
        with sync.Fori(0, DEPTH - 1) as layer:
            with sync.Fori(2, BATCH) as part:
                unit_loads(layer * BATCH + part)
                even_values(layer * BATCH + part)
            unit_loads(layer * BATCH + BATCH)
            value_weights(layer + 1)
            even_values(layer * BATCH + BATCH)
            unit_loads(layer * BATCH + BATCH + 1)
            reload(layer + 1)
            even_values(layer * BATCH + BATCH + 1)
        with sync.Fori(UNITS - BATCH + 2, UNITS) as v:
            unit_loads(v)
            even_values(v)

    @block.gpsimd
    def _(pool):
        nc.gpsimd.memset(kbd[:, :, :, :], 0.0).then_inc(zeroed, 1)
        for v in (v_odd, v_even):
            nc.gpsimd.memset(v[:, :, :, :, :], 0.0).then_inc(zeroed, 1)
        nc.gpsimd.memset(gp[:, :, :], 0.0).then_inc(zeroed, 1)
        nc.gpsimd.memset(ap[:, :, :], 0.0).then_inc(zeroed, 1)
        pool.wait_ge(zeroed, 5)
        for half in range(2):
            r = slice(64 * half, 64 * half + 64)
            for v in (v_odd, v_even):
                nc.gpsimd.memset(v[r, :, half, :, DH:VW], 1.0).then_inc(zeroed, 1)

        def rope_add(v, t, half):
            n = 2 * v + t
            r = slice(half * INNER, (half + 1) * INNER)
            pool.wait_ge(roped, 4 * n + 2 * half + 2)
            nc.gpsimd.tensor_tensor(qk[t][:, r], qk[t][:, r], rot[:, r], ALU.add).then_inc(rope_added, 1)

        def rope_norm(v, t, half):
            n = 2 * v + t
            pool.wait_ge(rn_done, n + 1)
            pool.wait_ge(rope_added, 2 * n + half + 1)
            h = qk[t][:, half * INNER:(half + 1) * INNER].rearrange("p (h d) -> p h d", d=DH)
            w = rn[t][:, half * HEADS:(half + 1) * HEADS].unsqueeze(2).broadcast_to([P, HEADS, DH])
            nc.gpsimd.tensor_tensor(h, h, w, ALU.mult).then_inc(qk_done, 1)

        def hidden(u):
            pool.wait_ge(gelu_done, u + 1)
            nc.gpsimd.tensor_tensor(gp[:, :, :], gp[:, :, :], ap[:, :, :], ALU.mult).then_inc(h_done, 1)

        def body(it):
            proj, ffn = has(it, 1), has(it, -1)
            if proj:
                rope_add(it + 1, 0, 0)
                rope_add(it + 1, 0, 1)
                rope_norm(it + 1, 0, 0)
            if ffn:
                hidden(it - 1)
            if proj:
                rope_norm(it + 1, 0, 1)
                rope_add(it + 1, 1, 0)
                rope_add(it + 1, 1, 1)
                rope_norm(it + 1, 1, 0)
                rope_norm(it + 1, 1, 1)

        over_units(pool, body)

    @block.tensor
    def _(pe):
        pe.wait_ge(consts_done, 5)
        pe.wait_ge(zeroed, 9)

        def project_qk(v, n):
            layer = v // BATCH
            par = layer % 2
            t, c = n // 4, n % 4
            if n == 0:
                pe.wait_ge(x_staged, v + 1)
                pe.wait_ge(split_done, BATCH * layer + 1)
            if n >= 2:
                pe.wait_ge(roped, 8 * v + n - 1)
            elif started(v):
                pe.wait_ge(v_evac, 4 * v - 1 + n)
            dst = proj_bank[n % 2][:, :]
            tile = slice(t * P, (t + 1) * P)
            w_hi = wh[:, bass.ds(par, 1), c * 512:(c + 1) * 512].rearrange("p l n -> p (l n)")
            w_lo = wl[:, bass.ds(par, 1), c * 512:(c + 1) * 512].rearrange("p l n -> p (l n)")
            nc.tensor.matmul(dst, xh[:, tile], w_hi, start=True, stop=False)
            nc.tensor.matmul(dst, xh[:, tile], w_lo, start=False, stop=False)
            nc.tensor.matmul(dst, xl[:, tile], w_hi, start=False, stop=True).then_inc(proj_mm, 1)

        def project_v(v, slot):
            layer = v // BATCH
            n = 8 + slot
            if slot == 0:
                pe.wait_ge(wv_dma, 16 * (layer + 1))
            if slot < 2:
                pe.wait_ge(roped, 8 * v + n - 1)
            else:
                pe.wait_ge(v_evac, 4 * v + slot - 1)
            for half in range(2):
                for odd in range(2):
                    r = 64 * half + 32 * odd
                    w = WIN * (2 * slot + odd)
                    mm = nc.tensor.matmul(proj_bank[n % 2][r:r + 32, :], xf[:, w:w + WIN],
                                          wv[:, half * 512:(half + 1) * 512], start=True, stop=True)
            mm.then_inc(proj_mm, 1)

        def transpose4(u, n, blocks):
            if not isinstance(u, int) or N_TR * u + n > 1:
                pe.wait_ge(tr_evac, N_TR * u + n - 1)
            for m in range(4):
                mm = nc.tensor.transpose(tr_bank[n % 2][:, m * P:(m + 1) * P], blocks(m), ident[:, :])
            mm.then_inc(tr_mm, 1)

        def transpose_qk(u, t, c):
            pe.wait_ge(qk_done, 4 * u + 2 * t + c // 2 + 1)
            transpose4(u, TR["qk", t, c], lambda m: qk[t][:, (4 * c + m) * P:(4 * c + m + 1) * P])

        def score(u, t, n):
            last = 4 * u + 2 * t + n - 1
            if started(last):
                pe.wait_ge(sc_evac, last)
            pe.wait_ge(tr_evac, N_TR * u + 1 + max(TR["qk", t, n], *(TR["qk", k, 2 + n] for k in range(t + 1))))
            dst = sc_bank[n]
            nc.tensor.matmul(dst[:, :], identb[:, :], maskb[:, t, :].unsqueeze(1).broadcast_to([P, 8, 2 * WIN]),
                             start=True, stop=False, skip_group_check=True)
            for m in range(4):
                for j in range(4):
                    w = 4 * t + j
                    keys = kbd[:, 4 * n + m, :, WIN * w:WIN * w + 2 * WIN]
                    if w % 2 == 0:
                        keys = keys.rearrange("p b (k c) -> p b k c", k=2)[:, :, ::-1, :]
                    mm = nc.tensor.matmul(dst[32 * j:32 * j + 32, m * P:(m + 1) * P],
                                          qT[t][:, 4 * n + m, WIN * j:WIN * j + WIN], keys,
                                          start=False, stop=True, skip_group_check=True)
            mm.then_inc(sc_mm, 1)

        def transpose_p(u, t, m):
            pe.wait_ge(exp_done, 4 * u + 2 * t + m + 1)
            transpose4(u, TR["p", t, m], lambda k: pr[t][:, 4 * m + k, :, :].rearrange("p b c -> p (b c)"))

        def attend(u, t, c):
            last = N_PV * u + 3 * t + c
            if started(last):
                pe.wait_ge(pv_evac, last)
            lo, hi = PV_CHUNKS[c]
            if c == 0:
                pe.wait_ge(tr_evac, N_TR * u + TR["p", t, 1] + 1)
                if t == 0:
                    pe.wait_ge(ve_dma, 64 * (u + 1))
                    pe.wait_ge(v_evac, 4 * u + 4)
            for k in range(lo, hi):
                for j in range(4):
                    v = v_odd if j % 2 else v_even
                    mm = nc.tensor.matmul(pv_bank[32 * j:32 * j + 32, (k - lo) * 2 * VW:(k - lo + 1) * 2 * VW],
                                          pT[:, k, WIN * j:WIN * j + WIN], v[:, 2 * t + j // 2, :, k, :],
                                          start=True, stop=True, skip_group_check=True)
            mm.then_inc(pv_mm, 1)

        def transpose_o(u, t, m):
            pe.wait_ge(pv_evac, N_PV * u + 3 * t + 2 + m)
            transpose4(u, TR["o", t, m], lambda k: o[:, 4 * m + k, :, :].rearrange("p b d -> p (b d)"))

        def out_proj(u):
            pe.wait_ge(wo_dma, 16 * (u // BATCH + 1))
            pe.wait_ge(tr_evac, N_TR * u + TR["o", 1, 1] + 1)
            if started(u):
                pe.wait_ge(state_ready, BATCH + u)
            for k in range(PAIRS):
                mm = nc.tensor.matmul(f_bank[:, 0:SEQ], wo[:, k, :], oT[:, k, :], start=(k == 0), stop=(k == PAIRS - 1))
            mm.then_inc(f_mm, 1)

        def norm_centre(u):
            pe.wait_ge(res1, u + 1)
            nc.tensor.matmul(f_bank[:, 0:SEQ], centre[:, :], xs[:, bass.ds(u % BATCH, 1), 0:SEQ].rearrange("p b s -> p (b s)"),
                             start=True, stop=True, skip_group_check=True).then_inc(f_mm, 1)

        def norm_var(u):
            pe.wait_ge(f_squared, u + 1)
            nc.tensor.matmul(f_bank[:, SEQ:2 * SEQ], ones_mean[:, :], fq[:, :], start=True, stop=True,
                             skip_group_check=True).then_inc(f_mm, 1)

        def ffn_in(u, c):
            rows = P if c < HC - 1 else HLAST
            if c == 0:
                pe.wait_ge(w1_dma, 16 * (u // BATCH + 1))
                pe.wait_ge(f_norm, u + 1)
            else:
                pe.wait_ge(h_evac, HC * u + c)
            nc.tensor.matmul(f_bank[0:rows, 0:SEQ], w1[:, c * P:c * P + rows], fx[:, :], start=True, stop=True,
                             skip_group_check=True)
            nc.tensor.matmul(f_bank[0:rows, SEQ:2 * SEQ], w1[:, DIM_INNER + c * P:DIM_INNER + c * P + rows], fx[:, :],
                             start=True, stop=True, skip_group_check=True).then_inc(f_mm, 1)

        def ffn_out(u):
            pe.wait_ge(w2_dma, 16 * (u // BATCH + 1))
            pe.wait_ge(h_done, u + 1)
            for c in range(HC):
                mm = nc.tensor.matmul(f_bank[:, 0:SEQ], w2[:, c, :], gp[:, c, :], start=(c == 0), stop=(c == HC - 1))
            mm.then_inc(f_mm, 1)

        def body(it):
            proj, attn, ffn = has(it, 1), has(it, 0), has(it, -1)
            if attn:
                transpose_qk(it, 0, 0)
            if ffn:
                out_proj(it - 1)
            if attn:
                transpose_qk(it, 0, 1)
            if proj:
                project_qk(it + 1, 0)
            if attn:
                transpose_qk(it, 0, 2)
            if ffn:
                norm_centre(it - 1)
            if proj:
                project_qk(it + 1, 1)
            if attn:
                transpose_qk(it, 0, 3)
                score(it, 0, 0)
                transpose_qk(it, 1, 0)
            if proj:
                project_qk(it + 1, 2)
            if ffn:
                norm_var(it - 1)
            if attn:
                transpose_qk(it, 1, 1)
                transpose_qk(it, 1, 2)
                score(it, 0, 1)
            if proj:
                project_qk(it + 1, 3)
            if attn:
                transpose_qk(it, 1, 3)
                score(it, 1, 0)
            if proj:
                project_qk(it + 1, 4)
            if attn:
                transpose_p(it, 0, 0)
                transpose_p(it, 0, 1)
                score(it, 1, 1)
                attend(it, 0, 0)
            if proj:
                project_qk(it + 1, 5)
            if ffn:
                ffn_in(it - 1, 0)
            if proj:
                project_qk(it + 1, 6)
            if attn:
                attend(it, 0, 1)
            if ffn:
                ffn_in(it - 1, 1)
            if proj:
                project_qk(it + 1, 7)
            if attn:
                transpose_p(it, 1, 0)
                attend(it, 0, 2)
                transpose_p(it, 1, 1)
            if ffn:
                ffn_in(it - 1, 2)
            if attn:
                transpose_o(it, 0, 0)
                attend(it, 1, 0)
                transpose_o(it, 0, 1)
            if proj:
                project_v(it + 1, 0)
            if attn:
                attend(it, 1, 1)
            if proj:
                project_v(it + 1, 1)
            if attn:
                transpose_o(it, 1, 0)
                attend(it, 1, 2)
            if proj:
                project_v(it + 1, 2)
                project_v(it + 1, 3)
            if ffn:
                ffn_out(it - 1)
            if attn:
                transpose_o(it, 1, 1)

        over_units(pe, body)

    @block.scalar
    def _(act):
        act.wait_ge(first_dma, 32)
        act.wait_ge(zeroed, 9)

        load_ln_exp(nc, act)

        def evac_qk(u, t, c):
            n = TR["qk", t, c]
            act.wait_ge(tr_mm, N_TR * u + n + 1)
            src = tr_bank[n % 2][:, :].rearrange("p (m s) -> p m s", m=4)
            if c < 2:
                if c == 0 and started(u):
                    act.wait_ge(sc_mm, 4 * (u - 1) + 2 * t + 2)
                nc.scalar.copy(qT[t][:, 4 * c:4 * c + 4, :], src).then_inc(tr_evac, 1)
            else:
                k0 = 4 * (c - 2)
                at = slice(WIN + t * P, WIN + (t + 1) * P)
                if c == 2 and started(u):
                    act.wait_ge(sc_mm, 4 * u)
                nc.scalar.copy(kbd[0:DH, k0:k0 + 4, 0, at], src[0:DH])
                nc.scalar.copy(kbd[DH:P, k0:k0 + 4, 1, at], src[DH:P]).then_inc(tr_evac, 1)

        def exps(u, t, n):
            act.wait_ge(sc_evac, 4 * u + 2 * t + n + 1)
            v = pr[t][:, 4 * n:4 * n + 4, :, :]
            nc.scalar.activation(v, v, ACT.Exp).then_inc(exp_done, 1)

        def evac_pt(u, t, m):
            n = TR["p", t, m]
            act.wait_ge(tr_mm, N_TR * u + n + 1)
            if m == 0 and started(2 * u + t if isinstance(u, int) else u):
                act.wait_ge(pv_mm, N_PV * u + 3 * t)
            nc.scalar.copy(pT[:, 4 * m:4 * m + 4, :], tr_bank[n % 2][:, :].rearrange("p (k s) -> p k s", k=4))\
                .then_inc(tr_evac, 1)

        def evac_ot(u, t, m):
            n = TR["o", t, m]
            act.wait_ge(tr_mm, N_TR * u + n + 1)
            if m == 0 and t == 0 and started(u):
                act.wait_ge(f_mm, N_F * (u - 1) + 1)
            nc.scalar.copy(oT[:, 4 * m:4 * m + 4, t * P:(t + 1) * P],
                           tr_bank[n % 2][:, :].rearrange("p (k s) -> p k s", k=4)).then_inc(tr_evac, 1)

        def squares(v, n):
            act.wait_ge(proj_mm, N_PROJ * v + n + 1)
            if not isinstance(v, int) or 8 * v + n >= 2:
                act.wait_ge(sums_done, 8 * v + n - 1)
            nc.scalar.activation(sqr[:, n % 2, :], proj_bank[n % 2][:, :], ACT.Square).then_inc(squared, 1)

        def inverse_norms(v, t):
            n = 2 * v + t
            act.wait_ge(floored, n + 1)
            if started(v):
                act.wait_ge(qk_done, 2 * (n - 2) + 2)
            nc.scalar.activation(rn[t][:, :], ss[t][:, :], ACT.Ln).then_inc(rn_log, 1)
            act.wait_ge(rn_log, n + 1)
            nc.scalar.activation(rn[t][:, :], rn[t][:, :], ACT.Exp, scale=-0.5).then_inc(rn_done, 1)

        def evac_v(v, slot):
            act.wait_ge(proj_mm, N_PROJ * v + 8 + slot + 1)
            if slot == 0 and started(v):
                act.wait_ge(ve_dma, 64 * v)
                act.wait_ge(pv_mm, N_PV * (v - 1) + 3)
            if slot == 2 and started(v):
                act.wait_ge(pv_mm, N_PV * v)
            src = proj_bank[slot % 2]
            nc.scalar.copy(v_odd[0:DH, slot, 0, :, 0:DH], src[0:DH, :].rearrange("p (h d) -> p h d", d=DH))
            nc.scalar.copy(v_odd[DH:P, slot, 1, :, 0:DH], src[DH:P, :].rearrange("p (h d) -> p h d", d=DH))\
                .then_inc(v_evac, 1)

        def norm_square(u):
            act.wait_ge(f_mm, N_F * u + 2)
            nc.scalar.activation(fq[:, :], f_bank[:, 0:SEQ], ACT.Square).then_inc(f_squared, 1)

        def norm_root(u):
            act.wait_ge(f_mm, N_F * u + 3)
            if started(u):
                act.wait_ge(f_scaled, u)
            nc.scalar.activation(fr[:, :], f_bank[:, SEQ:2 * SEQ], ACT.Ln, bias=eps_col[:, 0:1]).then_inc(f_log, 1)
            act.wait_ge(f_log, u + 1)
            nc.scalar.activation(fr[:, :], fr[:, :], ACT.Exp, scale=-0.5).then_inc(f_rstd, 1)

        def evac_hidden(u, c):
            rows = P if c < HC - 1 else HLAST
            layer = u // BATCH
            act.wait_ge(f_mm, N_F * u + 4 + c)
            if c == 0 and started(u):
                act.wait_ge(f_mm, N_F * u)
            for dst, half, col in ((ap, 0, C_B1A), (gp, 1, C_B1G)):
                ins = nc.scalar.activation(dst[0:rows, c, :], f_bank[0:rows, half * SEQ:(half + 1) * SEQ], ACT.Identity,
                                           bias=cols[0:rows, bass.ds(layer, 1), col + c:col + c + 1].rearrange("p l c -> p (l c)"))
            ins.then_inc(h_evac, 1)

        def gelu(u):
            act.wait_ge(h_evac, HC * (u + 1))
            nc.scalar.activation(gp[:, :, :], gp[:, :, :], ACT.Gelu).then_inc(gelu_done, 1)
            load_ln_exp(nc, act)

        def body(it):
            proj, attn, ffn = has(it, 1), has(it, 0), has(it, -1)
            if attn:
                evac_qk(it, 0, 0)
                evac_qk(it, 0, 1)
            if proj:
                squares(it + 1, 0)
            if attn:
                evac_qk(it, 0, 2)
            if proj:
                squares(it + 1, 1)
            if ffn:
                norm_square(it - 1)
            if attn:
                evac_qk(it, 0, 3)
                evac_qk(it, 1, 0)
            if proj:
                squares(it + 1, 2)
            if ffn:
                norm_root(it - 1)
            if attn:
                evac_qk(it, 1, 1)
                exps(it, 0, 0)
                evac_qk(it, 1, 2)
            if proj:
                squares(it + 1, 3)
            if attn:
                evac_qk(it, 1, 3)
                exps(it, 0, 1)
            if proj:
                squares(it + 1, 4)
            if attn:
                evac_pt(it, 0, 0)
                evac_pt(it, 0, 1)
            if proj:
                inverse_norms(it + 1, 0)
                squares(it + 1, 5)
            if ffn:
                evac_hidden(it - 1, 0)
            if attn:
                exps(it, 1, 0)
            if proj:
                squares(it + 1, 6)
            if attn:
                exps(it, 1, 1)
            if ffn:
                evac_hidden(it - 1, 1)
            if proj:
                squares(it + 1, 7)
            if attn:
                evac_pt(it, 1, 0)
                evac_pt(it, 1, 1)
            if ffn:
                evac_hidden(it - 1, 2)
            if attn:
                evac_ot(it, 0, 0)
            if ffn:
                gelu(it - 1)
            if proj:
                evac_v(it + 1, 0)
                evac_v(it + 1, 1)
            if attn:
                evac_ot(it, 0, 1)
                evac_ot(it, 1, 0)
            if proj:
                evac_v(it + 1, 2)
                evac_v(it + 1, 3)
            if attn:
                evac_ot(it, 1, 1)
            if proj:
                inverse_norms(it + 1, 1)

        over_units(act, body)

    @block.vector
    def _(dve):
        dve.wait_ge(scale_dma, 16 * 8)
        base = qk[1][:, 0:TILES * 4 * DH].rearrange("p (t k d) -> p t k d", t=TILES, k=4)
        for t in range(TILES):
            for kind in range(4):
                at = TILES * 4 * DH + kind * DEPTH * DH
                row = qk[1][:, at:at + DEPTH * DH].rearrange("p (l d) -> p l d", l=DEPTH)
                ins = nc.vector.tensor_tensor(tab[:, :, t, kind, :], row,
                                              base[:, t, kind, :].unsqueeze(1).broadcast_to([P, DEPTH, DH]), ALU.mult)
        ins.then_inc(consts_done, 1)
        nc.vector.tensor_copy(maskb[:, :, :], rot[:, 0:TILES * 2 * WIN].rearrange("p (t c) -> p t c", t=TILES)).then_inc(consts_done, 1)
        nc.vector.tensor_copy(identb[:, :], ident[:, :]).then_inc(consts_done, 1)
        nc.vector.memset(ss[0][:, :], 0.0).then_inc(state_ready, BATCH)
        nc.vector.tensor_tensor(centre[:, :], ident[:, :], ones_mean[:, :], ALU.subtract).then_inc(consts_done, 1)
        dve.wait_ge(first_dma, 32)
        nc.vector.tensor_copy(wh[:, 0, :], qk[0][:, :]).then_inc(consts_done, 1)
        dve.wait_ge(consts_done, 5)
        nc.vector.tensor_tensor(wl[:, 0, :], qk[0][:, :], wh[:, 0, :].bitcast(F32), ALU.subtract).then_inc(split_done, 1)
        dve.wait_ge(split_done, 1)

        def unit_input(v):
            return xs[:, bass.ds(v % BATCH, 1), 0:SEQ].rearrange("p b s -> p (b s)")

        def stage_high(v):
            if started(v):
                dve.wait_ge(proj_mm, N_PROJ * v)
            dve.wait_ge(state_ready, v + 1)
            nc.vector.tensor_copy(xf[:, :], unit_input(v))
            nc.vector.tensor_copy(xh[:, :], unit_input(v)).then_inc(x_hi, 1)

        def stage_low(v):
            dve.wait_ge(x_hi, v + 1)
            nc.vector.tensor_tensor(xl[:, :], unit_input(v), xh[:, :].bitcast(F32), ALU.subtract).then_inc(x_staged, 1)

        def split_target(v, w):
            return w[:, bass.ds((v // BATCH + 1) % 2, 1), bass.ds((v % BATCH) * SPLIT, SPLIT)].rearrange("p l n -> p (l n)")

        def split_high(v):
            dve.wait_ge(raw_dma, 16 * (v + 1))
            nc.vector.tensor_copy(split_target(v, wh), wraw[:, :]).then_inc(split_hi, 1)

        def split_low(v):
            dve.wait_ge(split_hi, v + 1)
            nc.vector.tensor_tensor(split_target(v, wl), wraw[:, :], split_target(v, wh).bitcast(F32),
                                    ALU.subtract).then_inc(split_done, 1)

        def rotate(v, n):
            layer = v // BATCH
            t, c = n // 4, n % 4
            kind = 2 * (c // 2)
            dve.wait_ge(squared, 8 * v + n + 1)
            if c % 2 == 0 and started(2 * v + t if isinstance(v, int) else v):
                dve.wait_ge(rope_added, 2 * (2 * v + t) - 1 + c // 2)
            if started(v):
                dve.wait_ge(tr_mm, N_TR * (v - 1) + TR["qk", t, c] + 1)
            src = proj_bank[n % 2][:, :].rearrange("p (h a d) -> p h a d", a=2, d=WIN)
            cos = tab[:, bass.ds(layer, 1), t, kind, :].broadcast_to([P, 8, DH])
            sin = tab[:, bass.ds(layer, 1), t, kind + 1, :].broadcast_to([P, 8, DH])
            r = slice(c * 512, (c + 1) * 512)
            nc.vector.tensor_tensor(qk[t][:, r].rearrange("p (h d) -> p h d", d=DH),
                                    proj_bank[n % 2][:, :].rearrange("p (h d) -> p h d", d=DH), cos, ALU.mult)
            nc.vector.tensor_tensor(rot[:, r].rearrange("p (h a d) -> p h a d", a=2, d=WIN), src[:, :, ::-1, :],
                                    sin.rearrange("p h (a d) -> p h a d", a=2), ALU.mult).then_inc(roped, 1)

        def head_sums(v, n):
            t, c = n // 4, n % 4
            dve.wait_ge(squared, 8 * v + n + 1)
            if c == 0 and started(v):
                dve.wait_ge(rn_log, 2 * v + t - 1)
            nc.vector.tensor_reduce(ss[t][:, c * 8:(c + 1) * 8], sqr[:, c % 2, :].rearrange("p (h d) -> p h d", d=DH),
                                    AX.X, ALU.add).then_inc(sums_done, 1)

        def floor_sums(v, t):
            dve.wait_ge(sums_done, 8 * v + 4 * t + 4)
            nc.vector.tensor_scalar(ss[t][:, :], ss[t][:, :], 1e-24, None, ALU.max).then_inc(floored, 1)

        def pair_scores(n):
            return sc_bank[n][:, :].rearrange("p (h c) -> p h c", c=2 * WIN)

        def softmax_max(u, t, n):
            k = 4 * u + 2 * t + n
            dve.wait_ge(sc_mm, k + 1)
            if started(k - 1 if isinstance(k, int) else k):
                dve.wait_ge(sc_evac, k - 1)
            nc.vector.tensor_reduce(mx[:, n, :], pair_scores(n), AX.X, ALU.max).then_inc(max_done, 1)

        def softmax_subtract(u, t, n):
            dve.wait_ge(max_done, 4 * u + 2 * t + n + 1)
            if started(u):
                dve.wait_ge(tr_mm, N_TR * (u - 1) + TR["p", t, n] + 1)
            nc.vector.tensor_tensor(pr[t][:, 4 * n:4 * n + 4, :, :].rearrange("p k b c -> p (k b) c"), pair_scores(n),
                                    mx[:, n, :].unsqueeze(2).broadcast_to([P, 8, 2 * WIN]), ALU.subtract)\
                .then_inc(sc_evac, 1)

        def attended(c):
            return pv_bank[:, 0:2 * pairs_of(c) * VW].rearrange("p (h e) -> p h e", e=VW)

        def pairs_of(c):
            return PV_CHUNKS[c][1] - PV_CHUNKS[c][0]

        def reciprocals(u, t, c):
            dve.wait_ge(pv_mm, N_PV * u + 3 * t + c + 1)
            nc.vector.reciprocal(rs[:, c % 2, 0:2 * pairs_of(c)], attended(c)[:, :, DH]).then_inc(recip_done, 1)

        def normalise(u, t, c):
            lo, hi = PV_CHUNKS[c]
            m = 2 * (hi - lo)
            dve.wait_ge(recip_done, N_PV * u + 3 * t + c + 1)
            if c == 0:
                if t == 1:
                    dve.wait_ge(tr_mm, N_TR * u + TR["o", 0, 1] + 1)
                elif started(u):
                    dve.wait_ge(tr_mm, N_TR * (u - 1) + TR["o", 1, 1] + 1)
            nc.vector.tensor_tensor(o[:, lo:hi, :, :].rearrange("p k b d -> p (k b) d"), attended(c)[:, :, 0:DH],
                                    rs[:, c % 2, 0:m].unsqueeze(2).broadcast_to([P, m, DH]), ALU.mult).then_inc(pv_evac, 1)

        def halves(u):
            b = bass.ds(u % BATCH, 1)
            for half in range(2):
                r = slice(64 * half, 64 * half + 64)
                yield r, xs[r, b, half:half + SEQ].rearrange("p b s -> p (b s)")

        def residual1(u):
            dve.wait_ge(f_mm, N_F * u + 1)
            for r, v in halves(u):
                ins = nc.vector.tensor_tensor(v, f_bank[r, 0:SEQ], v, ALU.add)
            ins.then_inc(res1, 1)

        def norm_column(u, c):
            return cols[:, bass.ds(u // BATCH, 1), c:c + 1].rearrange("p l c -> p (l c)")

        def norm_scale(u):
            dve.wait_ge(f_rstd, u + 1)
            nc.vector.scalar_tensor_tensor(out=fx[:, :], in0=f_bank[:, 0:SEQ], scalar=norm_column(u, C_G), in1=fr[:, :],
                                           op0=ALU.mult, op1=ALU.mult).then_inc(f_scaled, 1)

        def norm_shift(u):
            dve.wait_ge(f_scaled, u + 1)
            nc.vector.tensor_scalar(fx[:, :], fx[:, :], norm_column(u, C_B), None, ALU.add).then_inc(f_norm, 1)

        def residual2(u):
            layer = bass.ds(u // BATCH, 1)
            dve.wait_ge(f_mm, N_F * u + 7)
            for r, v in halves(u):
                ins = nc.vector.scalar_tensor_tensor(out=v, in0=f_bank[r, 0:SEQ],
                                                     scalar=cols[r, layer, C_B2:C_B2 + 1].rearrange("p l c -> p (l c)"),
                                                     in1=v, op0=ALU.add, op1=ALU.add)
            ins.then_inc(state_ready, 1)

        def body(it):
            proj, attn, ffn = has(it, 1), has(it, 0), has(it, -1)
            if proj:
                stage_high(it + 1)
                stage_low(it + 1)
            if ffn:
                residual1(it - 1)
            if proj:
                rotate(it + 1, 0)
                head_sums(it + 1, 0)
                rotate(it + 1, 1)
            if attn:
                softmax_max(it, 0, 0)
            if proj:
                head_sums(it + 1, 1)
                split_high(it + 1)
            if attn:
                softmax_subtract(it, 0, 0)
            if proj:
                head_sums(it + 1, 2)
                rotate(it + 1, 2)
            if attn:
                softmax_max(it, 0, 1)
            if ffn:
                norm_scale(it - 1)
            if attn:
                softmax_subtract(it, 0, 1)
            if proj:
                head_sums(it + 1, 3)
                rotate(it + 1, 3)
            if ffn:
                norm_shift(it - 1)
            if attn:
                softmax_max(it, 1, 0)
            if proj:
                floor_sums(it + 1, 0)
                rotate(it + 1, 4)
            if attn:
                softmax_subtract(it, 1, 0)
            if proj:
                head_sums(it + 1, 4)
            if attn:
                reciprocals(it, 0, 0)
                softmax_max(it, 1, 1)
                normalise(it, 0, 0)
            if proj:
                rotate(it + 1, 5)
            if attn:
                softmax_subtract(it, 1, 1)
                reciprocals(it, 0, 1)
                normalise(it, 0, 1)
            if proj:
                head_sums(it + 1, 5)
                rotate(it + 1, 6)
            if attn:
                reciprocals(it, 0, 2)
                normalise(it, 0, 2)
                reciprocals(it, 1, 0)
                normalise(it, 1, 0)
            if proj:
                rotate(it + 1, 7)
                split_low(it + 1)
            if attn:
                reciprocals(it, 1, 1)
                normalise(it, 1, 1)
                reciprocals(it, 1, 2)
            if proj:
                head_sums(it + 1, 6)
                head_sums(it + 1, 7)
            if attn:
                normalise(it, 1, 2)
            if proj:
                floor_sums(it + 1, 1)
            if ffn:
                residual2(it - 1)

        over_units(dve, body)


def build_last(nc, ctx, sb, sem, bank, ident, ones_mean, eps_col, x1, xs, out):
    y = sb(ctx, "y", [P, TOK])
    xc = sb(ctx, "xc2", [P, TOK])
    sq = sb(ctx, "sq2", [P, TOK])
    rstd = sb(ctx, "rstd2", [P, TOK])
    res = sb(ctx, "res", [P, TOK])
    copied = sem(ctx, "l_copied")
    mean_mm = sem(ctx, "l_mean_mm")
    centred = sem(ctx, "l_centred")
    squared = sem(ctx, "l_squared")
    var_mm = sem(ctx, "l_var_mm")
    log_done = sem(ctx, "l_log_done")
    rstd_done = sem(ctx, "l_rstd_done")
    scaled = sem(ctx, "l_scaled")
    added = sem(ctx, "l_added")
    out_mm = sem(ctx, "l_out_mm")
    out_evac = sem(ctx, "l_out_evac")
    stored = sem(ctx, "l_stored")

    def tok(g):
        return slice(g * GT, (g + 1) * GT)

    block = ctx.enter_context(nc.Block())

    @block.sync
    def _(sync):
        ov = out.rearrange("b (t p) d -> p (b t) d", p=P)
        for g in range(GROUPS):
            sync.wait_ge(out_evac, g + 1)
            sync.dma_start(ov[:, 4 * g:4 * g + 4, :], res[:, tok(g)].rearrange("p (t d) -> p t d", d=DIM)).then_inc(stored, 16)
        sync.wait_ge(stored, 16 * GROUPS)

    @block.tensor
    def _(pe):
        for g in range(GROUPS):
            pe.wait_ge(copied, g + 1)
            nc.tensor.matmul(bank[g][:, :], ones_mean[:, :], y[:, tok(g)], start=True, stop=True).then_inc(mean_mm, 1)
        for g in range(GROUPS):
            pe.wait_ge(squared, g + 1)
            nc.tensor.matmul(bank[4 + g][:, :], ones_mean[:, :], sq[:, tok(g)], start=True, stop=True).then_inc(var_mm, 1)
        for g in range(GROUPS):
            pe.wait_ge(added, g + 1)
            for t in range(4):
                mm = nc.tensor.transpose(bank[g][:, t * P:(t + 1) * P], xc[:, g * GT + t * P:g * GT + (t + 1) * P], ident[:, :])
            mm.then_inc(out_mm, 1)

    @block.scalar
    def _(act):
        for g in range(GROUPS):
            act.wait_ge(centred, g + 1)
            nc.scalar.activation(sq[:, tok(g)], xc[:, tok(g)], ACT.Square).then_inc(squared, 1)
        for g in range(GROUPS):
            act.wait_ge(var_mm, g + 1)
            nc.scalar.activation(rstd[:, tok(g)], bank[4 + g][:, :], ACT.Ln, bias=eps_col[:, 0:1]).then_inc(log_done, 1)
            act.wait_ge(log_done, g + 1)
            nc.scalar.activation(rstd[:, tok(g)], rstd[:, tok(g)], ACT.Exp, scale=-0.5).then_inc(rstd_done, 1)
        for g in range(GROUPS):
            act.wait_ge(out_mm, g + 1)
            nc.scalar.copy(res[:, tok(g)], bank[g][:, :]).then_inc(out_evac, 1)

    @block.vector
    def _(dve):
        for g in range(GROUPS):
            for half in range(2):
                r = slice(64 * half, 64 * half + 64)
                ins = nc.vector.tensor_copy(y[r, tok(g)].rearrange("p (b s) -> p b s", b=2), xs[r, 2 * g:2 * g + 2, half:half + SEQ])
            ins.then_inc(copied, 1)
        for g in range(GROUPS):
            dve.wait_ge(mean_mm, g + 1)
            dve.wait_ge(copied, g + 1)
            nc.vector.tensor_tensor(xc[:, tok(g)], y[:, tok(g)], bank[g][:, :], ALU.subtract).then_inc(centred, 1)
        for g in range(GROUPS):
            dve.wait_ge(rstd_done, g + 1)
            nc.vector.tensor_tensor(xc[:, tok(g)], xc[:, tok(g)], rstd[:, tok(g)], ALU.mult).then_inc(scaled, 1)
            dve.wait_ge(scaled, g + 1)
            nc.vector.tensor_tensor(xc[:, tok(g)], xc[:, tok(g)], x1[:, tok(g)], ALU.add).then_inc(added, 1)


def rotary_constants():
    half = np.arange(0, DH, 2, dtype=np.float64)
    freqs = np.arange(SEQ)[:, None] / 10000.0 ** (half / DH)[None, :]
    base = (half + 0.4 * DH) / (1.4 * DH)
    scale = base[None, :] ** ((np.arange(SEQ) - SEQ // 2) / (WIN // 2))[:, None]
    cos, sin = np.cos(freqs), np.sin(freqs)
    cos2, sin2, sc2 = (np.concatenate(p, 1) for p in ((cos, cos), (-sin, sin), (scale, scale)))
    t = np.stack([cos2 * sc2 * 8.0, sin2 * sc2 * 8.0, cos2 / sc2, sin2 / sc2], 1)
    return np.ascontiguousarray(t.reshape(TILES, P, 4, DH).transpose(1, 0, 2, 3).reshape(P, -1)).astype(np.float32)


def mask_constants():
    m = np.zeros((P, TILES, 2 * WIN), np.float32)
    r, c = np.arange(WIN)[:, None], np.arange(WIN)[None, :]
    for t in range(TILES):
        for j in range(4):
            rows = slice(WIN * j, WIN * (j + 1))
            before, own = np.where(r > c, -1e30, 0.0), np.where(c > r, -1e30, 0.0)
            if t == 0 and j == 0:
                before = np.full((WIN, WIN), -1e30)
            m[rows, t] = np.concatenate((before, own) if j % 2 else (own, before), 1)
    return np.ascontiguousarray(m.reshape(P, -1))


def matrix_constants():
    u = np.triu(np.ones((P, P), np.float32))
    return np.concatenate([np.eye(P, dtype=np.float32), u, np.ones((P, P), np.float32), u], 1)


def kernel(**inputs):
    import concourse.bacc as bacc
    from concourse.bass_utils import run_bass_kernel_spmd

    a = {k.replace("L0_attn_", "a_").replace("L0_ffn_", "f_"): np.asarray(v) for k, v in inputs.items()}
    wqkv = a["f_Wqkv"]
    wv = wqkv[:, :, 2 * INNER:].reshape(DEPTH, DIM, PAIRS, 2, DH).transpose(0, 1, 3, 2, 4).reshape(DEPTH, DIM, INNER)
    wo = a["f_Wo"].reshape(DEPTH, PAIRS, P, DIM).transpose(0, 2, 1, 3).reshape(DEPTH, P, PAIRS * DIM)
    w2 = np.zeros((DEPTH, HC * P, DIM), np.float32)
    w2[:, :DIM_INNER] = a["f_W2"]
    w2 = w2.reshape(DEPTH, HC, P, DIM).transpose(0, 2, 1, 3).reshape(DEPTH, P, HC * DIM)
    b1 = np.zeros((DEPTH, 2, HC * P), np.float32)
    b1[:, :, :DIM_INNER] = a["f_b1"].reshape(DEPTH, 2, DIM_INNER)
    cols = np.zeros((P, DEPTH, N_COLS), np.float32)
    cols[:, :, C_G] = a["f_ln_g"].T
    cols[:, :, C_B] = a["f_ln_b"].T
    cols[:, :, C_B2] = a["f_b2"].T
    cols[:, :, C_B1A:C_B1A + 2 * HC] = b1.reshape(DEPTH, 2 * HC, P).transpose(2, 0, 1)
    conv = np.concatenate([a["a_conv_w"].reshape(CONV_DIM, D_CONV), a["a_conv_b"].reshape(CONV_DIM, 1)], 1)
    conv = conv.reshape(3, P, D_CONV + 1).transpose(1, 0, 2)
    arrays = {
        "x": a["a_x"], "w_in_t": a["a_W_in"].T, "conv_cols": conv, "a_log": a["a_A_log"],
        "dt_bias": a["a_dt_bias"], "d_skip": a["a_D_skip"], "w_out_t": a["a_W_out"].T,
        "w_qk": wqkv[:, :, :2 * INNER], "w_v": wv, "w_o": wo, "w_1": a["f_W1"], "w_2": w2,
        "q_scale": a["f_q_scale"], "k_scale": a["f_k_scale"], "cols_in": cols,
        "rope": rotary_constants(), "consts": matrix_constants(), "mask_in": mask_constants(),
    }
    arrays = {k: np.ascontiguousarray(v) for k, v in arrays.items()}
    nc = bacc.Bacc("TRN2", target_bir_lowering=False, num_devices=1)
    aps = {k: nc.dram_tensor(f"in_{k}", v.shape, mybir.dt.from_np(v.dtype), kind="ExternalInput").ap()
           for k, v in arrays.items()}
    out = nc.dram_tensor("out_y", (BATCH, SEQ, DIM), F32, kind="ExternalOutput").ap()
    build(nc, out=out, **aps)
    got = run_bass_kernel_spmd(nc, [{f"in_{k}": v for k, v in arrays.items()}], core_ids=[0])
    return got.results[0]["out_y"]
```

```python
from contextlib import ExitStack

import numpy as np

import concourse.bass as bass
from concourse import mybir

F32 = mybir.dt.float32
F32R = mybir.dt.float32r
ALU = mybir.AluOpType
ACT = mybir.ActivationFunctionType
AX = mybir.AxisListType

P = 128
BATCH, SEQ, DIM = 8, 256, 128
TOK = BATCH * SEQ
TILES = SEQ // P
D_INNER, D_STATE, D_CONV, NHEADS = 256, 64, 4, 2
CONV_DIM = D_INNER + 2 * D_STATE
PROJ = D_INNER + CONV_DIM + NHEADS
GROUPS = 4
GT = TOK // GROUPS
DEPTH, HEADS, DH, WIN = 6, 16, 64, 32
PAIRS = HEADS // 2
INNER = HEADS * DH
DIM_INNER = int(DIM * 4 * 2 / 3)
HC = 3
HLAST = DIM_INNER - 2 * P
UNITS = DEPTH * BATCH
VW = DH + 1
LN_EPS = 1e-5
LN_EXP_SET = 6
UNROLL = 4
N_PROJ, N_SC, N_TR, N_PV, N_F = 12, 4, 16, 6, 7
QK_COLS = 2 * INNER
SPLIT = QK_COLS // BATCH
PV_CHUNKS = [(0, 3), (3, 6), (6, 8)]
C_G, C_B, C_B2, C_B1A, C_B1G = 0, 1, 2, 3, 6
N_COLS = 9


def started(value):
    return not isinstance(value, int) or value > 0


def build(nc, x, w_in_t, conv_cols, a_log, dt_bias, d_skip, w_out_t, w_qk, w_v, w_o, w_1, w_2,
          q_scale, k_scale, cols_in, rope, consts, mask_in, out):
    whole = ExitStack()
    with whole:
        def sb(stack, name, shape, dt=F32):
            return stack.enter_context(nc.sbuf_tensor(name, shape, dt))

        def sem(stack, name):
            return stack.enter_context(nc.semaphore(name))

        ident = sb(whole, "ident", [P, P])
        ones_mean = sb(whole, "ones_mean", [P, P])
        eps_col = sb(whole, "eps_col", [P, 1])
        x1 = sb(whole, "x1", [P, TOK])
        xs = sb(whole, "xs", [P, BATCH, SEQ + 1])
        first = {name: sb(whole, name, shape) for name, shape in (
            ("qk0", [P, QK_COLS]), ("wv", [P, INNER]), ("wo", [P, PAIRS, DIM]), ("w1", [P, 2 * DIM_INNER]),
            ("w2", [P, HC, DIM]), ("cols", [P, DEPTH, N_COLS]), ("mask", [P, TILES, 2 * WIN]), ("centre", [P, P]),
            ("tab", [P, DEPTH, TILES, 4, DH]))}
        loaded = {name: sem(whole, f"{name}_dma") for name in ("first", "wv", "wo", "w1", "w2")}
        bank = [whole.enter_context(nc.psum_tensor(f"bank{i}", [P, 512], F32)) for i in range(8)]

        with ExitStack() as mixer:
            build_mixer(nc, mixer, sb, sem, bank, ident, ones_mean, eps_col, x1, xs, first, loaded, x, w_in_t,
                        conv_cols, a_log, dt_bias, d_skip, w_out_t, consts, w_qk, w_v, w_o, w_1, w_2, q_scale,
                        k_scale, cols_in, rope, mask_in)
        with ExitStack() as layers:
            build_layers(nc, layers, sb, sem, bank, ident, ones_mean, eps_col, xs, first, loaded, w_qk, w_v,
                         w_o, w_1, w_2)
        with ExitStack() as last:
            build_last(nc, last, sb, sem, bank, ident, ones_mean, eps_col, x1, xs, out)


def load_ln_exp(nc, act):
    act.add_instruction(mybir.InstLoadActFuncSet(name=nc.get_next_instruction_name(), act_func_set_id=LN_EXP_SET,
                                                 ins=[], outs=[]))


def build_mixer(nc, ctx, sb, sem, bank, ident, ones_mean, eps_col, x1, xs, first, loaded, x, w_in_t, conv_cols,
                a_log, dt_bias, d_skip, w_out_t, consts, w_qk, w_v, w_o, w_1, w_2, q_scale, k_scale, cols_in, rope,
                mask_in):
    NT = TOK // P
    HB = BATCH * TILES * NHEADS
    xin = sb(ctx, "xin", [P, NT, P])
    win = sb(ctx, "win", [P, PROJ])
    wout = sb(ctx, "wout", [P, NHEADS, DIM])
    tri = sb(ctx, "tri", [P, 3 * P])
    convw = sb(ctx, "convw", [P, 3, D_CONV + 1])
    heads = sb(ctx, "heads", [P, 4, NHEADS])
    xc = sb(ctx, "xc", [P, TOK])
    sq = sb(ctx, "sq", [P, TOK])
    rstd = sb(ctx, "rstd", [P, TOK])
    xn = sb(ctx, "xn", [P, TOK])
    zs = sb(ctx, "zs", [P, 2, TOK])
    raw = sb(ctx, "raw", [P, 3, BATCH, SEQ + 3])
    cv = sb(ctx, "cv", [P, 3, BATCH, SEQ])
    c_low = sb(ctx, "c_low", [D_STATE, BATCH, SEQ])
    sp = sb(ctx, "sp", [P, 12, HB])
    dec = sb(ctx, "dec", [P, 2, NHEADS, 3 * P])
    gm = sb(ctx, "gm", [P, 2, 3 * P])
    st = sb(ctx, "st", [P, 2, NHEADS, 3 * P])
    xnat = sb(ctx, "xnat", [P, 2, 4, P])
    yy = sb(ctx, "yy", [P, 2, NHEADS, SEQ])
    tri_r = sb(ctx, "tri_r", [P, 3 * P], F32R)
    da_r = sb(ctx, "da_r", [P, 2, HB], F32R)
    diag = sb(ctx, "diag", [P, D_CONV, P])
    BIAS, R, NEG, E, U, L, V, M, DT, DA, CS, TMP = range(12)

    stage = zs[:, 0, :]

    def seq_square(k, b):
        return (sq, xc)[k][:, b * SEQ:(b + 1) * SEQ]

    def seq_scale(k, b):
        return rstd[:, b * SEQ:(b + 1) * SEQ] if k == 0 else raw[:, 0, b, 0:SEQ]

    def scale_rows(n):
        return zs[:, n, TILES * 4 * DH:TILES * 4 * DH + 2 * DEPTH * DH].rearrange("p (w l d) -> p w l d", w=2, l=DEPTH)

    scale_dma = sem(ctx, "m_scale_dma")
    tables_done = sem(ctx, "m_tables_done")
    x_in = [sem(ctx, f"m_x_in{g}") for g in range(GROUPS)]
    ident_dma = sem(ctx, "m_ident_dma")
    w_dma = sem(ctx, "m_w_dma")
    setup = sem(ctx, "m_setup")
    xt_mm = sem(ctx, "m_xt_mm")
    xt_evac = sem(ctx, "m_xt_evac")
    mean_mm = sem(ctx, "m_mean_mm")
    centred = sem(ctx, "m_centred")
    squared = sem(ctx, "m_squared")
    var_mm = sem(ctx, "m_var_mm")
    log_done = sem(ctx, "m_log_done")
    rstd_done = sem(ctx, "m_rstd_done")
    norm_done = sem(ctx, "m_norm_done")
    proj_mm = sem(ctx, "m_proj_mm")
    proj_evac = sem(ctx, "m_proj_evac")
    dt_mm = sem(ctx, "m_dt_mm")
    tap = sem(ctx, "m_tap")
    conv_done = sem(ctx, "m_conv_done")
    silu_done = sem(ctx, "m_silu_done")
    c_moved = sem(ctx, "m_c_moved")
    sp_step = sem(ctx, "m_sp_step")
    sp_act = sem(ctx, "m_sp_act")
    cs_mm = sem(ctx, "m_cs_mm")
    row_mm = sem(ctx, "m_row_mm")
    diff_done = sem(ctx, "m_diff_done")
    dec_done = sem(ctx, "m_dec_done")
    g_mm = sem(ctx, "m_g_mm")
    g_done = sem(ctx, "m_g_done")
    s_done = sem(ctx, "m_s_done")
    xnat_mm = sem(ctx, "m_xnat_mm")
    xnat_evac = sem(ctx, "m_xnat_evac")
    y_mm = sem(ctx, "m_y_mm")
    y_skip = sem(ctx, "m_y_skip")
    y_done = sem(ctx, "m_y_done")
    o_mm = sem(ctx, "m_o_mm")
    o_evac = sem(ctx, "m_o_evac")
    x1_done = sem(ctx, "m_x1_done")
    xs_done = sem(ctx, "m_xs_done")
    diag_done = sem(ctx, "m_diag_done")
    x1_scaled = sem(ctx, "m_x1_scaled")
    seq_centred, seq_squared, seq_var, seq_log, seq_rstd = (
        [sem(ctx, f"m_seq_{name}{k}") for k in range(2)] for name in ("centred", "squared", "var", "log", "rstd"))
    norm_bank = (bank[7], bank[5])

    CONV = "conv"
    JOBS = [(c, g) for c in (4, 2, 3, CONV, 0, 1) for g in range(GROUPS)]
    CONV_DONE = 4 * GROUPS
    DT_STEPS, SPLIT_STEPS, CS_STEPS = 13, 15, 16

    def tok(g):
        return slice(g * GT, (g + 1) * GT)

    def seq(b):
        return slice(b * SEQ, (b + 1) * SEQ)

    def yo(t):
        return t[:, :, :].rearrange("p n d -> p (n d)")

    block = ctx.enter_context(nc.Block())

    @block.sync
    def _(sync):
        xv = x.rearrange("b (t p) d -> p (b t) d", p=P)
        sync.dma_start(ident[:, :], consts[:, 0:P]).then_inc(ident_dma, 16)
        for g in range(GROUPS):
            sync.dma_start(xin[:, 4 * g:4 * g + 4, :], xv[:, 4 * g:4 * g + 4, :]).then_inc(x_in[g], 16)
        sync.dma_start(win[:, :], w_in_t).then_inc(w_dma, 16)
        sync.dma_start(convw[:, :, :], conv_cols).then_inc(w_dma, 16)
        sync.dma_start(tri[:, :], consts[:, P:4 * P]).then_inc(w_dma, 16)
        sync.dma_start(wout[:, :, :], w_out_t.rearrange("(h p) d -> p h d", p=P)).then_inc(w_dma, 16)
        for n, row in enumerate((a_log, dt_bias, d_skip)):
            sync.dma_start(heads[:, n, :], row.partition_broadcast(P)).then_inc(w_dma, 16)
        sync.dma_start(stage[:, 0:TILES * 4 * DH], rope).then_inc(scale_dma, 16)
        for n, row in enumerate((q_scale, k_scale)):
            dst = scale_rows(n)
            whole_row = row.partition_broadcast(P)
            sync.dma_start(dst[:, 0, :, :], whole_row).then_inc(scale_dma, 16)
            sync.dma_start(dst[:, 1, :, 0:WIN], whole_row[:, :, WIN:DH]).then_inc(scale_dma, 16)
            sync.dma_start(dst[:, 1, :, WIN:DH], whole_row[:, :, 0:WIN]).then_inc(scale_dma, 16)
        sync.dma_start(first["qk0"][:, :], w_qk[0]).then_inc(loaded["first"], 16)
        sync.dma_start(first["cols"][:, :, :], cols_in).then_inc(loaded["first"], 16)
        sync.dma_start(first["mask"][:, :, :], mask_in.rearrange("p (t c) -> p t c", t=TILES)).then_inc(loaded["first"], 16)
        sync.dma_start(first["wv"][:, :], w_v[0]).then_inc(loaded["wv"], 16)
        sync.dma_start(first["wo"][:, :, :], w_o[0].rearrange("p (n d) -> p n d", n=PAIRS)).then_inc(loaded["wo"], 16)
        sync.dma_start(first["w1"][:, :], w_1[0]).then_inc(loaded["w1"], 16)
        sync.dma_start(first["w2"][:, :, :], w_2[0].rearrange("p (n d) -> p n d", n=HC)).then_inc(loaded["w2"], 16)
        for g in range(GROUPS):
            sync.wait_ge(proj_evac, CONV_DONE - GROUPS + g + 1)
            sync.dma_start(c_low[:, 2 * g:2 * g + 2, :], cv[D_STATE:P, 2, 2 * g:2 * g + 2, :]).then_inc(c_moved, 16)

    W_ALL = 7 * 16

    @block.gpsimd
    def _(pool):
        nc.gpsimd.memset(ones_mean[:, :], 1.0 / DIM).then_inc(setup, 1)
        nc.gpsimd.memset(eps_col[:, :], LN_EPS).then_inc(setup, 1)
        nc.gpsimd.memset(raw[:, :, :, 0:3], 0.0).then_inc(setup, 1)
        nc.gpsimd.memset(xs[:, :, 0:1], 0.0).then_inc(setup, 1)

    @block.tensor
    def _(pe):
        pe.wait_ge(setup, 4)
        pe.wait_ge(ident_dma, 16)

        def mean_of(n, src, g, ready, count):
            pe.wait_ge(ready, count)
            if n >= 2:
                pe.wait_ge(log_done, n - 1)
            nc.tensor.matmul(bank[n % 2][:, :], ones_mean[:, :], src[:, tok(g)], start=True, stop=True).then_inc(mean_mm, 1)

        def var_of(n, g):
            pe.wait_ge(squared, n + 1)
            nc.tensor.matmul(bank[n % 2][:, :], ones_mean[:, :], sq[:, tok(g)], start=True, stop=True).then_inc(var_mm, 1)

        for g in range(GROUPS):
            pe.wait_ge(x_in[g], 16)
            if g >= 2:
                pe.wait_ge(xt_evac, g - 1)
            for t in range(4):
                mm = nc.tensor.transpose(bank[2 + g % 2][:, t * P:(t + 1) * P], xin[:, 4 * g + t, :], ident[:, :])
            mm.then_inc(xt_mm, 1)
        for g in range(GROUPS):
            mean_of(g, x1, g, xt_evac, g + 1)
            if g:
                var_of(g - 1, g - 1)
        var_of(GROUPS - 1, GROUPS - 1)
        pe.wait_ge(w_dma, W_ALL)
        for n, (c, g) in enumerate(JOBS):
            dst = bank[2 + n % 4][:, :]
            pe.wait_ge(norm_done, g + 1)
            if n >= 4:
                pe.wait_ge(proj_evac, n - 3)
            else:
                pe.wait_ge(xt_evac, GROUPS)
            if c == CONV:
                pe.wait_ge(diag_done, 1)
                for k in range(D_CONV):
                    mm = nc.tensor.matmul(dst, diag[:, k, :], raw[:, 2, 2 * g:2 * g + 2, k:k + SEQ], start=(k == 0),
                                          stop=(k == D_CONV - 1))
            else:
                mm = nc.tensor.matmul(dst, win[:, c * P:(c + 1) * P], xn[:, tok(g)], start=True, stop=True)
            mm.then_inc(proj_mm, 1)
        for t in range(NT):
            mm = nc.tensor.matmul(bank[6][:, NHEADS * t:NHEADS * (t + 1)], xn[:, t * P:(t + 1) * P],
                                  win[:, PROJ - NHEADS:PROJ], start=True, stop=True)
        mm.then_inc(dt_mm, 1)
        pe.wait_ge(sp_step, DT_STEPS)
        nc.tensor.matmul(bank[7][:, 0:HB], tri[:, 0:P], sp[:, DA, :], start=True, stop=True).then_inc(cs_mm, 1)

        pe.wait_ge(sp_step, SPLIT_STEPS)

        def rows(b):
            for h in range(NHEADS):
                c0, c1 = (2 * b) * NHEADS + h, (2 * b + 1) * NHEADS + h
                dst = bank[h]
                if b:
                    pe.wait_ge(diff_done, 2 * (b - 1) + h + 1)
                else:
                    pe.wait_ge(log_done, GROUPS)
                for n in range(2):
                    nc.tensor.matmul(dst[:, 0:2 * P], da_r[:, n, c0:c0 + 1].to_broadcast([P, P]), tri_r[:, P:3 * P],
                                     start=(n == 0), stop=True, skip_group_check=True)
                for n in range(2):
                    mm = nc.tensor.matmul(dst[:, P:3 * P], da_r[:, n, c1:c1 + 1].to_broadcast([P, P]),
                                          tri_r[:, 0:2 * P], start=False, stop=True, skip_group_check=True)
                mm.then_inc(row_mm, 1)

        def scores(b):
            if b:
                pe.wait_ge(g_done, b)
            else:
                pe.wait_ge(c_moved, 16 * GROUPS)
                pe.wait_ge(proj_evac, len(JOBS))
            nc.tensor.matmul(bank[2][:, 0:2 * P], cv[0:D_STATE, 2, b, 0:P], c_low[:, b, :], start=True, stop=True)
            nc.tensor.matmul(bank[2][:, 2 * P:3 * P], cv[0:D_STATE, 2, b, P:2 * P], c_low[:, b, P:2 * P],
                             start=True, stop=True).then_inc(g_mm, 1)

        def to_nat(b):
            if b:
                pe.wait_ge(xnat_evac, b)
            else:
                pe.wait_ge(silu_done, 2 * GROUPS)
            for h in range(NHEADS):
                for t in range(TILES):
                    mm = nc.tensor.transpose(bank[3][:, (2 * h + t) * P:(2 * h + t + 1) * P],
                                             cv[:, h, b, t * P:(t + 1) * P], ident[:, :])
            mm.then_inc(xnat_mm, 1)

        def ys(b):
            pe.wait_ge(xnat_evac, b + 1)
            if b:
                pe.wait_ge(y_skip, 2 * b)
            for h in range(NHEADS):
                pe.wait_ge(s_done, 2 * b + h + 1)
                dst = bank[4][:, h * SEQ:(h + 1) * SEQ]
                nc.tensor.matmul(dst, xnat[:, b % 2, 2 * h, :], st[:, b % 2, h, 0:SEQ], start=True, stop=True,
                                 skip_group_check=True)
                mm = nc.tensor.matmul(dst[:, P:SEQ], xnat[:, b % 2, 2 * h + 1, :], st[:, b % 2, h, SEQ:SEQ + P],
                                      start=False, stop=True, skip_group_check=True)
            mm.then_inc(y_mm, 1)

        def outs(b):
            pe.wait_ge(y_done, b + 1)
            if b:
                pe.wait_ge(o_evac, b)
            else:
                pe.wait_ge(sp_step, CS_STEPS)
            for h in range(NHEADS):
                mm = nc.tensor.matmul(bank[6][:, seq(b % 2)], wout[:, h, :], yy[:, b % 2, h, :], start=(h == 0),
                                      stop=(h == NHEADS - 1), skip_group_check=True)
            mm.then_inc(o_mm, 1)

        def seq_centre(k, b):
            pe.wait_ge((o_evac, x1_done)[k], b + 1)
            if b:
                pe.wait_ge((x1_done, xs_done)[k], b)
            else:
                pe.wait_ge(tables_done, 1)
            src = (yo(xin), x1)[k]
            nc.tensor.matmul(norm_bank[k][:, 0:SEQ], first["centre"][:, :], src[:, seq(b)], start=True, stop=True,
                             skip_group_check=True).then_inc(seq_centred[k], 1)

        def seq_variance(k, b):
            pe.wait_ge(seq_squared[k], b + 1)
            nc.tensor.matmul(norm_bank[k][:, SEQ:2 * SEQ], ones_mean[:, :], seq_square(k, b), start=True, stop=True,
                             skip_group_check=True).then_inc(seq_var[k], 1)

        for b in range(BATCH + 4):
            if b < BATCH:
                rows(b)
                scores(b)
            if 1 <= b <= BATCH:
                ys(b - 1)
            if b < BATCH:
                to_nat(b)
            if 3 <= b < BATCH + 3:
                seq_centre(0, b - 3)
            if b >= 4:
                seq_centre(1, b - 4)
            if 2 <= b < BATCH + 2:
                outs(b - 2)
            if 3 <= b < BATCH + 3:
                seq_variance(0, b - 3)
            if b >= 4:
                seq_variance(1, b - 4)

    @block.scalar
    def _(act):
        load_ln_exp(nc, act)
        for g in range(GROUPS):
            act.wait_ge(xt_mm, g + 1)
            nc.scalar.copy(x1[:, tok(g)], bank[2 + g % 2][:, :]).then_inc(xt_evac, 1)

        def square(g):
            act.wait_ge(centred, g + 1)
            nc.scalar.activation(sq[:, tok(g)], xc[:, tok(g)], ACT.Square).then_inc(squared, 1)

        def root(g):
            act.wait_ge(var_mm, g + 1)
            nc.scalar.activation(rstd[:, tok(g)], bank[g % 2][:, :], ACT.Ln, bias=eps_col[:, 0:1]).then_inc(log_done, 1)
            act.wait_ge(log_done, g + 1)
            nc.scalar.activation(rstd[:, tok(g)], rstd[:, tok(g)], ACT.Exp, scale=-0.5).then_inc(rstd_done, 1)

        for g in range(GROUPS):
            square(g)
            if g:
                root(g - 1)
        root(GROUPS - 1)
        for n, (c, g) in enumerate(JOBS):
            act.wait_ge(proj_mm, n + 1)
            src = bank[2 + n % 4][:, :]
            if c == CONV:
                nc.scalar.activation(cv[:, 2, 2 * g:2 * g + 2, :], src.rearrange("p (b s) -> p b s", b=2), ACT.Silu,
                                     bias=convw[:, 2, D_CONV:D_CONV + 1]).then_inc(proj_evac, 1)
            elif c < 2:
                act.wait_ge(tables_done, 1)
                nc.scalar.activation(zs[:, c, tok(g)], src, ACT.Silu).then_inc(proj_evac, 1)
            else:
                nc.scalar.copy(raw[:, c - 2, 2 * g:2 * g + 2, 3:], src.rearrange("p (b s) -> p b s", b=2))\
                    .then_inc(proj_evac, 1)
        for c in range(2):
            for g in range(GROUPS):
                act.wait_ge(conv_done, GROUPS * c + g + 1)
                dst = cv[:, c, 2 * g:2 * g + 2, :]
                nc.scalar.activation(dst, dst, ACT.Silu).then_inc(silu_done, 1)
        load_ln_exp(nc, act)
        act.wait_ge(w_dma, W_ALL)
        act.wait_ge(sp_step, 3)
        nc.scalar.activation(sp[:, E, :], sp[:, NEG, :], ACT.Exp).then_inc(sp_act, 1)
        nc.scalar.activation(heads[:, 3, :], heads[:, 0, :], ACT.Exp).then_inc(sp_act, 1)
        act.wait_ge(sp_step, 4)
        nc.scalar.activation(sp[:, L, :], sp[:, U, :], ACT.Ln).then_inc(sp_act, 1)

        def decays(b):
            act.wait_ge(xnat_mm, b + 1)
            if b >= 2:
                act.wait_ge(y_mm, b - 1)
            nc.scalar.copy(xnat[:, b % 2, :, :], bank[3][:, :].rearrange("p (k d) -> p k d", k=4)).then_inc(xnat_evac, 1)
            for h in range(NHEADS):
                act.wait_ge(diff_done, 2 * b + h + 1)
                nc.scalar.activation(dec[:, b % 2, h, :], dec[:, b % 2, h, :], ACT.Exp).then_inc(dec_done, 1)

        def seq_squares(k, b):
            act.wait_ge(seq_centred[k], b + 1)
            nc.scalar.activation(seq_square(k, b), norm_bank[k][:, 0:SEQ], ACT.Square).then_inc(seq_squared[k], 1)

        def seq_root(k, b):
            act.wait_ge(seq_var[k], b + 1)
            r = seq_scale(k, b)
            nc.scalar.activation(r, norm_bank[k][:, SEQ:2 * SEQ], ACT.Ln, bias=eps_col[:, 0:1]).then_inc(seq_log[k], 1)
            act.wait_ge(seq_log[k], b + 1)
            nc.scalar.activation(r, r, ACT.Exp, scale=-0.5).then_inc(seq_rstd[k], 1)

        for b in range(BATCH + 4):
            if b < BATCH:
                decays(b)
            if 3 <= b < BATCH + 3:
                seq_squares(0, b - 3)
            if b >= 4:
                seq_squares(1, b - 4)
            if 2 <= b < BATCH + 2:
                act.wait_ge(o_mm, b - 1)
                nc.scalar.copy(yo(xin)[:, seq(b - 2)], bank[6][:, seq(b % 2)]).then_inc(o_evac, 1)
            if 3 <= b < BATCH + 3:
                seq_root(0, b - 3)
            if b >= 4:
                seq_root(1, b - 4)

    @block.vector
    def _(dve):
        def centre(g):
            dve.wait_ge(mean_mm, g + 1)
            nc.vector.tensor_tensor(xc[:, tok(g)], x1[:, tok(g)], bank[g % 2][:, :], ALU.subtract).then_inc(centred, 1)

        centre(0)
        centre(1)
        for g in range(GROUPS):
            dve.wait_ge(rstd_done, g + 1)
            nc.vector.tensor_tensor(xn[:, tok(g)], xc[:, tok(g)], rstd[:, tok(g)], ALU.mult).then_inc(norm_done, 1)
            if g + 2 < GROUPS:
                centre(g + 2)
        dve.wait_ge(w_dma, W_ALL)
        for k in range(D_CONV):
            ins = nc.vector.tensor_scalar(diag[:, k, :], ident[:, :], convw[:, 2, k:k + 1], None, ALU.mult)
        ins.then_inc(diag_done, 1)
        dve.wait_ge(scale_dma, 16 * 7)
        base = stage[:, 0:TILES * 4 * DH].rearrange("p (t k d) -> p t k d", t=TILES, k=4)
        for t in range(TILES):
            for kind in range(4):
                nc.vector.tensor_tensor(first["tab"][:, :, t, kind, :], scale_rows(kind // 2)[:, kind % 2],
                                        base[:, t, kind, :].unsqueeze(1).broadcast_to([P, DEPTH, DH]), ALU.mult)
        dve.wait_ge(ident_dma, 16)
        nc.vector.tensor_tensor(first["centre"][:, :], ident[:, :], ones_mean[:, :], ALU.subtract).then_inc(tables_done, 1)
        dve.wait_ge(setup, 4)
        taps = 0
        for c in range(2):
            for g0 in (0, 2):
                for k in range(D_CONV):
                    for g in (g0, g0 + 1):
                        b0 = 2 * g
                        dst = cv[:, c, b0:b0 + 2, :]
                        if k == 0:
                            dve.wait_ge(proj_evac, GROUPS * (c + 1) + g + 1)
                            ins = nc.vector.tensor_scalar(dst, raw[:, c, b0:b0 + 2, 0:SEQ], convw[:, c, 0:1],
                                                          convw[:, c, D_CONV:D_CONV + 1], ALU.mult, ALU.add)
                        else:
                            dve.wait_ge(tap, taps if k == D_CONV - 1 and g > g0 else taps - 1)
                            ins = nc.vector.scalar_tensor_tensor(out=dst, in0=raw[:, c, b0:b0 + 2, k:k + SEQ],
                                                                 scalar=convw[:, c, k:k + 1], in1=dst, op0=ALU.mult,
                                                                 op1=ALU.add)
                        if k < D_CONV - 1:
                            taps += 1
                        ins.then_inc(tap if k < D_CONV - 1 else conv_done, 1)
        steps = [0]

        def step(ins):
            steps[0] += 1
            ins.then_inc(sp_step, 1)
            dve.wait_ge(sp_step, steps[0])

        def bc(row):
            return heads[:, row, :].unsqueeze(1).broadcast_to([P, HB // NHEADS, NHEADS])

        def v3(row):
            return sp[:, row, :].rearrange("p (n h) -> p n h", h=NHEADS)

        dve.wait_ge(dt_mm, 1)
        step(nc.vector.tensor_tensor(v3(R), bank[6][:, 0:HB].rearrange("p (n h) -> p n h", h=NHEADS), bc(1), ALU.add))
        step(nc.vector.tensor_scalar(sp[:, TMP, :], sp[:, R, :], -1.0, None, ALU.mult))
        step(nc.vector.tensor_tensor(sp[:, NEG, :], sp[:, R, :], sp[:, TMP, :], ALU.min))
        dve.wait_ge(sp_act, 1)
        step(nc.vector.tensor_scalar(sp[:, U, :], sp[:, E, :], 1.0, None, ALU.add))
        step(nc.vector.tensor_scalar(sp[:, V, :], sp[:, U, :], -1.0, None, ALU.add))
        step(nc.vector.tensor_scalar(sp[:, M, :], sp[:, V, :], 0.0, None, ALU.is_equal))
        step(nc.vector.tensor_tensor(sp[:, V, :], sp[:, V, :], sp[:, M, :], ALU.add))
        step(nc.vector.reciprocal(sp[:, TMP, :], sp[:, V, :]))
        dve.wait_ge(sp_act, 3)
        step(nc.vector.tensor_tensor(sp[:, L, :], sp[:, L, :], sp[:, M, :], ALU.add))
        step(nc.vector.tensor_tensor(sp[:, L, :], sp[:, L, :], sp[:, TMP, :], ALU.mult))
        step(nc.vector.tensor_tensor(sp[:, L, :], sp[:, L, :], sp[:, E, :], ALU.mult))
        step(nc.vector.scalar_tensor_tensor(out=sp[:, DT, :], in0=sp[:, R, :], scalar=0.0, in1=sp[:, L, :],
                                            op0=ALU.max, op1=ALU.add))
        step(nc.vector.scalar_tensor_tensor(out=v3(DA), in0=v3(DT), scalar=-1.0, in1=bc(3), op0=ALU.mult, op1=ALU.mult))
        assert steps[0] == DT_STEPS
        nc.vector.tensor_copy(tri_r[:, 0:P], tri[:, 0:P])
        nc.vector.tensor_copy(tri_r[:, P:2 * P], tri[:, 0:P])
        nc.vector.tensor_copy(tri_r[:, 2 * P:3 * P], tri[:, P:2 * P])
        step(nc.vector.tensor_copy(da_r[:, 0, :], sp[:, DA, :]))
        step(nc.vector.tensor_tensor(da_r[:, 1, :], sp[:, DA, :], da_r[:, 0, :].bitcast(F32), ALU.subtract))
        assert steps[0] == SPLIT_STEPS
        dve.wait_ge(cs_mm, 1)
        step(nc.vector.tensor_copy(sp[:, CS, :], bank[7][:, 0:HB]))
        assert steps[0] == CS_STEPS

        def decay(b):
            for h in range(NHEADS):
                dve.wait_ge(row_mm, 2 * b + h + 1)
                if b >= 2:
                    dve.wait_ge(s_done, 2 * (b - 2) + h + 1)
                c0, c1 = (2 * b) * NHEADS + h, (2 * b + 1) * NHEADS + h
                nc.vector.tensor_scalar(dec[:, b % 2, h, 0:SEQ], bank[h][:, 0:SEQ], sp[:, CS, c0:c0 + 1], 0.0,
                                        ALU.subtract, ALU.min)
                nc.vector.tensor_scalar(dec[:, b % 2, h, SEQ:], bank[h][:, SEQ:3 * P], sp[:, CS, c1:c1 + 1], 0.0,
                                        ALU.subtract, ALU.min).then_inc(diff_done, 1)

        def masked(b):
            dve.wait_ge(g_mm, b + 1)
            if b >= 2:
                dve.wait_ge(s_done, 2 * (b - 2) + 2)
            nc.vector.tensor_tensor(gm[:, b % 2, :], bank[2][:, 0:3 * P], tri[:, :], ALU.mult).then_inc(g_done, 1)

        def weights(b):
            dve.wait_ge(g_done, b + 1)
            for h in range(NHEADS):
                dve.wait_ge(dec_done, 2 * b + h + 1)
                if b >= 2:
                    dve.wait_ge(y_mm, b - 1)
                c0, c1 = (2 * b) * NHEADS + h, (2 * b + 1) * NHEADS + h
                for lo, hi, c in ((0, SEQ, c0), (SEQ, 3 * P, c1)):
                    ins = nc.vector.scalar_tensor_tensor(out=st[:, b % 2, h, lo:hi], in0=dec[:, b % 2, h, lo:hi],
                                                         scalar=sp[:, DT, c:c + 1], in1=gm[:, b % 2, lo:hi],
                                                         op0=ALU.mult, op1=ALU.mult)
                ins.then_inc(s_done, 1)

        def gate(b):
            dve.wait_ge(y_mm, b + 1)
            if b >= 2:
                dve.wait_ge(o_mm, b - 1)
            for h in range(NHEADS):
                nc.vector.scalar_tensor_tensor(out=yy[:, b % 2, h, :], in0=cv[:, h, b, :], scalar=heads[:, 2, h:h + 1],
                                               in1=bank[4][:, h * SEQ:(h + 1) * SEQ], op0=ALU.mult,
                                               op1=ALU.add).then_inc(y_skip, 1)
            dve.wait_ge(y_skip, 2 * b + 2)
            nc.vector.tensor_tensor(yy[:, b % 2, :, :], yy[:, b % 2, :, :], zs[:, :, b * SEQ:(b + 1) * SEQ],
                                    ALU.mult).then_inc(y_done, 1)

        def write_x1(b):
            dve.wait_ge(seq_rstd[0], b + 1)
            nc.vector.tensor_tensor(xn[:, seq(b)], norm_bank[0][:, 0:SEQ], seq_scale(0, b), ALU.mult).then_inc(x1_scaled, 1)
            dve.wait_ge(x1_scaled, b + 1)
            nc.vector.tensor_tensor(x1[:, seq(b)], x1[:, seq(b)], xn[:, seq(b)], ALU.add).then_inc(x1_done, 1)

        def write_xs(b):
            dve.wait_ge(seq_rstd[1], b + 1)
            for half in range(2):
                rows = slice(DH * half, DH * half + DH)
                ins = nc.vector.tensor_tensor(xs[rows, b, half:half + SEQ], norm_bank[1][rows, 0:SEQ],
                                              seq_scale(1, b)[rows], ALU.mult)
            ins.then_inc(xs_done, 1)

        dve.wait_ge(silu_done, 2 * GROUPS)
        for b in range(BATCH + 4):
            if b < BATCH:
                decay(b)
                masked(b)
            if 1 <= b <= BATCH:
                gate(b - 1)
            if b < BATCH:
                weights(b)
            if 3 <= b < BATCH + 3:
                write_x1(b - 3)
            if b >= 4:
                write_xs(b - 4)


def build_layers(nc, ctx, sb, sem, bank, ident, ones_mean, eps_col, xs, first, loaded, w_qk, w_v, w_o, w_1, w_2):
    wh = sb(ctx, "wh", [P, 2, QK_COLS], F32R)
    wl = sb(ctx, "wl", [P, 2, QK_COLS], F32R)
    wraw = sb(ctx, "wraw", [P, SPLIT])
    wv, wo, w1, w2, cols, tab = (first[name] for name in ("wv", "wo", "w1", "w2", "cols", "tab"))
    centre, mask = first["centre"], first["mask"]
    xh = sb(ctx, "xh", [P, SEQ], F32R)
    xl = sb(ctx, "xl", [P, SEQ], F32R)
    xf = sb(ctx, "xf", [P, SEQ])
    qk = [first["qk0"], sb(ctx, "qk1", [P, QK_COLS])]
    rot = sb(ctx, "rot", [P, QK_COLS])
    sqr = sb(ctx, "sqr", [P, 2, 512])
    ss = [sb(ctx, f"ss{t}", [P, 2 * HEADS]) for t in range(TILES)]
    rn = [sb(ctx, f"rn{t}", [P, 2 * HEADS]) for t in range(TILES)]
    qT = [sb(ctx, f"qT{t}", [P, PAIRS, P]) for t in range(TILES)]
    kbd = sb(ctx, "kbd", [P, PAIRS, 2, WIN + SEQ])
    v_odd = sb(ctx, "v_odd", [P, SEQ // (2 * WIN), 2, PAIRS, VW])
    v_even = sb(ctx, "v_even", [P, SEQ // (2 * WIN), 2, PAIRS, VW])
    pr = [sb(ctx, f"pr{t}", [P, PAIRS, 2, 2 * WIN]) for t in range(TILES)]
    mx = sb(ctx, "mx", [P, 2, PAIRS])
    pT = sb(ctx, "pT", [P, PAIRS, P])
    rs = sb(ctx, "rs", [P, 2, 6])
    o = sb(ctx, "o", [P, PAIRS, 2, DH])
    oT = sb(ctx, "oT", [P, PAIRS, SEQ])
    fx = sb(ctx, "fx", [P, SEQ])
    fq = sb(ctx, "fq", [P, SEQ])
    fr = sb(ctx, "fr", [P, SEQ])
    gp = sb(ctx, "gp", [P, HC, SEQ])
    ap = sb(ctx, "ap", [P, HC, SEQ])

    proj_bank, sc_bank, tr_bank, pv_bank, f_bank = bank[0:2], bank[2:4], bank[4:6], bank[6], bank[7]

    zeroed = sem(ctx, "zeroed")
    consts_done = sem(ctx, "consts_done")
    raw_dma = sem(ctx, "raw_dma")
    split_hi = sem(ctx, "split_hi")
    split_done = sem(ctx, "split_done")
    first_dma, wv_dma, wo_dma, w1_dma, w2_dma = (loaded[name] for name in ("first", "wv", "wo", "w1", "w2"))
    x_hi = sem(ctx, "x_hi")
    x_staged = sem(ctx, "x_staged")
    proj_mm = sem(ctx, "proj_mm")
    squared = sem(ctx, "squared")
    roped = sem(ctx, "roped")
    sums_done = sem(ctx, "sums_done")
    floored = sem(ctx, "floored")
    rn_log = sem(ctx, "rn_log")
    rn_done = sem(ctx, "rn_done")
    rope_added = sem(ctx, "rope_added")
    qk_done = sem(ctx, "qk_done")
    tr_mm = sem(ctx, "tr_mm")
    tr_evac = sem(ctx, "tr_evac")
    sc_mm = sem(ctx, "sc_mm")
    max_done = sem(ctx, "max_done")
    sc_evac = sem(ctx, "sc_evac")
    subtracted = sem(ctx, "subtracted")
    exp_done = sem(ctx, "exp_done")
    v_evac = sem(ctx, "v_evac")
    ve_dma = sem(ctx, "ve_dma")
    pv_mm = sem(ctx, "pv_mm")
    recip_done = sem(ctx, "recip_done")
    pv_evac = sem(ctx, "pv_evac")
    f_mm = sem(ctx, "f_mm")
    res1 = sem(ctx, "res1")
    f_squared = sem(ctx, "f_squared")
    f_log = sem(ctx, "f_log")
    f_rstd = sem(ctx, "f_rstd")
    f_scaled = sem(ctx, "f_scaled")
    f_norm = sem(ctx, "f_norm")
    h_evac = sem(ctx, "h_evac")
    gelu_done = sem(ctx, "gelu_done")
    h_done = sem(ctx, "h_done")
    state_ready = sem(ctx, "state_ready")

    ZEROED = 9
    TR = {step: n for n, step in enumerate((
        ("qk", 0, 0), ("qk", 0, 1), ("qk", 0, 2), ("qk", 0, 3),
        ("qk", 1, 0), ("qk", 1, 1), ("qk", 1, 2), ("qk", 1, 3),
        ("p", 0, 0), ("p", 0, 1), ("p", 1, 0), ("p", 1, 1),
        ("o", 0, 0), ("o", 0, 1), ("o", 1, 0), ("o", 1, 1),
    ))}

    def over_units(eng, body):
        for it in (-1, 0, 1):
            body(it)
        with eng.Fori(0, (UNITS - 4) // UNROLL) as k:
            for step in range(UNROLL):
                body(UNROLL * k + 2 + step)
        for it in (UNITS - 2, UNITS - 1, UNITS):
            body(it)

    def has(it, lag):
        return not isinstance(it, int) or 0 <= it + lag < UNITS

    block = ctx.enter_context(nc.Block())

    @block.sync
    def _(sync):
        def ahead(value):
            if not isinstance(value, int):
                sync.to_reg(value)
            return value

        def unit_loads(v):
            part, dram_layer = v % BATCH, (v // BATCH + 1) % DEPTH
            src = w_qk[bass.ds(dram_layer, 1), :, bass.ds(part * SPLIT, SPLIT)].rearrange("l p n -> (l p) n")
            projected, split_before = ahead(N_PROJ * v), ahead(v + 1)
            ahead((dram_layer * (DIM * QK_COLS) + part * SPLIT) * 4)
            if started(v):
                sync.wait_ge(proj_mm, projected)
            sync.wait_ge(split_done, split_before)
            sync.dma_start(wraw[:, :], src).then_inc(raw_dma, 16)

        def value_weights(layer):
            sync.dma_start(wv[:, :], w_v[bass.ds(layer, 1)].rearrange("l p n -> (l p) n")).then_inc(wv_dma, 16)

        def even_values(v):
            written = ahead(4 * v + 4)
            sync.wait_ge(v_evac, written)
            for half in range(2):
                for odd in range(2):
                    r = slice(64 * half + 32 * odd, 64 * half + 32 * odd + 32)
                    n = SEQ // (2 * WIN) - odd
                    sync.dma_start(v_even[r, odd:odd + n, half, :, :], v_odd[r, 0:n, half, :, :]).then_inc(ve_dma, 16)

        def reload(layer):
            last = N_F * (BATCH * layer - 1)
            at = bass.ds(layer, 1)
            src_o = w_o[at].rearrange("l p (n d) -> (l p) n d", n=PAIRS)
            src_1 = w_1[at].rearrange("l p n -> (l p) n")
            src_2 = w_2[at].rearrange("l p (n d) -> (l p) n d", n=HC)
            counts = [ahead(last + k) for k in (1, 6, 7)]
            for size in (INNER * DIM, DIM * 2 * DIM_INNER, HC * P * DIM):
                ahead(layer * size * 4)
            sync.wait_ge(f_mm, counts[0])
            sync.dma_start(wo[:, :, :], src_o).then_inc(wo_dma, 16)
            sync.wait_ge(f_mm, counts[1])
            sync.dma_start(w1[:, :], src_1).then_inc(w1_dma, 16)
            sync.wait_ge(f_mm, counts[2])
            sync.dma_start(w2[:, :, :], src_2).then_inc(w2_dma, 16)

        unit_loads(0)
        sync.wait_ge(zeroed, ZEROED)
        even_values(0)
        unit_loads(1)
        even_values(1)
        with sync.Fori(0, DEPTH - 1) as layer:
            with sync.Fori(2, BATCH) as part:
                unit_loads(layer * BATCH + part)
                even_values(layer * BATCH + part)
            unit_loads(layer * BATCH + BATCH)
            value_weights(layer + 1)
            even_values(layer * BATCH + BATCH)
            unit_loads(layer * BATCH + BATCH + 1)
            reload(layer + 1)
            even_values(layer * BATCH + BATCH + 1)
        with sync.Fori(UNITS - BATCH + 2, UNITS) as v:
            unit_loads(v)
            even_values(v)

    @block.gpsimd
    def _(pool):
        for buffer in (v_odd, v_even):
            nc.gpsimd.memset(buffer[:, :, :, :, :], 0.0).then_inc(zeroed, 1)
        nc.gpsimd.memset(kbd[:, :, :, :], 0.0).then_inc(zeroed, 1)
        nc.gpsimd.memset(gp[:, :, :], 0.0).then_inc(zeroed, 1)
        nc.gpsimd.memset(ap[:, :, :], 0.0).then_inc(zeroed, 1)
        pool.wait_ge(zeroed, 5)
        for half in range(2):
            r = slice(64 * half, 64 * half + 64)
            for v in (v_odd, v_even):
                nc.gpsimd.memset(v[r, :, half, :, DH:VW], 1.0).then_inc(zeroed, 1)

        pool.wait_ge(zeroed, ZEROED)

        def rope_add(v, t, half):
            n = 2 * v + t
            r = slice(half * INNER, (half + 1) * INNER)
            pool.wait_ge(roped, 4 * n + 2 * half + 2)
            nc.gpsimd.tensor_tensor(qk[t][:, r], qk[t][:, r], rot[:, r], ALU.add).then_inc(rope_added, 1)

        def rope_norm(v, t, half):
            n = 2 * v + t
            pool.wait_ge(rn_done, n + 1)
            pool.wait_ge(rope_added, 2 * n + half + 1)
            h = qk[t][:, half * INNER:(half + 1) * INNER].rearrange("p (h d) -> p h d", d=DH)
            w = rn[t][:, half * HEADS:(half + 1) * HEADS].unsqueeze(2).broadcast_to([P, HEADS, DH])
            nc.gpsimd.tensor_tensor(h, h, w, ALU.mult).then_inc(qk_done, 1)

        def softmax_subtract(u, t, n):
            pool.wait_ge(max_done, 4 * u + 2 * t + n + 1)
            v = pr[t][:, 4 * n:4 * n + 4, :, :].rearrange("p k b c -> p (k b) c")
            nc.gpsimd.tensor_tensor(v, v, mx[:, n, :].unsqueeze(2).broadcast_to([P, 8, 2 * WIN]), ALU.subtract)\
                .then_inc(subtracted, 1)

        def hidden(u):
            pool.wait_ge(gelu_done, u + 1)
            nc.gpsimd.tensor_tensor(gp[:, :, :], gp[:, :, :], ap[:, :, :], ALU.mult).then_inc(h_done, 1)

        def body(it):
            proj, attn, ffn = has(it, 1), has(it, 0), has(it, -1)
            if attn:
                softmax_subtract(it, 0, 0)
                softmax_subtract(it, 0, 1)
            if proj:
                rope_add(it + 1, 0, 0)
            if attn:
                softmax_subtract(it, 1, 0)
                softmax_subtract(it, 1, 1)
            if proj:
                rope_add(it + 1, 0, 1)
            if ffn:
                hidden(it - 1)
            if proj:
                rope_norm(it + 1, 0, 0)
                rope_norm(it + 1, 0, 1)
                rope_add(it + 1, 1, 0)
                rope_norm(it + 1, 1, 0)
                rope_add(it + 1, 1, 1)
                rope_norm(it + 1, 1, 1)

        over_units(pool, body)

    @block.tensor
    def _(pe):

        def project_qk(v, n):
            layer = v // BATCH
            par = layer % 2
            t, c = n // 4, n % 4
            if n == 0:
                pe.wait_ge(x_staged, v + 1)
                pe.wait_ge(split_done, BATCH * layer + 1)
            if n >= 2:
                pe.wait_ge(roped, 8 * v + n - 1)
            elif started(v):
                pe.wait_ge(v_evac, 4 * v - 1 + n)
            dst = proj_bank[n % 2][:, :]
            tile = slice(t * P, (t + 1) * P)
            w_hi, w_lo = (w[:, bass.ds(par, 1), c * 512:(c + 1) * 512].rearrange("p l n -> p (l n)") for w in (wh, wl))
            nc.tensor.matmul(dst, xh[:, tile], w_hi, start=True, stop=False)
            nc.tensor.matmul(dst, xh[:, tile], w_lo, start=False, stop=False)
            nc.tensor.matmul(dst, xl[:, tile], w_hi, start=False, stop=True).then_inc(proj_mm, 1)
            if n == 0 and not isinstance(v, int):
                for later in (1, 2, 3):
                    pe.to_reg((par * QK_COLS + later * 512) * 4)

        def project_v(v, slot):
            layer = v // BATCH
            n = 8 + slot
            if slot == 0:
                pe.wait_ge(wv_dma, 16 * (layer + 1))
            if slot < 2:
                pe.wait_ge(roped, 8 * v + n - 1)
            else:
                pe.wait_ge(v_evac, 4 * v + slot - 1)
            for half in range(2):
                for odd in range(2):
                    r = 64 * half + 32 * odd
                    w = WIN * (2 * slot + odd)
                    mm = nc.tensor.matmul(proj_bank[n % 2][r:r + 32, :], xf[:, w:w + WIN],
                                          wv[:, half * 512:(half + 1) * 512], start=True, stop=True)
            mm.then_inc(proj_mm, 1)

        def transpose4(u, n, blocks):
            if not isinstance(u, int) or N_TR * u + n > 1:
                pe.wait_ge(tr_evac, N_TR * u + n - 1)
            for m in range(4):
                mm = nc.tensor.transpose(tr_bank[n % 2][:, m * P:(m + 1) * P], blocks(m), ident[:, :])
            mm.then_inc(tr_mm, 1)

        def transpose_qk(u, t, c):
            pe.wait_ge(qk_done, 4 * u + 2 * t + c // 2 + 1)
            transpose4(u, TR["qk", t, c], lambda m: qk[t][:, (4 * c + m) * P:(4 * c + m + 1) * P])

        def score(u, t, n):
            last = 4 * u + 2 * t + n - 1
            if started(last):
                pe.wait_ge(sc_evac, last)
            if isinstance(last, int) and last < 0:
                pe.wait_ge(zeroed, ZEROED)
            pe.wait_ge(tr_evac, N_TR * u + 1 + max(TR["qk", t, n], *(TR["qk", k, 2 + n] for k in range(t + 1))))
            dst = sc_bank[n]
            for m in range(4):
                for j in range(4):
                    w = 4 * t + j
                    keys = kbd[:, 4 * n + m, :, WIN * w:WIN * w + 2 * WIN]
                    if w % 2 == 0:
                        keys = keys.rearrange("p b (k c) -> p b k c", k=2)[:, :, ::-1, :]
                    mm = nc.tensor.matmul(dst[32 * j:32 * j + 32, m * P:(m + 1) * P],
                                          qT[t][:, 4 * n + m, WIN * j:WIN * j + WIN], keys,
                                          start=True, stop=True, skip_group_check=True)
            mm.then_inc(sc_mm, 1)

        def transpose_p(u, t, m):
            pe.wait_ge(exp_done, 4 * u + 2 * t + m + 1)
            transpose4(u, TR["p", t, m], lambda k: pr[t][:, 4 * m + k, :, :].rearrange("p b c -> p (b c)"))

        def attend(u, t, c):
            last = N_PV * u + 3 * t + c
            if started(last):
                pe.wait_ge(pv_evac, last)
            lo, hi = PV_CHUNKS[c]
            if c == 0:
                pe.wait_ge(tr_evac, N_TR * u + TR["p", t, 1] + 1)
                if t == 0:
                    pe.wait_ge(ve_dma, 64 * (u + 1))
                    pe.wait_ge(v_evac, 4 * u + 4)
            for k in range(lo, hi):
                for j in range(4):
                    v = v_odd if j % 2 else v_even
                    mm = nc.tensor.matmul(pv_bank[32 * j:32 * j + 32, (k - lo) * 2 * VW:(k - lo + 1) * 2 * VW],
                                          pT[:, k, WIN * j:WIN * j + WIN], v[:, 2 * t + j // 2, :, k, :],
                                          start=True, stop=True, skip_group_check=True)
            mm.then_inc(pv_mm, 1)

        def transpose_o(u, t, m):
            pe.wait_ge(pv_evac, N_PV * u + 3 * t + 2 + m)
            transpose4(u, TR["o", t, m], lambda k: o[:, 4 * m + k, :, :].rearrange("p b d -> p (b d)"))

        def out_proj(u):
            pe.wait_ge(wo_dma, 16 * (u // BATCH + 1))
            pe.wait_ge(tr_evac, N_TR * u + TR["o", 1, 1] + 1)
            if started(u):
                pe.wait_ge(state_ready, BATCH + u)
            for k in range(PAIRS):
                mm = nc.tensor.matmul(f_bank[:, 0:SEQ], wo[:, k, :], oT[:, k, :], start=(k == 0), stop=(k == PAIRS - 1))
            mm.then_inc(f_mm, 1)

        def norm_centre(u):
            pe.wait_ge(res1, u + 1)
            nc.tensor.matmul(f_bank[:, 0:SEQ], centre[:, :], xs[:, bass.ds(u % BATCH, 1), 0:SEQ].rearrange("p b s -> p (b s)"),
                             start=True, stop=True, skip_group_check=True).then_inc(f_mm, 1)

        def norm_var(u):
            pe.wait_ge(f_squared, u + 1)
            nc.tensor.matmul(f_bank[:, SEQ:2 * SEQ], ones_mean[:, :], fq[:, :], start=True, stop=True,
                             skip_group_check=True).then_inc(f_mm, 1)

        def ffn_in(u, c):
            rows = P if c < HC - 1 else HLAST
            if c == 0:
                pe.wait_ge(w1_dma, 16 * (u // BATCH + 1))
                pe.wait_ge(f_norm, u + 1)
            else:
                pe.wait_ge(h_evac, HC * u + c)
            nc.tensor.matmul(f_bank[0:rows, 0:SEQ], w1[:, c * P:c * P + rows], fx[:, :], start=True, stop=True,
                             skip_group_check=True)
            nc.tensor.matmul(f_bank[0:rows, SEQ:2 * SEQ], w1[:, DIM_INNER + c * P:DIM_INNER + c * P + rows], fx[:, :],
                             start=True, stop=True, skip_group_check=True).then_inc(f_mm, 1)

        def ffn_out(u):
            pe.wait_ge(w2_dma, 16 * (u // BATCH + 1))
            pe.wait_ge(h_done, u + 1)
            for c in range(HC):
                mm = nc.tensor.matmul(f_bank[:, 0:SEQ], w2[:, c, :], gp[:, c, :], start=(c == 0), stop=(c == HC - 1))
            mm.then_inc(f_mm, 1)

        def body(it):
            proj, attn, ffn = has(it, 1), has(it, 0), has(it, -1)
            if attn:
                transpose_qk(it, 0, 0)
                transpose_qk(it, 0, 1)
            if ffn:
                out_proj(it - 1)
            if attn:
                transpose_qk(it, 0, 2)
            if proj:
                project_qk(it + 1, 0)
                project_qk(it + 1, 1)
            if ffn:
                norm_centre(it - 1)
            if attn:
                transpose_qk(it, 0, 3)
                score(it, 0, 0)
            if ffn:
                norm_var(it - 1)
            if attn:
                transpose_qk(it, 1, 0)
                transpose_qk(it, 1, 1)
                score(it, 0, 1)
                transpose_qk(it, 1, 2)
                transpose_qk(it, 1, 3)
            if proj:
                project_qk(it + 1, 2)
                project_qk(it + 1, 3)
            if attn:
                score(it, 1, 0)
            if ffn:
                ffn_in(it - 1, 0)
            if attn:
                transpose_p(it, 0, 0)
                transpose_p(it, 0, 1)
                score(it, 1, 1)
                attend(it, 0, 0)
            if proj:
                project_qk(it + 1, 4)
            if ffn:
                ffn_in(it - 1, 1)
            if proj:
                project_qk(it + 1, 5)
            if attn:
                attend(it, 0, 1)
                transpose_p(it, 1, 0)
            if ffn:
                ffn_in(it - 1, 2)
            if proj:
                project_qk(it + 1, 6)
            if attn:
                attend(it, 0, 2)
                transpose_p(it, 1, 1)
            if proj:
                project_qk(it + 1, 7)
            if attn:
                transpose_o(it, 0, 0)
                attend(it, 1, 0)
                transpose_o(it, 0, 1)
            if proj:
                project_v(it + 1, 0)
            if attn:
                attend(it, 1, 1)
            if proj:
                project_v(it + 1, 1)
            if attn:
                attend(it, 1, 2)
            if proj:
                project_v(it + 1, 2)
            if attn:
                transpose_o(it, 1, 0)
            if ffn:
                ffn_out(it - 1)
            if attn:
                transpose_o(it, 1, 1)
            if proj:
                project_v(it + 1, 3)

        over_units(pe, body)

    @block.scalar
    def _(act):
        act.wait_ge(first_dma, 16 * 3)

        load_ln_exp(nc, act)

        def evac_qk(u, t, c):
            n = TR["qk", t, c]
            act.wait_ge(tr_mm, N_TR * u + n + 1)
            src = tr_bank[n % 2][:, :].rearrange("p (m s) -> p m s", m=4)
            if c < 2:
                if c == 0 and started(u):
                    act.wait_ge(sc_mm, 4 * (u - 1) + 2 * t + 2)
                nc.scalar.copy(qT[t][:, 4 * c:4 * c + 4, :], src).then_inc(tr_evac, 1)
            else:
                k0 = 4 * (c - 2)
                at = slice(WIN + t * P, WIN + (t + 1) * P)
                if c == 2 and started(u):
                    act.wait_ge(sc_mm, 4 * u)
                nc.scalar.copy(kbd[0:DH, k0:k0 + 4, 0, at], src[0:DH])
                nc.scalar.copy(kbd[DH:P, k0:k0 + 4, 1, at], src[DH:P]).then_inc(tr_evac, 1)

        def exps(u, t, n):
            act.wait_ge(subtracted, 4 * u + 2 * t + n + 1)
            v = pr[t][:, 4 * n:4 * n + 4, :, :]
            nc.scalar.activation(v, v, ACT.Exp).then_inc(exp_done, 1)

        def evac_pt(u, t, m):
            n = TR["p", t, m]
            act.wait_ge(tr_mm, N_TR * u + n + 1)
            if m == 0 and started(2 * u + t if isinstance(u, int) else u):
                act.wait_ge(pv_mm, N_PV * u + 3 * t)
            nc.scalar.copy(pT[:, 4 * m:4 * m + 4, :], tr_bank[n % 2][:, :].rearrange("p (k s) -> p k s", k=4))\
                .then_inc(tr_evac, 1)

        def evac_ot(u, t, m):
            n = TR["o", t, m]
            act.wait_ge(tr_mm, N_TR * u + n + 1)
            if m == 0 and t == 0 and started(u):
                act.wait_ge(f_mm, N_F * (u - 1) + 1)
            nc.scalar.copy(oT[:, 4 * m:4 * m + 4, t * P:(t + 1) * P],
                           tr_bank[n % 2][:, :].rearrange("p (k s) -> p k s", k=4)).then_inc(tr_evac, 1)

        def squares(v, n):
            act.wait_ge(proj_mm, N_PROJ * v + n + 1)
            if not isinstance(v, int) or 8 * v + n >= 2:
                act.wait_ge(sums_done, 8 * v + n - 1)
            nc.scalar.activation(sqr[:, n % 2, :], proj_bank[n % 2][:, :], ACT.Square).then_inc(squared, 1)

        def inverse_norms(v, t):
            n = 2 * v + t
            act.wait_ge(floored, n + 1)
            if started(v):
                act.wait_ge(qk_done, 2 * (n - 2) + 2)
            nc.scalar.activation(rn[t][:, :], ss[t][:, :], ACT.Ln).then_inc(rn_log, 1)
            act.wait_ge(rn_log, n + 1)
            nc.scalar.activation(rn[t][:, :], rn[t][:, :], ACT.Exp, scale=-0.5).then_inc(rn_done, 1)

        def evac_v(v, slot):
            act.wait_ge(proj_mm, N_PROJ * v + 8 + slot + 1)
            if isinstance(v, int) and v == 0 and slot == 0:
                act.wait_ge(zeroed, ZEROED)
            if slot == 0 and started(v):
                act.wait_ge(ve_dma, 64 * v)
                act.wait_ge(pv_mm, N_PV * (v - 1) + 3)
            if slot == 2 and started(v):
                act.wait_ge(pv_mm, N_PV * v)
            src = proj_bank[slot % 2]
            nc.scalar.copy(v_odd[0:DH, slot, 0, :, 0:DH], src[0:DH, :].rearrange("p (h d) -> p h d", d=DH))
            nc.scalar.copy(v_odd[DH:P, slot, 1, :, 0:DH], src[DH:P, :].rearrange("p (h d) -> p h d", d=DH))\
                .then_inc(v_evac, 1)

        def norm_square(u):
            act.wait_ge(f_mm, N_F * u + 2)
            nc.scalar.activation(fq[:, :], f_bank[:, 0:SEQ], ACT.Square).then_inc(f_squared, 1)

        def norm_root(u):
            act.wait_ge(f_mm, N_F * u + 3)
            if started(u):
                act.wait_ge(f_scaled, u)
            nc.scalar.activation(fr[:, :], f_bank[:, SEQ:2 * SEQ], ACT.Ln, bias=eps_col[:, 0:1]).then_inc(f_log, 1)
            act.wait_ge(f_log, u + 1)
            nc.scalar.activation(fr[:, :], fr[:, :], ACT.Exp, scale=-0.5).then_inc(f_rstd, 1)

        def evac_hidden(u, c):
            rows = P if c < HC - 1 else HLAST
            layer = u // BATCH
            act.wait_ge(f_mm, N_F * u + 4 + c)
            if c == 0 and started(u):
                act.wait_ge(f_mm, N_F * u)
            for dst, half, col in ((ap, 0, C_B1A), (gp, 1, C_B1G)):
                ins = nc.scalar.activation(dst[0:rows, c, :], f_bank[0:rows, half * SEQ:(half + 1) * SEQ], ACT.Identity,
                                           bias=cols[0:rows, bass.ds(layer, 1), col + c:col + c + 1].rearrange("p l c -> p (l c)"))
            ins.then_inc(h_evac, 1)

        def gelu(u):
            act.wait_ge(h_evac, HC * (u + 1))
            nc.scalar.activation(gp[:, :, :], gp[:, :, :], ACT.Gelu).then_inc(gelu_done, 1)
            load_ln_exp(nc, act)

        def body(it):
            proj, attn, ffn = has(it, 1), has(it, 0), has(it, -1)
            if attn:
                evac_qk(it, 0, 0)
                evac_qk(it, 0, 1)
                evac_qk(it, 0, 2)
            if proj:
                squares(it + 1, 0)
                squares(it + 1, 1)
            if ffn:
                norm_square(it - 1)
            if attn:
                evac_qk(it, 0, 3)
                evac_qk(it, 1, 0)
                evac_qk(it, 1, 1)
            if ffn:
                norm_root(it - 1)
            if attn:
                evac_qk(it, 1, 2)
            if proj:
                squares(it + 1, 2)
            if attn:
                evac_qk(it, 1, 3)
                exps(it, 0, 0)
                exps(it, 0, 1)
            if proj:
                squares(it + 1, 3)
            if attn:
                evac_pt(it, 0, 0)
                evac_pt(it, 0, 1)
            if ffn:
                evac_hidden(it - 1, 0)
            if proj:
                squares(it + 1, 4)
            if attn:
                exps(it, 1, 0)
            if ffn:
                evac_hidden(it - 1, 1)
            if proj:
                squares(it + 1, 5)
            if attn:
                exps(it, 1, 1)
            if ffn:
                evac_hidden(it - 1, 2)
            if proj:
                squares(it + 1, 6)
            if attn:
                evac_pt(it, 1, 0)
                evac_pt(it, 1, 1)
            if proj:
                squares(it + 1, 7)
            if ffn:
                gelu(it - 1)
            if proj:
                evac_v(it + 1, 0)
            if attn:
                evac_ot(it, 0, 0)
            if proj:
                inverse_norms(it + 1, 0)
                evac_v(it + 1, 1)
            if attn:
                evac_ot(it, 0, 1)
                evac_ot(it, 1, 0)
                evac_ot(it, 1, 1)
            if proj:
                inverse_norms(it + 1, 1)
                evac_v(it + 1, 2)
                evac_v(it + 1, 3)

        over_units(act, body)

    @block.vector
    def _(dve):
        dve.wait_ge(first_dma, 16 * 3)
        nc.vector.memset(ss[0][:, :], 0.0).then_inc(state_ready, BATCH)
        nc.vector.tensor_copy(wh[:, 0, :], qk[0][:, :]).then_inc(consts_done, 1)
        dve.wait_ge(consts_done, 1)
        nc.vector.tensor_tensor(wl[:, 0, :], qk[0][:, :], wh[:, 0, :].bitcast(F32), ALU.subtract).then_inc(split_done, 1)
        dve.wait_ge(split_done, 1)

        def unit_input(v):
            return xs[:, bass.ds(v % BATCH, 1), 0:SEQ].rearrange("p b s -> p (b s)")

        def stage_high(v):
            if started(v):
                dve.wait_ge(proj_mm, N_PROJ * v)
            dve.wait_ge(state_ready, v + 1)
            nc.vector.tensor_copy(xf[:, :], unit_input(v))
            nc.vector.tensor_copy(xh[:, :], unit_input(v)).then_inc(x_hi, 1)

        def stage_low(v):
            dve.wait_ge(x_hi, v + 1)
            nc.vector.tensor_tensor(xl[:, :], unit_input(v), xh[:, :].bitcast(F32), ALU.subtract).then_inc(x_staged, 1)

        def split_target(v, w):
            return w[:, bass.ds((v // BATCH + 1) % 2, 1), bass.ds((v % BATCH) * SPLIT, SPLIT)].rearrange("p l n -> p (l n)")

        def split_high(v):
            dve.wait_ge(raw_dma, 16 * (v + 1))
            nc.vector.tensor_copy(split_target(v, wh), wraw[:, :]).then_inc(split_hi, 1)

        def split_low(v):
            dve.wait_ge(split_hi, v + 1)
            nc.vector.tensor_tensor(split_target(v, wl), wraw[:, :], split_target(v, wh).bitcast(F32),
                                    ALU.subtract).then_inc(split_done, 1)

        def rotate(v, n):
            layer = v // BATCH
            t, c = n // 4, n % 4
            kind = 2 * (c // 2)
            dve.wait_ge(squared, 8 * v + n + 1)
            if c % 2 == 0 and started(2 * v + t if isinstance(v, int) else v):
                dve.wait_ge(rope_added, 2 * (2 * v + t) - 1 + c // 2)
            if started(v):
                dve.wait_ge(tr_mm, N_TR * (v - 1) + TR["qk", t, c] + 1)
            src = proj_bank[n % 2][:, :].rearrange("p (h a d) -> p h a d", a=2, d=WIN)
            cos = tab[:, bass.ds(layer, 1), t, kind, :].broadcast_to([P, 8, DH])
            sin = tab[:, bass.ds(layer, 1), t, kind + 1, :].broadcast_to([P, 8, DH])
            r = slice(c * 512, (c + 1) * 512)
            nc.vector.tensor_tensor(qk[t][:, r].rearrange("p (h d) -> p h d", d=DH),
                                    proj_bank[n % 2][:, :].rearrange("p (h d) -> p h d", d=DH), cos, ALU.mult)
            nc.vector.tensor_tensor(rot[:, r].rearrange("p (h a d) -> p h a d", a=2, d=WIN), src[:, :, ::-1, :],
                                    sin.rearrange("p h (a d) -> p h a d", a=2), ALU.mult).then_inc(roped, 1)

        def head_sums(v, n):
            t, c = n // 4, n % 4
            dve.wait_ge(squared, 8 * v + n + 1)
            if c == 0 and started(v):
                dve.wait_ge(rn_log, 2 * v + t - 1)
            nc.vector.tensor_reduce(ss[t][:, c * 8:(c + 1) * 8], sqr[:, c % 2, :].rearrange("p (h d) -> p h d", d=DH),
                                    AX.X, ALU.add).then_inc(sums_done, 1)

        def floor_sums(v, t):
            dve.wait_ge(sums_done, 8 * v + 4 * t + 4)
            nc.vector.tensor_scalar(ss[t][:, :], ss[t][:, :], 1e-24, None, ALU.max).then_inc(floored, 1)

        def mask_scores(u, t, n):
            dve.wait_ge(sc_mm, 4 * u + 2 * t + n + 1)
            if started(u):
                dve.wait_ge(tr_mm, N_TR * (u - 1) + TR["p", t, n] + 1)
            nc.vector.tensor_tensor(pr[t][:, 4 * n:4 * n + 4, :, :].rearrange("p k b c -> p (k b) c"),
                                    sc_bank[n][:, :].rearrange("p (h c) -> p h c", c=2 * WIN),
                                    mask[:, t, :].unsqueeze(1).broadcast_to([P, 8, 2 * WIN]), ALU.add).then_inc(sc_evac, 1)

        def softmax_max(u, t, n):
            k = 4 * u + 2 * t + n
            dve.wait_ge(sc_evac, k + 1)
            if started(k - 1 if isinstance(k, int) else k):
                dve.wait_ge(subtracted, k - 1)
            nc.vector.tensor_reduce(mx[:, n, :], pr[t][:, 4 * n:4 * n + 4, :, :].rearrange("p k b c -> p (k b) c"), AX.X,
                                    ALU.max).then_inc(max_done, 1)

        def attended(c):
            return pv_bank[:, 0:2 * pairs_of(c) * VW].rearrange("p (h e) -> p h e", e=VW)

        def pairs_of(c):
            return PV_CHUNKS[c][1] - PV_CHUNKS[c][0]

        def reciprocals(u, t, c):
            dve.wait_ge(pv_mm, N_PV * u + 3 * t + c + 1)
            nc.vector.reciprocal(rs[:, c % 2, 0:2 * pairs_of(c)], attended(c)[:, :, DH]).then_inc(recip_done, 1)

        def normalise(u, t, c):
            lo, hi = PV_CHUNKS[c]
            m = 2 * (hi - lo)
            dve.wait_ge(recip_done, N_PV * u + 3 * t + c + 1)
            if c == 0:
                if t == 1:
                    dve.wait_ge(tr_mm, N_TR * u + TR["o", 0, 1] + 1)
                elif started(u):
                    dve.wait_ge(tr_mm, N_TR * (u - 1) + TR["o", 1, 1] + 1)
            nc.vector.tensor_tensor(o[:, lo:hi, :, :].rearrange("p k b d -> p (k b) d"), attended(c)[:, :, 0:DH],
                                    rs[:, c % 2, 0:m].unsqueeze(2).broadcast_to([P, m, DH]), ALU.mult).then_inc(pv_evac, 1)

        def halves(u):
            b = bass.ds(u % BATCH, 1)
            for half in range(2):
                r = slice(64 * half, 64 * half + 64)
                yield r, xs[r, b, half:half + SEQ].rearrange("p b s -> p (b s)")

        def residual1(u):
            dve.wait_ge(f_mm, N_F * u + 1)
            for r, v in halves(u):
                ins = nc.vector.tensor_tensor(v, f_bank[r, 0:SEQ], v, ALU.add)
            ins.then_inc(res1, 1)

        def norm_column(u, c):
            return cols[:, bass.ds(u // BATCH, 1), c:c + 1].rearrange("p l c -> p (l c)")

        def norm_scale(u):
            dve.wait_ge(f_rstd, u + 1)
            nc.vector.scalar_tensor_tensor(out=fx[:, :], in0=f_bank[:, 0:SEQ], scalar=norm_column(u, C_G), in1=fr[:, :],
                                           op0=ALU.mult, op1=ALU.mult).then_inc(f_scaled, 1)

        def norm_shift(u):
            dve.wait_ge(f_scaled, u + 1)
            nc.vector.tensor_scalar(fx[:, :], fx[:, :], norm_column(u, C_B), None, ALU.add).then_inc(f_norm, 1)

        def residual2(u):
            layer = bass.ds(u // BATCH, 1)
            dve.wait_ge(f_mm, N_F * u + 7)
            for r, v in halves(u):
                ins = nc.vector.scalar_tensor_tensor(out=v, in0=f_bank[r, 0:SEQ],
                                                     scalar=cols[r, layer, C_B2:C_B2 + 1].rearrange("p l c -> p (l c)"),
                                                     in1=v, op0=ALU.add, op1=ALU.add)
            ins.then_inc(state_ready, 1)

        def body(it):
            proj, attn, ffn = has(it, 1), has(it, 0), has(it, -1)
            if proj:
                stage_high(it + 1)
                stage_low(it + 1)
            if ffn:
                residual1(it - 1)
            if proj:
                rotate(it + 1, 0)
                rotate(it + 1, 1)
            if attn:
                mask_scores(it, 0, 0)
            if proj:
                head_sums(it + 1, 0)
            if attn:
                softmax_max(it, 0, 0)
                mask_scores(it, 0, 1)
            if ffn:
                norm_scale(it - 1)
            if attn:
                softmax_max(it, 0, 1)
            if ffn:
                norm_shift(it - 1)
            if proj:
                split_high(it + 1)
                head_sums(it + 1, 1)
                rotate(it + 1, 2)
            if attn:
                mask_scores(it, 1, 0)
            if proj:
                head_sums(it + 1, 2)
            if attn:
                softmax_max(it, 1, 0)
            if proj:
                rotate(it + 1, 3)
                head_sums(it + 1, 3)
            if attn:
                reciprocals(it, 0, 0)
                mask_scores(it, 1, 1)
                normalise(it, 0, 0)
                softmax_max(it, 1, 1)
            if proj:
                rotate(it + 1, 4)
            if attn:
                reciprocals(it, 0, 1)
            if proj:
                head_sums(it + 1, 4)
            if attn:
                normalise(it, 0, 1)
            if proj:
                rotate(it + 1, 5)
                floor_sums(it + 1, 0)
            if attn:
                reciprocals(it, 0, 2)
            if proj:
                head_sums(it + 1, 5)
            if attn:
                normalise(it, 0, 2)
            if proj:
                rotate(it + 1, 6)
            if attn:
                reciprocals(it, 1, 0)
                normalise(it, 1, 0)
            if proj:
                split_low(it + 1)
                rotate(it + 1, 7)
            if attn:
                reciprocals(it, 1, 1)
                normalise(it, 1, 1)
            if proj:
                head_sums(it + 1, 6)
                head_sums(it + 1, 7)
            if attn:
                reciprocals(it, 1, 2)
                normalise(it, 1, 2)
            if proj:
                floor_sums(it + 1, 1)
            if ffn:
                residual2(it - 1)

        over_units(dve, body)


def build_last(nc, ctx, sb, sem, bank, ident, ones_mean, eps_col, x1, xs, out):
    y = sb(ctx, "y", [P, TOK])
    xc = sb(ctx, "xc2", [P, TOK])
    sq = sb(ctx, "sq2", [P, TOK])
    rstd = sb(ctx, "rstd2", [P, TOK])
    res = sb(ctx, "res", [P, TOK])
    copied = sem(ctx, "l_copied")
    mean_mm = sem(ctx, "l_mean_mm")
    centred = sem(ctx, "l_centred")
    squared = sem(ctx, "l_squared")
    var_mm = sem(ctx, "l_var_mm")
    log_done = sem(ctx, "l_log_done")
    rstd_done = sem(ctx, "l_rstd_done")
    scaled = sem(ctx, "l_scaled")
    added = sem(ctx, "l_added")
    out_mm = sem(ctx, "l_out_mm")
    out_evac = sem(ctx, "l_out_evac")
    stored = sem(ctx, "l_stored")

    def tok(g):
        return slice(g * GT, (g + 1) * GT)

    block = ctx.enter_context(nc.Block())

    @block.sync
    def _(sync):
        ov = out.rearrange("b (t p) d -> p (b t) d", p=P)
        for g in range(GROUPS):
            sync.wait_ge(out_evac, g + 1)
            sync.dma_start(ov[:, 4 * g:4 * g + 4, :], res[:, tok(g)].rearrange("p (t d) -> p t d", d=DIM)).then_inc(stored, 16)
        sync.wait_ge(stored, 16 * GROUPS)

    @block.tensor
    def _(pe):
        for g in range(GROUPS):
            pe.wait_ge(copied, g + 1)
            nc.tensor.matmul(bank[g][:, :], ones_mean[:, :], y[:, tok(g)], start=True, stop=True).then_inc(mean_mm, 1)
        for g in range(GROUPS):
            pe.wait_ge(squared, g + 1)
            nc.tensor.matmul(bank[4 + g][:, :], ones_mean[:, :], sq[:, tok(g)], start=True, stop=True).then_inc(var_mm, 1)
        for g in range(GROUPS):
            pe.wait_ge(added, g + 1)
            for t in range(4):
                mm = nc.tensor.transpose(bank[g][:, t * P:(t + 1) * P], xc[:, g * GT + t * P:g * GT + (t + 1) * P], ident[:, :])
            mm.then_inc(out_mm, 1)

    @block.scalar
    def _(act):
        for g in range(GROUPS):
            act.wait_ge(centred, g + 1)
            nc.scalar.activation(sq[:, tok(g)], xc[:, tok(g)], ACT.Square).then_inc(squared, 1)
        for g in range(GROUPS):
            act.wait_ge(var_mm, g + 1)
            nc.scalar.activation(rstd[:, tok(g)], bank[4 + g][:, :], ACT.Ln, bias=eps_col[:, 0:1]).then_inc(log_done, 1)
            act.wait_ge(log_done, g + 1)
            nc.scalar.activation(rstd[:, tok(g)], rstd[:, tok(g)], ACT.Exp, scale=-0.5).then_inc(rstd_done, 1)
        for g in range(GROUPS):
            act.wait_ge(out_mm, g + 1)
            nc.scalar.copy(res[:, tok(g)], bank[g][:, :]).then_inc(out_evac, 1)

    @block.vector
    def _(dve):
        for g in range(GROUPS):
            for half in range(2):
                r = slice(64 * half, 64 * half + 64)
                ins = nc.vector.tensor_copy(y[r, tok(g)].rearrange("p (b s) -> p b s", b=2), xs[r, 2 * g:2 * g + 2, half:half + SEQ])
            ins.then_inc(copied, 1)
        for g in range(GROUPS):
            dve.wait_ge(mean_mm, g + 1)
            dve.wait_ge(copied, g + 1)
            nc.vector.tensor_tensor(xc[:, tok(g)], y[:, tok(g)], bank[g][:, :], ALU.subtract).then_inc(centred, 1)
        for g in range(GROUPS):
            dve.wait_ge(rstd_done, g + 1)
            nc.vector.tensor_tensor(xc[:, tok(g)], xc[:, tok(g)], rstd[:, tok(g)], ALU.mult).then_inc(scaled, 1)
            dve.wait_ge(scaled, g + 1)
            nc.vector.tensor_tensor(xc[:, tok(g)], xc[:, tok(g)], x1[:, tok(g)], ALU.add).then_inc(added, 1)


def rotary_constants():
    half = np.arange(0, DH, 2, dtype=np.float64)
    freqs = np.arange(SEQ)[:, None] / 10000.0 ** (half / DH)[None, :]
    base = (half + 0.4 * DH) / (1.4 * DH)
    scale = base[None, :] ** ((np.arange(SEQ) - SEQ // 2) / (WIN // 2))[:, None]
    cos, sin = np.cos(freqs), np.sin(freqs)
    cos2, sin2, sc2 = (np.concatenate(p, 1) for p in ((cos, cos), (-sin, sin), (scale, scale)))
    t = np.stack([cos2 * sc2 * 8.0, sin2 * sc2 * 8.0, cos2 / sc2, sin2 / sc2], 1)
    return np.ascontiguousarray(t.reshape(TILES, P, 4, DH).transpose(1, 0, 2, 3).reshape(P, -1)).astype(np.float32)


def mask_constants():
    m = np.zeros((P, TILES, 2 * WIN), np.float32)
    r, c = np.arange(WIN)[:, None], np.arange(WIN)[None, :]
    for t in range(TILES):
        for j in range(4):
            rows = slice(WIN * j, WIN * (j + 1))
            before, own = np.where(r > c, -1e30, 0.0), np.where(c > r, -1e30, 0.0)
            if t == 0 and j == 0:
                before = np.full((WIN, WIN), -1e30)
            m[rows, t] = np.concatenate((before, own) if j % 2 else (own, before), 1)
    return np.ascontiguousarray(m.reshape(P, -1))


def matrix_constants():
    u = np.triu(np.ones((P, P), np.float32))
    return np.concatenate([np.eye(P, dtype=np.float32), u, np.ones((P, P), np.float32), u], 1)


def kernel(**inputs):
    import concourse.bacc as bacc
    from concourse.bass_utils import run_bass_kernel_spmd

    a = {k.replace("L0_attn_", "a_").replace("L0_ffn_", "f_"): np.asarray(v) for k, v in inputs.items()}
    wqkv = a["f_Wqkv"]
    wv = wqkv[:, :, 2 * INNER:].reshape(DEPTH, DIM, PAIRS, 2, DH).transpose(0, 1, 3, 2, 4).reshape(DEPTH, DIM, INNER)
    wo = a["f_Wo"].reshape(DEPTH, PAIRS, P, DIM).transpose(0, 2, 1, 3).reshape(DEPTH, P, PAIRS * DIM)
    w2 = np.zeros((DEPTH, HC * P, DIM), np.float32)
    w2[:, :DIM_INNER] = a["f_W2"]
    w2 = w2.reshape(DEPTH, HC, P, DIM).transpose(0, 2, 1, 3).reshape(DEPTH, P, HC * DIM)
    b1 = np.zeros((DEPTH, 2, HC * P), np.float32)
    b1[:, :, :DIM_INNER] = a["f_b1"].reshape(DEPTH, 2, DIM_INNER)
    cols = np.zeros((P, DEPTH, N_COLS), np.float32)
    cols[:, :, C_G] = a["f_ln_g"].T
    cols[:, :, C_B] = a["f_ln_b"].T
    cols[:, :, C_B2] = a["f_b2"].T
    cols[:, :, C_B1A:C_B1A + 2 * HC] = b1.reshape(DEPTH, 2 * HC, P).transpose(2, 0, 1)
    conv = np.concatenate([a["a_conv_w"].reshape(CONV_DIM, D_CONV), a["a_conv_b"].reshape(CONV_DIM, 1)], 1)
    conv = conv.reshape(3, P, D_CONV + 1).transpose(1, 0, 2)
    arrays = {
        "x": a["a_x"], "w_in_t": a["a_W_in"].T, "conv_cols": conv, "a_log": a["a_A_log"],
        "dt_bias": a["a_dt_bias"], "d_skip": a["a_D_skip"], "w_out_t": a["a_W_out"].T,
        "w_qk": wqkv[:, :, :2 * INNER], "w_v": wv, "w_o": wo, "w_1": a["f_W1"], "w_2": w2,
        "q_scale": a["f_q_scale"], "k_scale": a["f_k_scale"], "cols_in": cols,
        "rope": rotary_constants(), "consts": matrix_constants(), "mask_in": mask_constants(),
    }
    arrays = {k: np.ascontiguousarray(v) for k, v in arrays.items()}
    nc = bacc.Bacc("TRN2", target_bir_lowering=False, num_devices=1)
    aps = {k: nc.dram_tensor(f"in_{k}", v.shape, mybir.dt.from_np(v.dtype), kind="ExternalInput").ap()
           for k, v in arrays.items()}
    out = nc.dram_tensor("out_y", (BATCH, SEQ, DIM), F32, kind="ExternalOutput").ap()
    build(nc, out=out, **aps)
    got = run_bass_kernel_spmd(nc, [{f"in_{k}": v for k, v in arrays.items()}], core_ids=[0])
    return got.results[0]["out_y"]
```
